# Optimizing a Trainium2 kernel written in Bass

```python
import numpy as np
import jax
import jax.numpy as jnp

def _softmax(x, axis=-1):
    return jax.nn.softmax(x, axis=axis)

def _gelu(x):
    return jax.nn.gelu(x, approximate=True)

def _silu(x):
    return jax.nn.silu(x)

def _sigmoid(x):
    return jax.nn.sigmoid(x)

def _layernorm(x, axis=-1, eps=1e-05):
    m = jnp.mean(x, axis=axis, keepdims=True)
    v = jnp.var(x, axis=axis, keepdims=True)
    return (x - m) / jnp.sqrt(v + eps)

def _scatter_add(tgt, idx, src, axis=0):
    return tgt.at[idx].add(src)

def _segment_sum(src, seg, n):
    return jax.ops.segment_sum(src, seg, n)
kernel_name = 'mk_gnn_preln_d2_gnn_r8_2c0e8a'

def setup_inputs(seed: int=0):
    np.random.seed(seed)
    _w = jnp.asarray

    def _rec_inputs():
        import jax
        import jax.numpy as jnp
        _gk = jax.random.key(seed)
        x = -0.0001126 + 1 * jax.random.normal(jax.random.fold_in(_gk, 1), (3750, 256), jnp.float32)
        _s = jax.random.randint(jax.random.fold_in(_gk, 2), (30000,), 0, 3750, jnp.int32)
        _d = jax.random.randint(jax.random.fold_in(_gk, 3), (30000,), 0, 3750, jnp.int32)
        _loop = jnp.arange(3750, dtype=jnp.int32)
        src = jnp.concatenate([_s, _d, _loop])
        dst = jnp.concatenate([_d, _s, _loop])
        _o = jnp.argsort(dst, stable=True)
        src = src[_o]
        dst = dst[_o]
        edge_type_8 = jax.random.randint(jax.random.fold_in(_gk, 13), (63750,), 0, 8, jnp.int32)
        return (x, src, dst, edge_type_8)
    x, src, dst, edge_type_8 = _rec_inputs()

    def _L0_gnn_setup():
        import jax, jax.numpy as jnp
        import numpy as np
        N_NODES = 3750
        N_EDGES = 60000
        IN_FEAT = 256
        OUT_FEAT = 256
        N_RELS = 8
        N_HEADS = 4
        HEAD_DIM = OUT_FEAT // N_HEADS
        LEAKY_SLOPE = 0.2
        key = jax.random.key(seed)
        ks = jax.random.split(key, 8)
        inputs = jax.random.normal(ks[0], (N_NODES, IN_FEAT), dtype=jnp.float32)
        conv_weights = jax.random.normal(ks[1], (N_RELS, N_HEADS, IN_FEAT, HEAD_DIM), dtype=jnp.float32) * (1.0 / np.sqrt(IN_FEAT))
        attn_l = jax.random.normal(ks[2], (N_RELS, N_HEADS, HEAD_DIM), dtype=jnp.float32) * 0.1
        attn_r = jax.random.normal(ks[3], (N_RELS, N_HEADS, HEAD_DIM), dtype=jnp.float32) * 0.1
        h_bias = jax.random.normal(ks[4], (OUT_FEAT,), dtype=jnp.float32) * 0.02
        edge_src = jax.random.randint(ks[5], (N_EDGES,), 0, N_NODES, dtype=jnp.int32)
        edge_dst = jax.random.randint(ks[6], (N_EDGES,), 0, N_NODES, dtype=jnp.int32)
        edge_type = jax.random.randint(ks[7], (N_EDGES,), 0, N_RELS, dtype=jnp.int32)
        return {'inputs': inputs, 'conv_weights': conv_weights, 'attn_l': attn_l, 'attn_r': attn_r, 'h_bias': h_bias, 'edge_src': edge_src, 'edge_dst': edge_dst, 'edge_type': edge_type}
    _L0_gnn_all = _L0_gnn_setup()
    _L0_gnn_in = {k: v for k, v in _L0_gnn_all.items() if k in ('conv_weights', 'attn_l', 'attn_r', 'h_bias')}
    del _L0_gnn_all

    def _L1_gnn_setup():
        import jax, jax.numpy as jnp
        import numpy as np
        N_NODES = 6250
        N_EDGES = 100000
        IN_CH = 256
        HID_CH = 256
        OUT_CH = 256
        N_LAYERS = 3
        key = jax.random.key(seed)
        ks = jax.random.split(key, 8)
        s_in = 1.0 / np.sqrt(IN_CH)
        s_h = 1.0 / np.sqrt(HID_CH)
        return {'x': jax.random.normal(ks[0], (N_NODES, IN_CH), dtype=jnp.float32), 'W_in': jax.random.normal(ks[1], (IN_CH, HID_CH), dtype=jnp.float32) * s_in, 'b_in': jnp.zeros((HID_CH,), dtype=jnp.float32), 'W_agg': jax.random.normal(ks[2], (N_LAYERS, HID_CH, HID_CH), dtype=jnp.float32) * s_h, 'W_self': jax.random.normal(ks[3], (N_LAYERS, HID_CH, HID_CH), dtype=jnp.float32) * s_h, 'b_hid': jnp.zeros((N_LAYERS, HID_CH), dtype=jnp.float32), 'W_out': jax.random.normal(ks[4], (HID_CH, OUT_CH), dtype=jnp.float32) * s_h, 'b_out': jnp.zeros((OUT_CH,), dtype=jnp.float32), 'edge_index': jax.random.randint(ks[5], (2, N_EDGES), 0, N_NODES, dtype=jnp.int64)}
    _L1_gnn_all = _L1_gnn_setup()
    _L1_gnn_in = {k: v for k, v in _L1_gnn_all.items() if k in ('W_in', 'b_in', 'W_agg', 'W_self', 'b_hid', 'W_out', 'b_out')}
    del _L1_gnn_all
    return {'x': x, 'src': src, 'dst': dst, 'edge_type_8': edge_type_8, 'L0_gnn_conv_weights': _L0_gnn_in['conv_weights'], 'L0_gnn_attn_l': _L0_gnn_in['attn_l'], 'L0_gnn_attn_r': _L0_gnn_in['attn_r'], 'L0_gnn_h_bias': _L0_gnn_in['h_bias'], 'L1_gnn_W_in': _L1_gnn_in['W_in'], 'L1_gnn_b_in': _L1_gnn_in['b_in'], 'L1_gnn_W_agg': _L1_gnn_in['W_agg'], 'L1_gnn_W_self': _L1_gnn_in['W_self'], 'L1_gnn_b_hid': _L1_gnn_in['b_hid'], 'L1_gnn_W_out': _L1_gnn_in['W_out'], 'L1_gnn_b_out': _L1_gnn_in['b_out']}

def reference(x, src, dst, edge_type_8, L0_gnn_conv_weights, L0_gnn_attn_l, L0_gnn_attn_r, L0_gnn_h_bias, L1_gnn_W_in, L1_gnn_b_in, L1_gnn_W_agg, L1_gnn_W_self, L1_gnn_b_hid, L1_gnn_W_out, L1_gnn_b_out):
    import jax
    import jax.numpy as jnp

    def _L0_gnn_ref(inputs, conv_weights, attn_l, attn_r, h_bias, edge_src, edge_dst, edge_type):
        import jax, jax.numpy as jnp
        import numpy as np
        N_NODES = 3750
        N_EDGES = 60000
        IN_FEAT = 256
        OUT_FEAT = 256
        N_RELS = 8
        N_HEADS = 4
        HEAD_DIM = OUT_FEAT // N_HEADS
        LEAKY_SLOPE = 0.2
        feat_all = jnp.einsum('ni,rhid->rnhd', inputs, conv_weights)
        feat_src_e = feat_all[edge_type, edge_src]
        feat_dst_e = feat_all[edge_type, edge_dst]
        el = jnp.sum(feat_src_e * attn_l[edge_type], axis=-1)
        er = jnp.sum(feat_dst_e * attn_r[edge_type], axis=-1)
        e = jax.nn.leaky_relu(el + er, negative_slope=LEAKY_SLOPE)
        m = jax.ops.segment_max(e, edge_dst, num_segments=N_NODES)
        ex = jnp.exp(e - m[edge_dst])
        denom = jax.ops.segment_sum(ex, edge_dst, num_segments=N_NODES)
        alpha = ex / denom[edge_dst]
        h = jax.ops.segment_sum(alpha[..., None] * feat_src_e, edge_dst, num_segments=N_NODES)
        h = h.reshape(N_NODES, OUT_FEAT) + h_bias
        return h

    def _L1_gnn_ref(x, W_in, b_in, W_agg, W_self, b_hid, W_out, b_out, edge_index):
        import jax, jax.numpy as jnp
        import numpy as np
        N_NODES = 6250
        N_EDGES = 100000
        IN_CH = 256
        HID_CH = 256
        OUT_CH = 256
        N_LAYERS = 3
        n = x.shape[0]
        dst = edge_index[0]
        src = edge_index[1]
        n_layers = W_agg.shape[0]
        h = x @ W_in + b_in
        deg = jax.ops.segment_sum(jnp.ones_like(dst, dtype=h.dtype), dst, num_segments=n)
        deg = jnp.maximum(deg, 1.0)[:, None]
        for l in range(n_layers):
            agg = jax.ops.segment_sum(h[src], dst, num_segments=n) / deg
            h = jax.nn.relu(agg @ W_agg[l] + h @ W_self[l] + b_hid[l])
        return h @ W_out + b_out
    edge_index = jnp.stack([src, dst])
    h = jnp.maximum(_layernorm(x, axis=-1), 0.0)
    x = x + _L0_gnn_ref(h, L0_gnn_conv_weights, L0_gnn_attn_l, L0_gnn_attn_r, L0_gnn_h_bias, src, dst, edge_type_8)
    h = jnp.maximum(_layernorm(x, axis=-1), 0.0)
    x = x + _L1_gnn_ref(h, L1_gnn_W_in, L1_gnn_b_in, L1_gnn_W_agg, L1_gnn_W_self, L1_gnn_b_hid, L1_gnn_W_out, L1_gnn_b_out, edge_index)
    return x

_drawn_inputs = setup_inputs


def setup_inputs(seed=0):
    import zlib

    import numpy as np

    out = dict(_drawn_inputs(seed))
    spreads = {'L1_gnn_b_in': (0.0, 0.1), 'L1_gnn_b_hid': (0.0, 0.1), 'L1_gnn_b_out': (0.0, 0.1)}
    factors = {'L0_gnn_h_bias': 3.257}
    for name, (base, spread) in spreads.items():
        noise = np.random.default_rng([zlib.crc32(name.encode()), seed]).standard_normal(out[name].shape)
        drawn = base * np.exp(spread * noise) if base else spread * noise
        out[name] = jnp.asarray(drawn.astype(out[name].dtype))
    for name, factor in factors.items():
        out[name] = (out[name] * factor).astype(out[name].dtype)
    return out
```

```python
import concourse.bass as bass
from concourse import mybir
from contextlib import ExitStack

FP32 = mybir.dt.float32
BF16 = mybir.dt.bfloat16
I32 = mybir.dt.int32
ALU = mybir.AluOpType
ACT = mybir.ActivationFunctionType
AX = mybir.AxisListType

P = 128
N, E, F, R, H, D = 3750, 63750, 256, 8, 4, 64
LAYERS = 3
K2 = F // P
NBLK = (N + P - 1) // P
NC = 8
CW = 4 * P
NP = NC * CW
RH = R * H
U, G = 4, 5
TB = U * G
TURNS = -(-E // (P * TB))
TURNS_SORTED = -(-(E + N) // (P * TB))
CT = 5
T = CT * P
BIG = 1e30
EPS = 1e-5
SLOPE = 0.2
BANK = [0, 1, 0, 1, 2]
PS_TILES = 10
NTAB = (NBLK + 1) * P


class Chain:

    def __init__(self, eng, sem, before=0):
        self.eng, self.sem, self.before, self.n = eng, sem, before, 0

    def link(self, ins):
        ins.then_inc(self.sem, 1)
        self.n += 1
        self.eng.wait_ge(self.sem, self.before + self.n)


def gnn_kernel(nc, x, src, dst, etype, conv_w, attn_l, attn_r, h_bias, w_in, b_in, w_agg, w_self,
               b_hid, w_out, b_out, out):
    ctx = ExitStack()
    with ctx:
        def sb(name, shape, dt=FP32):
            return ctx.enter_context(nc.sbuf_tensor(name, shape, dt))

        def dram(name, shape, dt=FP32):
            return nc.dram_tensor(name, shape, dt, kind="Internal").ap()

        names = {}

        phase_sems = []

        def sem(name):
            names[name] = names.get(name, 0) + 1
            s = nc.alloc_semaphore(f"{name}_{names[name]}")
            phase_sems.append(s)
            return s

        passed = nc.alloc_semaphore("passed")

        def end_phase():
            with nc.Block() as block:
                @block.gpsimd
                def _(pool):
                    for s in phase_sems:
                        pool.sem_clear(s)
            for s in phase_sems:
                nc.release_semaphore(s)
            phase_sems.clear()

        el_tab = dram("el_tab", [NTAB, RH])
        er_tab = dram("er_tab", [NTAB, RH])
        feat_tab = dram("feat_tab", [NP * R, F])
        x1_tab = dram("x1_tab", [NP, F])
        h_tab = [dram(f"h_tab{i}", [NP, F]) for i in range(2)]
        dstm_row = dram("dstm_row", [CT, P, P])

        work = sb("work", [P, 13312])
        hT = sb("hT", [P, K2, NP])
        deg = sb("deg", [P, NP])
        wbuf = sb("wbuf", [P, 4096])
        stg = sb("stg", [P, 6400])
        acc = work[:, 0:8192].rearrange("p (k n) -> p k n", k=K2)
        ring = work[:, 8192:13312].rearrange("p (s f) -> p s f", s=TB)
        src_i = sb("src_i", [P, T], I32)
        fidx_i = sb("fidx_i", [P, T], I32)
        dstloc = sb("dstloc", [P, T])
        nodeid = sb("nodeid", [P, T])
        typ_t = sb("typ_t", [P, T])
        pad_t = sb("pad_t", [P, T])
        alpha = sb("alpha", [P, T, H])
        base_i = sb("base_i", [1, T], I32)
        io_i = sb("io_i", [P, P + 1], I32)
        iota_w = sb("iota_w", [P, P])
        iota_p = sb("iota_p", [P, 1])
        ident = sb("ident", [P, P])
        ones = sb("ones", [P, P])
        ones_b = sb("ones_b", [P, P], BF16)
        hb_c = sb("hb_c", [P, K2])
        bin_c = sb("bin_c", [P, K2])
        bin_b = sb("bin_b", [P, F])
        bh_c = sb("bh_c", [P, LAYERS, K2])
        bout_b = sb("bout_b", [P, F])
        wlr = sb("wlr", [P, K2, 2 * RH])
        eps_c = sb("eps_c", [P, 1])
        stats = sb("stats", [P, 4, 6])
        mv = sb("mv", [P, 4, 2])
        std = sb("std", [P, 4])
        rstd = sb("rstd", [P, 4])
        idx_ring = sb("idx_ring", [P, TB], I32)
        small = sb("small", [P, 64])
        turns_i = sb("turns_i", [1, 1], I32)
        cT = sb("cT", [P, 2, CT, H])
        PS = ctx.enter_context(nc.psum_tensor("PS", [P, 8, 512], FP32))

        held = {}

        def base_regs(eng):
            if eng.engine not in held:
                held[eng.engine] = [eng.alloc_register(f"window{u}") for u in range(U)]
            return held[eng.engine]

        def turns_of(eng):
            return eng.value_load(turns_i[0:1, 0:1], min_val=TURNS, max_val=TURNS_SORTED)

        s_ld, s_io, s_pr, s_c = sem("loaded"), sem("iotas"), sem("products"), sem("consts")
        wc = wbuf[:, :].rearrange("p (k n) -> p k n", k=K2)
        x_all = work[:, 0:8192].rearrange("p (b f) -> p b f", b=32)
        s_xl, s_xz = sem("x_loaded"), sem("x_zeroed")
        prod = [work[:, 8192 + 2048 * i:8192 + 2048 * (i + 1)] for i in range(2)]

        with nc.Block() as block:
            @block.sync
            def _(sp):
                for k in range(K2):
                    for r in range(R):
                        sp.dma_start(wc[:, k, r * F:(r + 1) * F].rearrange("p (h d) -> p h d", h=H),
                                     conv_w[r, :, k * P:(k + 1) * P, :].rearrange("h p d -> p h d")
                                     ).then_inc(s_ld, 16)
                for i, a in enumerate((attn_l, attn_r)):
                    sp.dma_start(stg[:, i * 2048:(i + 1) * 2048],
                                 a.rearrange("(o r) h d -> o (r h d)", o=1).to_broadcast([P, 2048])
                                 ).then_inc(s_ld, 16)
                sp.wait_ge(s_xz, 1)
                full = NBLK - 1
                sp.dma_start(x_all[:, 0:full, :],
                             x[0:full * P, :].rearrange("(b p) f -> p b f", p=P)).then_inc(s_xl, 16)
                sp.dma_start(x_all[0:N - full * P, full, :], x[full * P:N, :]).then_inc(s_xl, 16)
                for buf, v in ((hb_c, h_bias), (bin_c, b_in)):
                    sp.dma_start(buf[:, :], v.rearrange("(k p) -> p k", p=P),
                                 allow_slow_non_contiguous=True).then_inc(s_ld, 16)
                sp.dma_start(bh_c[:, :, :], b_hid.rearrange("l (k p) -> p l k", p=P),
                             allow_slow_non_contiguous=True).then_inc(s_ld, 16)
                for buf, v in ((bin_b, b_in), (bout_b, b_out)):
                    sp.dma_start(buf[:, :], v.rearrange("(o n) -> o n", o=1).to_broadcast([P, F])
                                 ).then_inc(s_ld, 16)
                sp.wait_ge(s_ld, 16 * (K2 * R + 2 + 5))
                sp.wait_ge(s_xl, 32)

            @block.gpsimd
            def _(pool):
                pool.iota(io_i[:, 0:P], pattern=[[1, P]], base=0, channel_multiplier=0).then_inc(s_io, 1)
                pool.iota(io_i[:, P:P + 1], pattern=[[1, 1]], base=0, channel_multiplier=1).then_inc(s_io, 1)

            @block.vector
            def _(dve):
                dve.memset(x_all[:, NBLK - 1:32, :], 0.0).then_inc(s_xz, 1)
                dve.memset(ones[:, :], 1.0)
                dve.memset(ones_b[:, :], 1.0)
                dve.memset(eps_c[:, :], EPS)
                dve.memset(alpha[:, :, :], 0.0)
                c = Chain(dve, s_c)
                dve.wait_ge(s_io, 2)
                c.link(dve.tensor_copy(iota_w[:, :], io_i[:, 0:P]))
                c.link(dve.tensor_copy(iota_p[:, :], io_i[:, P:P + 1]))
                c.link(dve.tensor_scalar(ident[:, :], iota_w[:, :], iota_p[:, :], None, ALU.is_equal))
                dve.wait_ge(s_ld, 16 * (K2 * R + 2 + 5))
                for i in range(2):
                    for k in range(K2):
                        c.link(dve.tensor_tensor(prod[k], wc[:, k, :], stg[:, i * 2048:(i + 1) * 2048],
                                                 ALU.mult))
                        c.link(dve.tensor_reduce(wlr[:, k, i * RH:(i + 1) * RH],
                                                 prod[k].rearrange("p (c d) -> p c d", d=D), AX.X, ALU.add))

        def row(i):
            return work[:, i * T:(i + 1) * T].rearrange("p (c j) -> p c j", c=CT)

        def hrow(i):
            return hT[:, :, :].rearrange("p k n -> p (k n)")[:, i * T:(i + 1) * T].rearrange(
                "p (c j) -> p c j", c=CT)

        ROW0 = 8192 // T + 1
        key, dstm, srcr, typr, fidx = [hrow(i) for i in range(5)]
        raw = [hrow(5 + i).bitcast(I32) for i in range(4)]
        rows4 = hT[0:H, :, :].rearrange("p k n -> p (k n)")

        def load_rows(block, arrays, pads):
            s_pad, s_rl, s_cv = sem("pads_set"), sem("rows_loaded"), sem("rows_converted")
            whole, rest = divmod(E - 3 * P * P, P)

            @block.sync
            def _(sp):
                sp.wait_ge(s_pad, len(arrays))
                for a, buf in zip(arrays, raw):
                    sp.dma_start(buf[:, 0:3, :], a[0:3 * P * P].rearrange("(c p j) -> p c j", c=3, p=P)
                                 ).then_inc(s_rl, 16)
                    sp.dma_start(buf[0:whole, 3, :], a[3 * P * P:E - rest].rearrange("(p j) -> p j", j=P)
                                 ).then_inc(s_rl, 16)
                    sp.dma_start(buf[whole:whole + 1, 3, 0:rest],
                                 a[E - rest:E].rearrange("(o j) -> o j", o=1)).then_inc(s_rl, 16)
                sp.wait_ge(s_rl, 48 * len(arrays))

            @block.vector
            def _(dve):
                for v, buf in zip(pads, raw):
                    dve.memset(buf[:, 3:CT, :], v).then_inc(s_pad, 1)
                dve.wait_ge(s_rl, 48 * len(arrays))
                for buf, to in zip(raw, (key, dstm, srcr, typr)):
                    dve.tensor_copy(to, buf).then_inc(s_cv, 1)
                dve.wait_ge(s_cv, 4)

        with nc.Block() as block:
            load_rows(block, (dst, dst, src, etype), (N - 1, -1, 0, 0))

        base_r, last_r = stg[0:H, 0:T], stg[0:H, T:2 * T]
        first_c = stg[:, 2 * T:2 * T + CT * H].rearrange("p (c h) -> p c h", h=H)
        last_c = stg[:, 2 * T + 32:2 * T + 32 + CT * H].rearrange("p (c h) -> p c h", h=H)

        def tile_ends():
            s_fc, s_tp, s_br = sem("ends_picked"), sem("ends_turned"), sem("ends_rowed")
            with nc.Block() as block:
                @block.vector
                def _(dve):
                    dve.tensor_copy(first_c, key[:, :, 0:1].to_broadcast([P, CT, H])).then_inc(s_fc, 1)
                    dve.tensor_copy(last_c, key[:, :, P - 1:P].to_broadcast([P, CT, H])).then_inc(s_fc, 1)
                    dve.wait_ge(s_tp, 1)
                    for i, to in enumerate((base_r, last_r)):
                        dve.tensor_copy(to[:, 0:512], PS[0:H, 2 * i, :]).then_inc(s_br, 1)
                        dve.tensor_copy(to[:, 512:T], PS[0:H, 2 * i + 1, 0:P]).then_inc(s_br, 1)
                    dve.wait_ge(s_br, 4)

                @block.tensor
                def _(pe):
                    pe.wait_ge(s_fc, 2)
                    for i, c4 in enumerate((first_c, last_c)):
                        for c in range(CT):
                            mm = pe.transpose(PS[0:H, 2 * i + c // 4, (c % 4) * P:(c % 4 + 1) * P],
                                              c4[:, c, :], ident[:, :])
                    mm.then_inc(s_tp, 1)

        tile_ends()

        s_k, s_ks, s_kr = sem("check_steps"), sem("check_sum"), sem("check_rows")
        bad, viol = small[:, 0:4], stg[:, 2048:2048 + CT * (P - 1)].rearrange("p (c j) -> p c j", c=CT)
        with nc.Block() as block:
            @block.vector
            def _(dve):
                c = Chain(dve, s_k)
                c.link(dve.tensor_tensor(viol, key[:, :, 1:P], key[:, :, 0:P - 1], ALU.is_lt))
                c.link(dve.tensor_reduce(bad[:, 0:1], viol, AX.XY, ALU.add))
                c.link(dve.tensor_tensor(small[:, 8:8 + CT], last_c[:, :, 0], first_c[:, :, 0], ALU.subtract))
                c.link(dve.tensor_scalar(small[:, 16:16 + CT], small[:, 8:8 + CT], float(P - 1), None, ALU.is_gt))
                c.link(dve.tensor_reduce(bad[:, 1:2], small[:, 16:16 + CT], AX.X, ALU.add))
                c.link(dve.tensor_tensor(bad[:, 2:3], bad[:, 0:1], bad[:, 1:2], ALU.add))
                c.link(dve.tensor_tensor(stg[0:1, 3000:3000 + T - 1], last_r[0:1, 0:T - 1], base_r[0:1, 1:T],
                                         ALU.is_gt))
                c.link(dve.tensor_reduce(small[0:1, 24:25], stg[0:1, 3000:3000 + T - 1], AX.X, ALU.add))
                dve.wait_ge(s_ks, 1)
                c.link(dve.tensor_tensor(small[0:1, 25:26], PS[0:1, 0, 0:1], small[0:1, 24:25], ALU.add))
                c.link(dve.tensor_scalar(small[0:1, 26:27], small[0:1, 25:26], 0.0,
                                         float(TURNS_SORTED - TURNS), ALU.is_gt, ALU.mult))
                c.link(dve.tensor_scalar(turns_i[0:1, 0:1], small[0:1, 26:27], float(TURNS), None, ALU.add))

            @block.tensor
            def _(pe):
                pe.wait_ge(s_k, 8)
                pe.matmul(PS[0:1, 0, 0:1], bad[:, 2:3], ones[:, 0:1], start=True, stop=True).then_inc(s_ks, 1)

        end_phase()
        SW = -(-(E + N) // P)
        rec = work[:, 8192:8192 + 4 * SW].rearrange("p (j a) -> p j a", a=4)
        raw_s = [work[:, 8192 + (4 + i) * SW:8192 + (5 + i) * SW].bitcast(I32) for i in range(3)]
        pos, hit, rank, tmp, zero = [stg[:, i * SW:(i + 1) * SW] for i in range(5)]
        entry_i, pos_i = [stg[:, (5 + i) * SW:(6 + i) * SW].bitcast(I32) for i in range(2)]
        val, place0, off = small[:, 32:33], small[:, 33:34], small[:, 34:35]
        tri = stg[:, 7 * SW:7 * SW + P]
        idx4, rec4 = idx_ring[:, 0:4], stg[:, 4000:4016].rearrange("p (s a) -> p s a", a=4)
        rec_tab = dram("rec_tab", [P * SW, 4])
        back = work[:, 8192:8192 + CT * 4 * P].rearrange("p (c j a) -> p c j a", c=CT, a=4)
        back_whole, back_rest = divmod(SW, P)
        s_z, s_l, s_e, s_a, s_pk, s_pp, s_pi, s_cp, s_is, s_sd, s_rl, s_rd = [sem(a) for a in (
            "rows_zeroed", "edges_loaded", "entries_numbered", "sort_steps", "ranks_ready", "offsets_ready",
            "places_ready", "records_picked", "scatters_issued", "all_scattered", "sorted_loaded", "place_steps")]
        s_sc = [sem(f"scattered{i}") for i in range(4)]
        full, rest = divmod(E, SW)
        STEPS = 8

        with nc.Block() as block:
            @block.sync
            def _(sp):
                with sp.If(turns_of(sp) > TURNS):
                    sp.wait_ge(s_z, 3)
                    for a, buf in zip((dst, src, etype), raw_s):
                        sp.dma_start(buf[0:full, :], a[0:full * SW].rearrange("(p j) -> p j", j=SW)
                                     ).then_inc(s_l, 16)
                        sp.dma_start(buf[full:full + 1, 0:rest], a[full * SW:E].rearrange("(o j) -> o j", o=1)
                                     ).then_inc(s_l, 16)
                    sp.wait_ge(s_cp, 2 * SW)
                    sp.wait_ge(s_sd, 1)
                    rows = rec_tab.rearrange("(t j) a -> t (j a)", j=P)
                    for cc in range(back_whole + 1):
                        k = P if cc < back_whole else back_rest
                        sp.dma_start(back[0:k, cc, :, :].rearrange("p j a -> p (j a)"), rows[cc * P:cc * P + k, :]
                                     ).then_inc(s_rl, 16)

            @block.gpsimd
            def _(pool):
                with pool.If(turns_of(pool) > TURNS):
                    pool.iota(entry_i, pattern=[[1, SW]], base=-E, channel_multiplier=SW).then_inc(s_e, 1)
                    with pool.Fori(0, SW // 4) as i:
                        for s in range(4):
                            pool.wait_ge(s_cp, i * 8 + 2 * s + 2)
                            pool.sem_inc(s_is, 1)
                            pool.indirect_dma_start(
                                out=rec_tab[:, :], out_offset=bass.IndirectOffsetOnAxis(ap=idx4[:, s:s + 1], axis=0),
                                in_=rec4[:, s, :], in_offset=None).then_inc(s_sc[s], 16)
                    for s in range(4):
                        pool.wait_ge(s_sc[s], 16 * (SW // 4) + 16)
                    pool.sem_inc(s_sd, 1)

            @block.tensor
            def _(pe):
                with pe.If(turns_of(pe) > TURNS):
                    with pe.Fori(0, N) as v:
                        pe.wait_ge(s_pk, v * STEPS + 2)
                        pe.matmul(PS[:, 0, 0:1], tri, rank[:, SW - 1:SW], start=True, stop=True)
                        pe.matmul(PS[:, 0, 1:2], ones[:, :], rank[:, SW - 1:SW], start=True, stop=True
                                  ).then_inc(s_pp, 1)

            @block.vector
            def _(dve):
                with dve.If(turns_of(dve) > TURNS):
                    for buf in raw_s:
                        dve.memset(buf, 0).then_inc(s_z, 1)
                    c = Chain(dve, s_a)
                    for a in (pos, zero, val):
                        c.link(dve.memset(a, 0.0))
                    c.link(dve.memset(place0, -1.0))
                    c.link(dve.tensor_scalar(tri, iota_w[:, :], iota_p[:, :], None, ALU.is_gt))
                    dve.wait_ge(s_l, 96)
                    dve.wait_ge(s_e, 1)
                    c.link(dve.tensor_copy(tmp, entry_i))
                    c.link(dve.tensor_scalar(hit, tmp, 0.0, None, ALU.is_lt))
                    c.link(dve.tensor_scalar(tmp, tmp, 0.0, float(N - 1), ALU.max, ALU.min))
                    c.link(dve.tensor_tensor(rec[:, :, 0], raw_s[0], tmp, ALU.add))
                    c.link(dve.scalar_tensor_tensor(rec[:, :, 1], rec[:, :, 0], 1.0, hit, ALU.add, ALU.mult))
                    c.link(dve.tensor_scalar(rec[:, :, 1], rec[:, :, 1], 1.0, None, ALU.subtract))
                    c.link(dve.tensor_copy(rec[:, :, 2], raw_s[1]))
                    c.link(dve.tensor_copy(rec[:, :, 3], raw_s[2]))
                    dve.sem_inc(passed, 1)
                    with dve.Fori(0, N) as v:
                        c = Chain(dve, s_pk, v * STEPS)
                        c.link(dve.tensor_scalar(hit, rec[:, :, 0], val, None, ALU.is_equal))
                        c.link(dve.tensor_tensor_scan(rank, hit, zero, 0.0, ALU.add, ALU.add))
                        dve.wait_ge(s_pp, v + 1)
                        c.link(dve.tensor_tensor(off, PS[:, 0, 0:1], place0, ALU.add))
                        c.link(dve.scalar_tensor_tensor(tmp, rank, off, hit, ALU.add, ALU.mult))
                        c.link(dve.tensor_tensor(pos, pos, tmp, ALU.add))
                        c.link(dve.tensor_tensor(place0, place0, PS[:, 0, 1:2], ALU.add))
                        c.link(dve.tensor_scalar(val, val, 1.0, None, ALU.add))
                        c.link(dve.tensor_copy(small[:, 35:36], place0))
                        dve.sem_inc(passed, 1)
                    dve.tensor_copy(pos_i, pos).then_inc(s_pi, 1)
                    dve.wait_ge(s_pi, 1)
                    for s in range(4):
                        dve.sem_inc(s_sc[s], 16)
                    with dve.Fori(0, SW // 4) as i:
                        for s in range(4):
                            dve.wait_ge(s_sc[s], i * 16 + 16)
                            dve.tensor_copy(idx4[:, s:s + 1], pos_i[:, bass.ds(i * 4 + s, 1)]).then_inc(s_cp, 1)
                            dve.tensor_copy(rec4[:, s, :], rec[:, bass.ds(i * 4 + s, 1), :].rearrange("p o a -> p (o a)")
                                            ).then_inc(s_cp, 1)
                    c = Chain(dve, s_rd)
                    for a, v in zip((key, dstm, srcr, typr), (N - 1, -1, 0, 0)):
                        c.link(dve.memset(a[:, back_whole:CT, :], float(v)))
                    dve.wait_ge(s_rl, 16 * (back_whole + 1))
                    for i, a in enumerate((key, dstm, srcr, typr)):
                        c.link(dve.tensor_copy(a[:, 0:back_whole, :], back[:, 0:back_whole, :, i]))
                        c.link(dve.tensor_copy(a[0:back_rest, back_whole, :], back[0:back_rest, back_whole, :, i]))

        tile_ends()

        s_f, s_tt, s_te, s_bb, s_dr = (sem("fidx_made"), sem("rows_turned"), sem("tiles_made"),
                                       sem("base_spread"), sem("dstm_stored"))
        with nc.Block() as block:
            @block.vector
            def _(dve):
                c = Chain(dve, s_f)
                c.link(dve.scalar_tensor_tensor(fidx, srcr, float(R), typr, ALU.mult, ALU.add))
                e = Chain(dve, s_te)
                for i, to in enumerate((src_i, fidx_i, dstloc, typ_t)):
                    dve.wait_ge(s_tt, i + 1)
                    b = 2 * (i % 2)
                    e.link(dve.tensor_copy(to[:, 0:512], PS[:, b, :]))
                    e.link(dve.tensor_copy(to[:, 512:T], PS[:, b + 1, 0:P]))
                e.link(dve.tensor_scalar(pad_t[:, :], dstloc[:, :], 0.0, -BIG, ALU.is_lt, ALU.mult))
                dve.wait_ge(s_bb, 1)
                for a, b in ((0, 512), (512, T)):
                    pb = PS[:, 4 + a // 512, 0:b - a]
                    e.link(dve.tensor_tensor(dstloc[:, a:b], dstloc[:, a:b], pb, ALU.subtract))
                    e.link(dve.tensor_scalar(nodeid[:, a:b], pb, iota_p[:, :], None, ALU.add))
                e.link(dve.tensor_copy(base_i[:, :], base_r[0:1, :]))

            @block.tensor
            def _(pe):
                for i, fr in enumerate((srcr, fidx, dstm, typr)):
                    if i == 0:
                        pe.wait_ge(s_f, 1)
                    if i >= 2:
                        pe.wait_ge(s_te, 2 * (i - 1))
                    for c in range(CT):
                        mm = pe.transpose(PS[:, 2 * (i % 2) + c // 4, (c % 4) * P:(c % 4 + 1) * P],
                                          fr[:, c, :], ident[:, :])
                    mm.then_inc(s_tt, 1)
                for a, b in ((0, 512), (512, T)):
                    mm = pe.matmul(PS[:, 4 + a // 512, 0:b - a], ones[0:1, :], base_r[0:1, a:b],
                                   start=True, stop=True)
                mm.then_inc(s_bb, 1)

            @block.sync
            def _(sp):
                sp.dma_start(dstm_row.rearrange("c p j -> p c j"), dstm).then_inc(s_dr, 16)
                sp.wait_ge(s_dr, 16)

        same = sb("same", [P, T + 1])
        firstm = sb("firstm", [P, T])
        lastm = sb("lastm", [P, T])
        s_sm = sem("segments_marked")
        with nc.Block() as block:
            @block.vector
            def _(dve):
                c = Chain(dve, s_sm)
                c.link(dve.memset(same[:, :], 0.0))
                sv = same[:, 0:T].rearrange("p (c j) -> p c j", c=CT)
                c.link(dve.tensor_tensor(sv[:, :, 1:P], key[:, :, 1:P], key[:, :, 0:P - 1], ALU.is_equal))
                c.link(dve.tensor_tensor(firstm[:, :].rearrange("p (c j) -> p c j", c=CT), key,
                                         key[:, :, 0:1].to_broadcast([P, CT, P]), ALU.is_equal))
                c.link(dve.tensor_tensor(lastm[:, :].rearrange("p (c j) -> p c j", c=CT), key,
                                         key[:, :, P - 1:P].to_broadcast([P, CT, P]), ALU.is_equal))

        cont = sb("cont", [H, T + 1])
        single = sb("single", [H, T])
        with nc.Block() as block:
            s_ct = sem("conts_made")

            @block.vector
            def _(dve):
                c = Chain(dve, s_ct)
                c.link(dve.memset(cont[:, :], 0.0))
                c.link(dve.tensor_tensor(cont[:, 1:T], base_r[:, 1:T], last_r[:, 0:T - 1], ALU.is_equal))
                c.link(dve.tensor_tensor(single[:, :], base_r[:, :], last_r[:, :], ALU.is_equal))

        hN = stg[:, 4096:5120].rearrange("p (b f) -> p b f", b=4)
        hTs = stg[:, 5120:6144].rearrange("p (k n) -> p k n", k=K2)
        elr = work[:, 8192:8192 + 32 * 2 * RH].rearrange("p (b n) -> p b n", b=32)

        def layernorm4(dve, rows, c, std_done, std_ready, turn):
            for b in range(4):
                last = dve.bn_stats(stats[:, b, :], rows(b))
                c.link(last)
            dve.sem_inc(passed, 1)
            for b in range(4):
                dve.bn_aggr(mv[:, b, :], stats[:, b, :]).then_inc(c.sem, 1)
            c.n += 4
            dve.wait_ge(c.sem, c.before + c.n)
            dve.sem_inc(std_ready, 1)
            dve.wait_ge(std_done, turn + 1)
            c.link(dve.reciprocal(rstd[:, :], std[:, :]))

        s_n, s_vr, s_sd, s_hn, s_tp, s_ht, s_el, s_ee, s_et = [sem(x) for x in (
            "ln_steps", "var_ready", "std_done", "hn_ready", "hn_turned", "ht_ready", "el_ready",
            "el_kept", "el_stored")]
        LN_STEPS = 4 + 4 + 1
        with nc.Block() as block:
            @block.vector
            def _(dve):
                with dve.Fori(0, NC) as c8:
                    c = Chain(dve, s_n, c8 * LN_STEPS)
                    layernorm4(dve, lambda b: x_all[:, bass.ds(c8 * 4 + b, 1), :].rearrange("p o f -> p (o f)"),
                               c, s_sd, s_vr, c8)
                    dve.wait_ge(s_tp, c8 + 1)
                    for b in range(4):
                        ins = dve.tensor_scalar(hN[:, b, :], x_all[:, bass.ds(c8 * 4 + b, 1), :].rearrange(
                            "p o f -> p (o f)"), mv[:, b, 0:1], rstd[:, b:b + 1], ALU.subtract, ALU.mult)
                        ins.then_inc(s_hn, 1)
                    dve.wait_ge(s_hn, c8 * 4 + 4)
                    dve.wait_ge(s_el, c8 + 1)
                    dve.tensor_copy(elr[:, bass.ds(c8 * 4, 4), :],
                                    PS[:, 4, 0:256].rearrange("p (b n) -> p b n", b=4)).then_inc(s_ee, 1)

            @block.scalar
            def _(act):
                with act.Fori(0, NC) as c8:
                    act.wait_ge(s_vr, c8 + 1)
                    act.activation(std[:, :], mv[:, :, 1], ACT.Sqrt, bias=eps_c[:, :]).then_inc(s_sd, 1)
                    act.wait_ge(s_tp, c8 + 2)
                    for k in range(K2):
                        act.activation(hTs[:, k, :], PS[:, k, :], ACT.Relu).then_inc(s_ht, 1)
                    for k in range(K2):
                        act.activation(hT[:, k, bass.ds(c8 * CW, CW)], PS[:, k, :], ACT.Relu).then_inc(s_ht, 1)

            @block.tensor
            def _(pe):
                pe.sem_inc(s_tp, 1)
                with pe.Fori(0, NC) as c8:
                    pe.wait_ge(s_hn, c8 * 4 + 4)
                    for b in range(4):
                        for k in range(K2):
                            mm = pe.transpose(PS[:, k, b * P:(b + 1) * P], hN[:, b, k * P:(k + 1) * P], ident[:, :])
                    mm.then_inc(s_tp, 1)
                    pe.wait_ge(s_ht, c8 * 4 + 4)
                    for b in range(4):
                        for k in range(K2):
                            mm = pe.matmul(PS[:, 4, b * 2 * RH:(b + 1) * 2 * RH], hTs[:, k, b * P:(b + 1) * P],
                                           wlr[:, k, :], start=(k == 0), stop=(k == K2 - 1))
                    mm.then_inc(s_el, 1)
                    pe.wait_ge(s_ee, c8 + 1)

            @block.sync
            def _(sp):
                sp.wait_ge(s_ee, NC)
                for tab, o in ((el_tab, 0), (er_tab, RH)):
                    sp.dma_start(tab.rearrange("(b p) n -> p b n", p=P), elr[:, 0:NBLK + 1, o:o + RH]
                                 ).then_inc(s_et, 16)
                sp.wait_ge(s_et, 32)

        end_phase()

        dst_b = stg[:, 0:G * 512].rearrange("p (g n) -> p g n", g=G)
        onehotT = stg[:, 2560:2560 + G * 512].rearrange("p (g u n) -> p g u n", g=G, u=U)
        el_ring = stg[:, 5120:5120 + TB * RH].rearrange("p (s n) -> p s n", s=TB)
        er_ring = stg[:, 5760:5760 + TB * RH].rearrange("p (s n) -> p s n", s=TB)
        oh_b = sb("oh_b", [P, G, U, P], BF16)
        fblk = sb("fblk", [P, 2, K2, P])
        tsum = sb("tsum", [P, U, R, H])
        tmask = sb("tmask", [P, U, R])
        fout = work[:, 8192:8192 + 4096].rearrange("p (i n) -> p i n", i=2)
        s_gf, s_ix, s_is, s_oh, s_ohs, s_er, s_dg, s_da, s_post = [sem(x) for x in (
            "group_free", "idx_ready", "gathers_issued", "onehots_ready", "oh_bf_ready", "er_ready", "deg_ready",
            "deg_added", "post_steps")]
        s_ga = [sem(f"el_rows{g}") for g in range(G)]
        s_db = [sem(f"dst_rows{g}") for g in range(G)]
        s_ew = [sem(f"er_window{g}") for g in range(G)]
        s_fb, s_fm, s_fe, s_fd = sem("fblk_ready"), sem("feat_ready"), sem("feat_kept"), [
            sem("feat_stored0"), sem("feat_stored1")]
        s_fs = sem("feat_free")
        PRE = NC * 4 - TURNS_SORTED

        with nc.Block() as block:
            def feat_matmuls(pe, b, q):
                if q == 0:
                    pe.wait_ge(s_fb, b + 1)
                pe.wait_ge(s_fe, b * 4 + q + 1)
                for k in range(K2):
                    mm = pe.matmul(PS[:, 6 + q % 2, :], fblk[:, 0, k, :], wc[:, k, q * 512:(q + 1) * 512],
                                   start=(k == 0), stop=(k == K2 - 1))
                mm.then_inc(s_fm, 1)

            def feat_fetch(act, b):
                act.wait_ge(s_fm, b * 4 + 1)
                act.activation(fblk[:, 0, :, :], hT[:, :, bass.ds(b * P, P)], ACT.Copy).then_inc(s_fb, 1)

            def feat_keep(act, b, q):
                act.wait_ge(s_fm, b * 4 + q + 2)
                if q == 0:
                    act.wait_ge(s_fs, b * 16 + 16)
                act.activation(fout[:, 0, q * 512:(q + 1) * 512], PS[:, 6 + q % 2, :], ACT.Copy).then_inc(s_fe, 1)

            def feat_store(act, b):
                act.wait_ge(s_fe, b * 4 + 6)
                act.dma_start(feat_tab.rearrange("(n r) f -> n (r f)", r=R)[bass.ds(b * P, P), :],
                              fout[:, 0, :]).then_inc(s_fs, 16)

            @block.gpsimd
            def _(pool):
                n = turns_of(pool)
                with pool.Fori(0, n) as i:
                    for g in range(G):
                        pool.wait_ge(s_ix, i * G + g + 1)
                        pool.sem_inc(s_is, 1)
                        for u in range(U):
                            s = g * U + u
                            pool.indirect_dma_start(
                                out=el_ring[:, s, :], out_offset=None, in_=el_tab[:, :],
                                in_offset=bass.IndirectOffsetOnAxis(ap=idx_ring[:, s:s + 1], axis=0)
                            ).then_inc(s_ga[g], 16)

            @block.sync
            def _(sp):
                n = turns_of(sp)
                with sp.Fori(0, n) as i:
                    for g in range(G):
                        base = base_regs(sp)
                        sp.load(base, base_i[0:1, bass.ds(i * TB + g * U, U)])
                        sp.wait_ge(s_gf, i * G + g + 1)
                        sp.dma_start(dst_b[:, g, :],
                                     dstm_row.rearrange("(o c) p j -> o (c p j)", o=1)[
                                         :, bass.ds((i * TB + g * U) * P, U * P)].to_broadcast([P, U * P])
                                     ).then_inc(s_db[g], 16)
                        for u in range(U):
                            b0 = sp.snap(base[u], min_val=0, max_val=N - 1)
                            sp.dma_start(er_ring[:, g * U + u, :], er_tab[bass.ds(b0, P), :]).then_inc(s_ew[g], 16)

            @block.scalar
            def _(act):
                n = turns_of(act)
                act.sem_inc(s_fs, 16)

                def feat_all(b):
                    feat_fetch(act, b)
                    for q in range(4):
                        feat_keep(act, b, q)
                    feat_store(act, b)

                with act.Fori(0, PRE) as b:
                    feat_all(b)
                with act.Fori(0, n) as i:
                    b = i + PRE
                    for g in range(G):
                        act.wait_ge(s_gf, i * G + g + 1)
                        act.copy(idx_ring[:, g * U:(g + 1) * U], src_i[:, bass.ds(i * TB + g * U, U)]
                                 ).then_inc(s_ix, 1)
                        if g == 0:
                            feat_fetch(act, b)
                        else:
                            feat_keep(act, b, g - 1)
                    feat_store(act, b)
                act.wait_ge(s_fs, (n + PRE) * 16 + 16)
                act.sem_inc(passed, 1)

            @block.tensor
            def _(pe):
                n = turns_of(pe)
                pe.sem_inc(s_fm, 1)
                pe.sem_inc(s_fe, 2)
                with pe.Fori(0, PRE) as b:
                    for q in range(4):
                        feat_matmuls(pe, b, q)
                with pe.Fori(0, n) as i:
                    for g in range(G):
                        pe.wait_ge(s_ew[g], i * 16 * U + 16 * U)
                        pe.wait_ge(s_gf, i * G + g + G - 1)
                        for u in range(U):
                            s = g * U + u
                            pe.wait_ge(s_oh, i * 2 * TB + 2 * s + 2)
                            pe.matmul(PS[:, 3 + BANK[g], u * RH:(u + 1) * RH], onehotT[:, g, u, :], er_ring[:, s, :],
                                      start=True, stop=True)
                            pe.matmul(PS[:, BANK[g], u * P:(u + 1) * P], ones_b[:, :],
                                      oh_b[:, g, u, :], start=True, stop=True).then_inc(s_er, 1)
                        if g < 4:
                            feat_matmuls(pe, i + PRE, g)

            POST = 4

            @block.vector
            def _(dve):
                n = turns_of(dve)
                dve.memset(deg[:, :], 0.0).then_inc(s_da, 1)
                dve.memset(small[:, 0:1], 0.0).then_inc(s_gf, G)
                with dve.Fori(0, n) as i:
                    for g in range(G):
                        base = base_regs(dve)
                        dve.load(base, base_i[0:1, bass.ds(i * TB + g * U, U)])
                        base = [dve.snap(b, min_val=0, max_val=N - 1) for b in base]
                        dve.wait_ge(s_db[g], i * 16 + 16)
                        for u in range(U):
                            s = g * U + u
                            t = bass.ds(i * TB + s, 1)
                            dve.tensor_scalar(onehotT[:, g, u, :], dst_b[:, g, u * P:(u + 1) * P], nodeid[:, t],
                                              None, ALU.is_equal).then_inc(s_oh, 1)
                            dve.tensor_scalar(oh_b[:, g, u, :], iota_w[:, :], dstloc[:, t], None,
                                              ALU.is_equal).then_inc(s_oh, 1)
                        c = Chain(dve, s_post, i * (POST * G) + g * POST)
                        c.link(dve.tensor_tensor(
                            tmask[:, :, :], typ_t[:, bass.ds(i * TB + g * U, U)].unsqueeze(2).to_broadcast([P, U, R]),
                            iota_w[:, 0:R].unsqueeze(1).to_broadcast([P, U, R]), ALU.is_equal))
                        for u in range(U):
                            s, b0 = g * U + u, base[u]
                            dve.wait_ge(s_er, i * TB + (g + 1) * U)
                            dve.wait_ge(s_da, i * TB + s + 1)
                            dve.tensor_tensor(deg[:, bass.ds(b0, P)], deg[:, bass.ds(b0, P)],
                                              PS[:, BANK[g], u * P:(u + 1) * P], ALU.add
                                              ).then_inc(s_da, 1)
                        dve.wait_ge(s_ga[g], i * 16 * U + 16 * U)
                        erp = PS[:, 3 + BANK[g], 0:U * RH]
                        c.link(dve.tensor_tensor(tsum[:, :, :, :].rearrange("p u r h -> p (u r h)"), erp,
                                                 el_ring[:, g * U:(g + 1) * U, :].rearrange("p u n -> p (u n)"),
                                                 ALU.add))
                        c.link(dve.tensor_tensor(tsum[:, :, :, :].rearrange("p u r h -> p (u r) h"),
                                                 tsum[:, :, :, :].rearrange("p u r h -> p (u r) h"),
                                                 tmask[:, :, :].rearrange("p u r -> p (u r)").unsqueeze(2)
                                                 .to_broadcast([P, U * R, H]), ALU.mult))
                        last = dve.tensor_reduce(alpha[:, bass.ds(i * TB + g * U, U), :],
                                                 tsum[:, :, :, :].rearrange("p u r h -> p u h r"), AX.X, ALU.add)
                        c.link(last)
                        dve.sem_inc(s_gf, 1)
                dve.wait_ge(s_da, n * TB + 1)
                dve.sem_inc(passed, 1)

        end_phase()

        V, FW, BW = [w.rearrange("p (h c j) -> p h c j", h=H, c=CT) for w in (
            work[:, 0:4 * T], work[:, 4 * T:8 * T], work[:, 8 * T:12 * T])]
        TM = work[:, 12 * T:16 * T].rearrange("p (h c j) -> p h c j", h=H, c=CT)
        hflat = rows4
        AR, FR, PR, SR, CR, DR, CM, CS, CB = [hflat[:, i * T:(i + 1) * T] for i in range(9)]
        CONTM = hflat[:, 9 * T:10 * T + 1]
        flat = lambda a: a.rearrange("p h c j -> p (h c j)")
        lane = lambda a, h: a[:, h, :, :].rearrange("p c j -> p (c j)")
        neg = stg[:, 0:T + 1]
        fneg, lneg = stg[:, 700:700 + T], stg[:, 1400:1400 + T]

        s_q, s_qt, s_qe = sem("scores_ready"), sem("scores_turned"), sem("scores_kept")
        with nc.Block() as block:
            @block.vector
            def _(dve):
                c = Chain(dve, s_q)
                a2 = alpha[:, :, :].rearrange("p t h -> p (t h)")
                c.link(dve.tensor_tensor(alpha[:, :, :], alpha[:, :, :],
                                         pad_t[:, :].unsqueeze(2).to_broadcast([P, T, H]), ALU.add))
                c.link(dve.scalar_tensor_tensor(a2, a2, SLOPE, a2, ALU.mult, ALU.max))
                for i in range(CT):
                    dve.wait_ge(s_qt, i + 1)
                    dve.tensor_copy(V[:, :, i, :], PS[:, i, :].rearrange("p (h j) -> p h j", h=H)).then_inc(s_qe, 1)
                c.link(dve.tensor_scalar(neg[:, :], same[:, :], 1.0, BIG, ALU.subtract, ALU.mult))
                c.link(dve.tensor_scalar(fneg, firstm[:, :], 1.0, BIG, ALU.subtract, ALU.mult))
                c.link(dve.tensor_scalar(lneg, lastm[:, :], 1.0, BIG, ALU.subtract, ALU.mult))
                dve.wait_ge(s_qe, CT)

            @block.tensor
            def _(pe):
                pe.wait_ge(s_q, 2)
                for i in range(CT):
                    for h in range(H):
                        mm = pe.transpose(PS[:, i, h * P:(h + 1) * P], alpha[:, i * P:(i + 1) * P, h], ident[:, :])
                    mm.then_inc(s_qt, 1)

        def segment(op_in, op, zero, mask, fmask, lmask):
            s_s, s_p, s_b = sem("segment_steps"), sem("ends_turned"), sem("carries_turned")
            with nc.Block() as block:
                @block.vector
                def _(dve):
                    c = Chain(dve, s_s)
                    for h in range(H):
                        dve.tensor_tensor_scan(lane(FW, h), mask[:, 0:T], lane(V, h), zero, op_in, op).then_inc(s_s, 1)
                        dve.tensor_tensor_scan(lane(BW, h)[:, ::-1], mask[:, 1:T + 1][:, ::-1],
                                               lane(V, h)[:, ::-1], zero, op_in, op).then_inc(s_s, 1)
                    c.n = 2 * H
                    dve.wait_ge(s_s, 2 * H)
                    c.link(dve.tensor_tensor(CS, cont[:, 0:T], single[:, :], ALU.mult))
                    c.link(dve.tensor_tensor(CB, cont[:, 1:T + 1], single[:, :], ALU.mult))
                    c.link(dve.tensor_copy(CONTM, cont[:, :]))
                    if zero:
                        for m in (CS, CB, CONTM):
                            c.link(dve.tensor_scalar(m, m, 1.0, BIG, ALU.subtract, ALU.mult))
                    dve.wait_ge(s_p, 1)
                    for i, to in enumerate((AR, FR)):
                        c.link(dve.tensor_copy(to[:, 0:512], PS[0:H, 2 * i, :]))
                        c.link(dve.tensor_copy(to[:, 512:T], PS[0:H, 2 * i + 1, 0:P]))
                    c.link(dve.tensor_tensor_scan(PR, CS, AR, zero, op_in, op))
                    c.link(dve.tensor_tensor_scan(SR[:, ::-1], CB[:, ::-1], FR[:, ::-1], zero, op_in, op))
                    c.link(dve.memset(CR, zero))
                    c.link(dve.memset(DR, zero))
                    c.link(dve.tensor_tensor(CR[:, 1:T], PR[:, 0:T - 1], CONTM[:, 1:T], op_in))
                    c.link(dve.tensor_tensor(DR[:, 0:T - 1], SR[:, 1:T], CONTM[:, 1:T], op_in))
                    dve.sem_inc(s_b, 1)
                    dve.wait_ge(s_b, 3)
                    c.link(dve.tensor_copy(cT[:, :, :, :].rearrange("p i c h -> p (i c h)"), PS[:, 4, 0:2 * CT * H]))
                    c.link(dve.tensor_tensor(flat(FW), flat(FW), flat(BW), op))
                    if not zero:
                        c.link(dve.tensor_tensor(flat(FW), flat(FW), flat(V), ALU.subtract))
                    for i, m in enumerate((fmask, lmask)):
                        for h in range(H):
                            c.link(dve.tensor_tensor(TM[:, h, :, :], m.rearrange("p (c j) -> p c j", c=CT),
                                                     cT[:, i, :, h:h + 1].to_broadcast([P, CT, P]), op_in))
                        c.link(dve.tensor_tensor(flat(FW), flat(FW), flat(TM), op))

                @block.tensor
                def _(pe):
                    pe.wait_ge(s_s, 2 * H)
                    for i, (a, j) in enumerate(((FW, P - 1), (BW, 0))):
                        for cc in range(CT):
                            mm = pe.transpose(PS[0:H, 2 * i + cc // 4, (cc % 4) * P:(cc % 4 + 1) * P],
                                              a[:, :, cc, j], ident[:, :])
                    mm.then_inc(s_p, 1)
                    pe.wait_ge(s_b, 1)
                    for i, a in enumerate((CR, DR)):
                        for cc in range(CT):
                            mm = pe.transpose(PS[:, 4, (i * CT + cc) * H:(i * CT + cc + 1) * H],
                                              a[:, cc * P:(cc + 1) * P], ident[0:H, 0:H])
                    mm.then_inc(s_b, 2)

        segment(ALU.add, ALU.max, -BIG, neg, fneg, lneg)
        s_x, s_xe = sem("shifted"), sem("exps_ready")
        with nc.Block() as block:
            @block.vector
            def _(dve):
                dve.tensor_tensor(flat(V), flat(V), flat(FW), ALU.subtract).then_inc(s_x, 1)

            @block.scalar
            def _(act):
                act.wait_ge(s_x, 1)
                act.activation(flat(V), flat(V), ACT.Exp).then_inc(s_xe, 1)
                act.wait_ge(s_xe, 1)
        segment(ALU.mult, ALU.add, 0.0, same, firstm[:, :], lastm[:, :])
        s_al, s_at, s_ae = sem("alphas_ready"), sem("alphas_turned"), sem("alphas_kept")
        with nc.Block() as block:
            @block.vector
            def _(dve):
                c = Chain(dve, s_al)
                c.link(dve.reciprocal(flat(FW), flat(FW)))
                c.link(dve.tensor_tensor(flat(V), flat(V), flat(FW), ALU.mult))
                for i in range(CT):
                    dve.wait_ge(s_at, i + 1)
                    dve.tensor_copy(alpha[:, i * P:(i + 1) * P, :].rearrange("p t h -> p h t"),
                                    PS[:, i, :].rearrange("p (h t) -> p h t", h=H)).then_inc(s_ae, 1)
                dve.wait_ge(s_ae, CT)

            @block.tensor
            def _(pe):
                pe.wait_ge(s_al, 2)
                for i in range(CT):
                    for h in range(H):
                        mm = pe.transpose(PS[:, i, h * P:(h + 1) * P], V[:, h, i, :], ident[:, :])
                    mm.then_inc(s_at, 1)

        onehot = stg[:, 0:TB * P].rearrange("p (s n) -> p s n", s=TB)

        def edge_pass(table, idx, scaled):
            s_gf, s_ix, s_is, s_oh, s_mm, s_add = [sem(x) for x in (
                "group_free", "idx_ready", "gathers_issued", "rows_ready", "tile_summed", "tile_added")]
            s_ga = [sem(f"rows{g}") for g in range(G)]
            with nc.Block() as block:
                @block.gpsimd
                def _(pool):
                    n = turns_of(pool)
                    with pool.Fori(0, n) as i:
                        for g in range(G):
                            pool.wait_ge(s_ix, i * G + g + 1)
                            pool.sem_inc(s_is, 1)
                            for u in range(U):
                                s = g * U + u
                                pool.indirect_dma_start(
                                    out=ring[:, s, :], out_offset=None, in_=table[:, :],
                                    in_offset=bass.IndirectOffsetOnAxis(ap=idx_ring[:, s:s + 1], axis=0)
                                ).then_inc(s_ga[g], 16)

                @block.scalar
                def _(act):
                    n = turns_of(act)
                    with act.Fori(0, n) as i:
                        for g in range(G):
                            act.wait_ge(s_mm, i * TB + g * U + U)
                            act.copy(idx_ring[:, g * U:(g + 1) * U], idx[:, bass.ds(i * TB + g * U, U)]
                                     ).then_inc(s_ix, 1)

                @block.tensor
                def _(pe):
                    n = turns_of(pe)
                    pe.sem_inc(s_mm, TB)
                    with pe.Fori(0, n) as i:
                        for g in range(G):
                            if not scaled:
                                pe.wait_ge(s_ga[g], i * 16 * U + 16 * U)
                            for u in range(U):
                                s = g * U + u
                                pe.wait_ge(s_oh, i * TB + s + 1)
                                pe.wait_ge(s_add, i * TB + (s | 1) + 1)
                                slot = s % PS_TILES
                                for k in range(K2):
                                    mm = pe.matmul(PS[:, slot // 2, (slot % 2) * F + k * P:(slot % 2) * F + (k + 1) * P],
                                                   ring[:, s, k * P:(k + 1) * P], onehot[:, s, :],
                                                   start=True, stop=True)
                                mm.then_inc(s_mm, 1)

                @block.vector
                def _(dve):
                    n = turns_of(dve)
                    dve.memset(acc[:, :, :], 0.0).then_inc(s_add, PS_TILES)
                    with dve.Fori(0, n) as i:
                        for g in range(G):
                            base = base_regs(dve)
                            dve.load(base, base_i[0:1, bass.ds(i * TB + g * U, U)])
                            for u in range(U):
                                s = g * U + u
                                t = bass.ds(i * TB + s, 1)
                                dve.wait_ge(s_mm, i * TB + s + 1)
                                oh = dve.tensor_scalar(onehot[:, s, :], iota_w[:, :], dstloc[:, t], None,
                                                       ALU.is_equal)
                                if scaled and u == 0:
                                    dve.wait_ge(s_ga[g], i * 16 * U + 16 * U)
                                if scaled:
                                    rs = ring[:, s, :].rearrange("p (h d) -> p h d", h=H)
                                    al = alpha[:, t, :].rearrange("p o h -> p (o h)").unsqueeze(2)
                                    oh = dve.tensor_tensor(rs, rs, al.to_broadcast([P, H, D]), ALU.mult)
                                oh.then_inc(s_oh, 1)
                            for u in range(U):
                                s = g * U + u
                                slot = s % PS_TILES
                                b0 = dve.snap(base[u], min_val=0, max_val=N - 1)
                                dve.wait_ge(s_mm, i * TB + (s | 1) + TB + 1)
                                dve.wait_ge(s_add, i * TB + s + PS_TILES)
                                a = acc[:, :, bass.ds(b0, P)]
                                dve.tensor_tensor(a, a, PS[:, slot // 2, (slot % 2) * F:(slot % 2 + 1) * F]
                                                  .rearrange("p (k n) -> p k n", k=K2), ALU.add).then_inc(s_add, 1)
                    dve.wait_ge(s_add, n * TB + PS_TILES)
                    dve.sem_inc(passed, 1)

        end_phase()
        edge_pass(feat_tab[0:NBLK * P * R, :], fidx_i, True)

        win = wbuf[:, 0:512].rearrange("p (k n) -> p k n", k=K2)
        wout = wbuf[:, 512:1024].rearrange("p (k n) -> p k n", k=K2)
        wag = wbuf[:, 1024:2560].rearrange("p (l k n) -> p l k n", l=LAYERS, k=K2)
        wse = wbuf[:, 2560:4096].rearrange("p (l k n) -> p l k n", l=LAYERS, k=K2)
        xs, ac, x1s, tab = [stg[:, 1024 * i:1024 * (i + 1)] for i in range(4)]
        b4 = lambda a: a.rearrange("p (b f) -> p b f", b=4)
        k2 = lambda a: a.rearrange("p (k n) -> p k n", k=K2)
        s_w, s_xl, s_xf, s_ac, s_t1, s_x1, s_n, s_vr, s_sd, s_hn, s_t2, s_ht, s_m1, s_m2, s_tb, s_st, s_dg = [sem(a) for a in (
            "weights_loaded", "x_loaded", "x_free", "acc_fetched", "acc_turned", "x1_ready", "ln_steps", "var_ready",
            "std_done", "hn_ready", "hn_turned", "ht_ready", "rows_ready", "cols_ready", "table_ready", "stored",
            "deg_steps")]
        s_ht2 = sem("h0_kept")
        x1_rows = x1_tab.rearrange("(c b p) f -> c p b f", b=4, p=P)
        h_rows = [t.rearrange("(c b p) f -> c p b f", b=4, p=P) for t in h_tab]
        LASTB = N - (NC - 1) * CW - P
        with nc.Block() as block:
            @block.sync
            def _(sp):
                for to, w in ((win, w_in), (wout, w_out)):
                    sp.dma_start(to, w.rearrange("(k p) n -> p k n", p=P)).then_inc(s_w, 16)
                for to, w in ((wag, w_agg), (wse, w_self)):
                    for l in range(LAYERS):
                        sp.dma_start(to[:, l, :, :], w[l].rearrange("(k p) n -> p k n", p=P)).then_inc(s_w, 16)

                def load_x(c8, last):
                    sp.wait_ge(s_xf, c8 + 1)
                    if not last:
                        sp.dma_start(b4(xs), x[bass.ds(c8 * CW, CW), :].rearrange("(b p) f -> p b f", p=P)
                                     ).then_inc(s_xl, 32)
                    else:
                        sp.dma_start(b4(xs)[:, 0, :], x[c8 * CW:c8 * CW + P, :]).then_inc(s_xl, 16)
                        sp.dma_start(b4(xs)[0:LASTB, 1, :], x[c8 * CW + P:N, :]).then_inc(s_xl, 16)

                with sp.Fori(0, NC - 1) as c8:
                    load_x(c8, False)
                load_x(NC - 1, True)
                sp.wait_ge(s_w, 16 * (2 + 2 * LAYERS))

            @block.scalar
            def _(act):
                with act.Fori(0, NC) as c8:
                    act.wait_ge(s_t1, c8 + 1)
                    for k in range(K2):
                        act.activation(k2(ac)[:, k, :], acc[:, k, bass.ds(c8 * CW, CW)], ACT.Identity,
                                       bias=hb_c[:, k:k + 1]).then_inc(s_ac, 1)
                    act.wait_ge(s_vr, c8 + 1)
                    act.activation(std[:, :], mv[:, :, 1], ACT.Sqrt, bias=eps_c[:, :]).then_inc(s_sd, 1)
                    act.wait_ge(s_t2, c8 + 2)
                    for k in range(K2):
                        act.activation(hTs[:, k, :], PS[:, 2 + k, :], ACT.Relu).then_inc(s_ht, 1)
                    act.wait_ge(s_x1, 2 * c8 + 2)
                    act.dma_start(x1_rows[bass.ds(c8, 1), :, :, :].rearrange("o p b f -> p (o b) f"), b4(x1s)
                                  ).then_inc(s_st, 16)
                    act.wait_ge(s_m2, c8 + 1)
                    for k in range(K2):
                        act.activation(hT[:, k, bass.ds(c8 * CW, CW)], PS[:, 6 + k, :], ACT.Identity,
                                       bias=bin_c[:, k:k + 1]).then_inc(s_ht2, 1)
                    act.wait_ge(s_tb, 2 * c8 + 2)
                    act.dma_start(h_rows[0][bass.ds(c8, 1), :, :, :].rearrange("o p b f -> p (o b) f"), b4(tab)
                                  ).then_inc(s_st, 16)
                act.wait_ge(s_st, 32 * NC)

            @block.tensor
            def _(pe):
                pe.sem_inc(s_t1, 1)
                pe.sem_inc(s_t2, 1)
                pe.wait_ge(s_w, 16 * (2 + 2 * LAYERS))
                with pe.Fori(0, NC) as c8:
                    pe.wait_ge(s_ac, 2 * c8 + 2)
                    for b in range(4):
                        for k in range(K2):
                            mm = pe.transpose(PS[:, b // 2, (b % 2) * F + k * P:(b % 2) * F + (k + 1) * P],
                                              k2(ac)[:, k, b * P:(b + 1) * P], ident[:, :])
                    mm.then_inc(s_t1, 1)
                    pe.wait_ge(s_hn, 4 * c8 + 4)
                    for b in range(4):
                        for k in range(K2):
                            mm = pe.transpose(PS[:, 2 + k, b * P:(b + 1) * P], hN[:, b, k * P:(k + 1) * P], ident[:, :])
                    mm.then_inc(s_t2, 1)
                    pe.wait_ge(s_ht, 2 * c8 + 2)
                    for b in range(4):
                        for k in range(K2):
                            mm = pe.matmul(PS[:, 4 + b // 2, (b % 2) * F:(b % 2 + 1) * F], hTs[:, k, b * P:(b + 1) * P],
                                           win[:, k, :], start=(k == 0), stop=(k == K2 - 1))
                    mm.then_inc(s_m1, 1)
                    for f in range(K2):
                        for k in range(K2):
                            mm = pe.matmul(PS[:, 6 + f, :], win[:, k, f * P:(f + 1) * P], hTs[:, k, :],
                                           start=(k == 0), stop=(k == K2 - 1))
                    mm.then_inc(s_m2, 1)
                    pe.wait_ge(s_ht2, 2 * c8 + 2)
                    pe.wait_ge(s_tb, 2 * c8 + 2)

            @block.vector
            def _(dve):
                c = Chain(dve, s_dg)
                c.link(dve.tensor_scalar(deg[:, :], deg[:, :], 1.0, None, ALU.max))
                c.link(dve.reciprocal(deg[:, :], deg[:, :]))
                c.link(dve.memset(xs, 0.0))
                dve.sem_inc(s_xf, 1)
                with dve.Fori(0, NC) as c8:
                    dve.wait_ge(s_xl, 32 * c8 + 32)
                    dve.wait_ge(s_t1, c8 + 2)
                    dve.wait_ge(s_st, 32 * c8 + 1) if False else None
                    for j in range(2):
                        dve.tensor_tensor(x1s[:, j * 512:(j + 1) * 512], PS[:, j, :], xs[:, j * 512:(j + 1) * 512],
                                          ALU.add).then_inc(s_x1, 1)
                    dve.wait_ge(s_x1, 2 * c8 + 2)
                    dve.sem_inc(s_xf, 1)
                    c = Chain(dve, s_n, c8 * LN_STEPS)
                    layernorm4(dve, lambda b: b4(x1s)[:, b, :], c, s_sd, s_vr, c8)
                    for b in range(4):
                        dve.tensor_scalar(hN[:, b, :], b4(x1s)[:, b, :], mv[:, b, 0:1], rstd[:, b:b + 1],
                                          ALU.subtract, ALU.mult).then_inc(s_hn, 1)
                    dve.wait_ge(s_hn, 4 * c8 + 4)
                    dve.wait_ge(s_m1, c8 + 1)
                    for j in range(2):
                        dve.tensor_tensor(tab[:, j * 512:(j + 1) * 512].rearrange("p (b f) -> p b f", b=2),
                                          PS[:, 4 + j, :].rearrange("p (b f) -> p b f", b=2),
                                          bin_b[:, :].unsqueeze(1).to_broadcast([P, 2, F]), ALU.add).then_inc(s_tb, 1)
                    dve.wait_ge(s_st, 32 * c8 + 32)

        sc, hn, ts = [stg[:, 2560 + 1024 * i:2560 + 1024 * (i + 1)] for i in range(3)]

        def hidden(l):
            last_layer = l == LAYERS - 1
            table = h_rows[(l + 1) % 2]
            s_so = sem("tail_stored")
            s_sc, s_mm, s_hr, s_tn, s_tk, s_st, s_hk, s_xl = [sem(a) for a in (
                "agg_scaled", "layer_summed", "h_ready", "h_turned", "table_ready", "stored", "h_kept", "x1_loaded")]
            with nc.Block() as block:
                @block.vector
                def _(dve):
                    with dve.Fori(0, NC) as c8:
                        cols = bass.ds(c8 * CW, CW)
                        dve.wait_ge(s_mm, c8 + 1)
                        for k in range(K2):
                            dve.tensor_tensor(k2(sc)[:, k, :], acc[:, k, cols], deg[:, cols], ALU.mult
                                              ).then_inc(s_sc, 1)
                        if not last_layer:
                            dve.wait_ge(s_hr, 2 * c8 + 2)
                            dve.tensor_copy(hT[:, :, cols], k2(hn)).then_inc(s_hk, 1)
                            dve.wait_ge(s_hk, c8 + 1)
                        dve.wait_ge(s_tn, c8 + 1)
                        if last_layer:
                            dve.wait_ge(s_xl, 16 * c8 + 16)
                        for j in range(2):
                            o = ts[:, j * 512:(j + 1) * 512]
                            if last_layer:
                                dve.tensor_tensor(x1b[:, j * 512:(j + 1) * 512], x1b[:, j * 512:(j + 1) * 512],
                                                  PS[:, 2 + j, :], ALU.add).then_inc(s_hk, 1)
                                dve.wait_ge(s_hk, 2 * c8 + j + 1)
                                dve.tensor_tensor(o.rearrange("p (b f) -> p b f", b=2),
                                                  x1b[:, j * 512:(j + 1) * 512].rearrange("p (b f) -> p b f", b=2),
                                                  bout_b[:, :].unsqueeze(1).to_broadcast([P, 2, F]), ALU.add
                                                  ).then_inc(s_tk, 1)
                            else:
                                dve.tensor_copy(o, PS[:, 2 + j, :]).then_inc(s_tk, 1)
                        dve.wait_ge(s_tk, 2 * c8 + 2)
                        dve.wait_ge(s_st, 16 * c8 + 16)

                @block.tensor
                def _(pe):
                    pe.sem_inc(s_mm, 1)
                    with pe.Fori(0, NC) as c8:
                        pe.wait_ge(s_sc, 2 * c8 + 2)
                        for f in range(K2):
                            for k in range(K2):
                                pe.matmul(PS[:, f, :], wse[:, l, k, f * P:(f + 1) * P], hT[:, k, bass.ds(c8 * CW, CW)],
                                          start=(k == 0), stop=False)
                            for k in range(K2):
                                mm = pe.matmul(PS[:, f, :], wag[:, l, k, f * P:(f + 1) * P], k2(sc)[:, k, :],
                                               start=False, stop=(k == K2 - 1))
                        mm.then_inc(s_mm, 1)
                        pe.wait_ge(s_hr, 2 * c8 + 2)
                        for b in range(4):
                            o = PS[:, 2 + b // 2, (b % 2) * F:(b % 2 + 1) * F]
                            for k in range(K2):
                                hb = k2(hn)[:, k, b * P:(b + 1) * P]
                                if last_layer:
                                    mm = pe.matmul(o, hb, wout[:, k, :], start=(k == 0), stop=(k == K2 - 1))
                                else:
                                    mm = pe.transpose(o[:, k * P:(k + 1) * P], hb, ident[:, :])
                        mm.then_inc(s_tn, 1)
                        pe.wait_ge(s_tk, 2 * c8 + 2)

                @block.scalar
                def _(act):
                    with act.Fori(0, NC) as c8:
                        act.wait_ge(s_mm, c8 + 2)
                        for f in range(K2):
                            act.activation(k2(hn)[:, f, :], PS[:, f, :], ACT.Relu, bias=bh_c[:, l, f:f + 1]
                                           ).then_inc(s_hr, 1)

                @block.sync
                def _(sp):
                    def store(c8, last):
                        if last_layer:
                            sp.dma_start(b4(x1b), x1_rows[bass.ds(c8, 1), :, :, :].rearrange("o p b f -> p (o b) f")
                                         ).then_inc(s_xl, 16)
                        sp.wait_ge(s_tk, 2 * c8 + 2)
                        if not last_layer:
                            sp.dma_start(table[bass.ds(c8, 1), :, :, :].rearrange("o p b f -> p (o b) f"), b4(ts)
                                         ).then_inc(s_st, 16)
                        elif not last:
                            sp.dma_start(out[bass.ds(c8 * CW, CW), :].rearrange("(b p) f -> p b f", p=P), b4(ts)
                                         ).then_inc(s_st, 16)
                        else:
                            sp.dma_start(out[c8 * CW:c8 * CW + P, :], b4(ts)[:, 0, :]).then_inc(s_st, 16)
                            sp.dma_start(out[c8 * CW + P:N, :], b4(ts)[0:LASTB, 1, :]).then_inc(s_so, 16)
                            sp.wait_ge(s_so, 16)
                        if last:
                            sp.wait_ge(s_st, 16 * NC)
                        elif last_layer:
                            sp.wait_ge(s_st, 16 * c8 + 16)
                            sp.sem_inc(passed, 1)

                    with sp.Fori(0, NC - 1) as c8:
                        store(c8, False)
                    store(NC - 1, True)

        x1b = stg[:, 0:1024]
        for l in range(LAYERS):
            end_phase()
            edge_pass(h_tab[l % 2], src_i, False)
            hidden(l)


_INS = ["x", "src", "dst", "edge_type_8", "L0_gnn_conv_weights", "L0_gnn_attn_l", "L0_gnn_attn_r",
        "L0_gnn_h_bias", "L1_gnn_W_in", "L1_gnn_b_in", "L1_gnn_W_agg", "L1_gnn_W_self", "L1_gnn_b_hid",
        "L1_gnn_W_out", "L1_gnn_b_out"]


def kernel(**inputs):
    import numpy as _np
    import concourse.bacc as _bacc
    from concourse import mybir as _mybir
    from concourse.bass_utils import run_bass_kernel_spmd as _run

    nc = _bacc.Bacc("TRN2", target_bir_lowering=False, num_devices=1)
    arrays, args = {}, []
    for name in _INS:
        a = _np.ascontiguousarray(inputs[name])
        arrays[f"in_{name}"] = a
        args.append(nc.dram_tensor(f"in_{name}", a.shape, _mybir.dt.from_np(a.dtype), kind="ExternalInput").ap())
    args.append(nc.dram_tensor("out_0", (N, F), _mybir.dt.float32, kind="ExternalOutput").ap())
    gnn_kernel(nc, *args)
    r = _run(nc, [arrays], core_ids=[0])
    return r.results[0]["out_0"]
```

```python
import concourse.bass as bass
from concourse import mybir
from contextlib import ExitStack, nullcontext

FP32 = mybir.dt.float32
BF16 = mybir.dt.bfloat16
I32 = mybir.dt.int32
ALU = mybir.AluOpType
ACT = mybir.ActivationFunctionType
AX = mybir.AxisListType

P = 128
N, E, F, R, H, D = 3750, 63750, 256, 8, 4, 64
LAYERS = 3
K2 = F // P
NBLK = (N + P - 1) // P
NC = 8
CW = 4 * P
NP = NC * CW
NTAB = (NBLK + 1) * P
RH = R * H
KW = 32
U, G = 4, 6
TB = U * G
ADDED = U
TURNS = -(-E // (P * TB))
TURNS_SORTED = -(-(E + ADDED * N) // (P * TB))
CT = 5
T = CT * P
NG = T // U
FBLK = TURNS_SORTED * G // 4 + 1
BIG = 1e30
EPS = 1e-5
SLOPE = 0.2
NBANK = 3
WLEN = 8192 + TB * F


class Chain:

    def __init__(self, eng, sem, before=0):
        self.eng, self.sem, self.before, self.n = eng, sem, before, 0

    def link(self, ins):
        ins.then_inc(self.sem, 1)
        self.n += 1
        self.eng.wait_ge(self.sem, self.before + self.n)


def gnn_kernel(nc, x, src, dst, etype, conv_w, attn_l, attn_r, h_bias, w_in, b_in, w_agg, w_self,
               b_hid, w_out, b_out, out):
    ctx = ExitStack()
    with ctx:
        def sb(name, shape, dt=FP32):
            return ctx.enter_context(nc.sbuf_tensor(name, shape, dt))

        def dram(name, shape, dt=FP32):
            return nc.dram_tensor(name, shape, dt, kind="Internal").ap()

        names = {}

        phase_sems = []

        def sem(name):
            names[name] = names.get(name, 0) + 1
            s = nc.alloc_semaphore(f"{name}_{names[name]}")
            phase_sems.append(s)
            return s

        passed = nc.alloc_semaphore("passed")
        s_ga = [nc.alloc_semaphore(f"rows_gathered{g}") for g in range(G)]

        def end_phase():
            with nc.Block() as block:
                @block.gpsimd
                def _(pool):
                    for s in phase_sems:
                        pool.sem_clear(s)
            for s in phase_sems:
                nc.release_semaphore(s)
            phase_sems.clear()

        el_tab = dram("el_tab", [NTAB, RH + KW])
        er_tab = dram("er_tab", [NTAB, RH + KW])
        feat_tab = dram("feat_tab", [FBLK * P * R, F])
        x1_tab = dram("x1_tab", [NP, F])
        h_tab = dram("h_tab", [NP, F])
        dstm_row = dram("dstm_row", [CT, P, P])

        work = sb("work", [P, WLEN])
        hT = sb("hT", [P, K2, FBLK * P])
        deg = sb("deg", [P, NP])
        wbuf = sb("wbuf", [P, 4096])
        stg = sb("stg", [P, 6400])
        acc = work[:, 0:8192].rearrange("p (k n) -> p k n", k=K2)
        ring = work[:, 8192:WLEN].rearrange("p (s f) -> p s f", s=TB)
        src_i = sb("src_i", [P, T], I32)
        fidx_i = sb("fidx_i", [P, T], I32)
        dstloc = sb("dstloc", [P, T])
        nodeid = sb("nodeid", [P, NG])
        typ_t = sb("typ_t", [P, T])
        pad_t = sb("pad_t", [P, T])
        alpha = sb("alpha", [P, T, H])
        base_i = sb("base_i", [1, NG], I32)
        io_i = sb("io_i", [P, P + 1], I32)
        iota_w = sb("iota_w", [P, P])
        iota_p = sb("iota_p", [P, 1])
        ident = sb("ident", [P, P])
        ones = sb("ones", [P, P])
        ones_b = sb("ones_b", [P, P], BF16)
        hb_c = sb("hb_c", [P, K2])
        bin_c = sb("bin_c", [P, K2])
        bh_c = sb("bh_c", [P, LAYERS, K2])
        bout_b = sb("bout_b", [P, F])
        wlr = sb("wlr", [P, K2, 2 * RH])
        eps_c = sb("eps_c", [P, 1])
        stats = sb("stats", [P, 2, 4, 6])
        mv = sb("mv", [P, 2, 4, 2])
        std = sb("std", [P, 2, 4])
        rstd = sb("rstd", [P, 2, 4])
        idx_ring = sb("idx_ring", [P, TB], I32)
        small = sb("small", [P, 64])
        turns_i = sb("turns_i", [1, 2], I32)
        flags_i = sb("flags_i", [1, 2], I32)
        msum = sb("msum", [KW, 3 * KW])
        cT = sb("cT", [P, 2, CT, H])
        PS = ctx.enter_context(nc.psum_tensor("PS", [P, 8, 512], FP32))

        held = {}

        def base_regs(eng):
            if eng.engine not in held:
                held[eng.engine] = [eng.alloc_register(f"window{g}") for g in range(G)]
            return held[eng.engine]

        def window_starts(eng, i):
            regs = base_regs(eng)
            eng.load(regs, base_i[0:1, bass.ds(i * G, G)])
            return [eng.snap(r, min_val=0, max_val=N - 1) for r in regs]

        def turns_of(eng, which=0):
            return eng.value_load(turns_i[0:1, which:which + 1], min_val=TURNS, max_val=TURNS_SORTED)

        def when(eng, flag):
            if flag is None:
                return nullcontext()
            return eng.If(eng.value_load(flags_i[0:1, flag:flag + 1], min_val=0, max_val=1) > 0)

        def over_chunks(eng, step):
            for c in range(2):
                step(c, c, c == 0, False)
            with eng.Fori(1, NC // 2 - 1) as i:
                step(2 * i, 0, False, False)
                step(2 * i + 1, 1, False, False)
            for c in range(NC - 2, NC):
                step(c, c % 2, False, c == NC - 1)

        def wait_past(eng, s, count):
            if not isinstance(count, int) or count > 0:
                eng.wait_ge(s, count)

        def gathered_turns(eng, passes):
            past = turns_of(eng) * min(passes, 2)
            return past + turns_of(eng, 1) * (passes - 2) if passes > 2 else past

        s_io, s_c = sem("iotas"), sem("consts")
        wc = wbuf[:, :].rearrange("p (k n) -> p k n", k=K2)
        x_all = work[:, 0:8192].rearrange("p (b f) -> p b f", b=32)
        s_xz = sem("x_zeroed")
        s_ld, s_xl, s_at = [nc.alloc_semaphore(a) for a in ("vectors_loaded", "all_x_loaded", "weights_in")]
        whash = alpha[:, :, :].rearrange("p t h -> p (t h)")[:, 0:32 * KW].rearrange("p (b k) -> p b k", b=32)
        hash_i = stg[:, 4096:4096 + 32 * KW].bitcast(I32)
        prod = [work[:, 8192 + 2048 * i:8192 + 2048 * (i + 1)] for i in range(2)]

        def hrow(i):
            return hT[:, :, :].rearrange("p k n -> p (k n)")[:, i * T:(i + 1) * T].rearrange(
                "p (c j) -> p c j", c=CT)

        key, dstm, srcr, typr, fidx = [hrow(i) for i in range(5)]
        raw = [hrow(5 + i).bitcast(I32) for i in range(4)]
        rows4 = hT[0:H, :, :].rearrange("p k n -> p (k n)")
        s_pad, s_rl, s_cv = sem("pads_set"), sem("rows_loaded"), sem("rows_converted")
        whole, rest = divmod(E - 3 * P * P, P)

        attn = [hT[:, :, :].rearrange("p k n -> p (k n)")[:, 9 * T + 2048 * i:9 * T + 2048 * (i + 1)]
                for i in range(2)]

        with nc.Block() as block:
            @block.sync
            def _(sp):
                sp.wait_ge(s_pad, 4)
                for a, buf in zip((dst, dst, src, etype), raw):
                    sp.dma_start(buf[:, 0:3, :], a[0:3 * P * P].rearrange("(c p j) -> p c j", c=3, p=P)
                                 ).then_inc(s_rl, 16)
                    sp.dma_start(buf[0:whole, 3, :], a[3 * P * P:E - rest].rearrange("(p j) -> p j", j=P)
                                 ).then_inc(s_rl, 16)
                    sp.dma_start(buf[whole:whole + 1, 3, 0:rest],
                                 a[E - rest:E].rearrange("(o j) -> o j", o=1)).then_inc(s_rl, 16)
                for a, buf in zip((attn_l, attn_r), attn):
                    sp.dma_start(buf, a.rearrange("(o r) h d -> o (r h d)", o=1).to_broadcast([P, 2048])
                                 ).then_inc(s_at, 16)
                for k in range(K2):
                    for r in range(R):
                        sp.dma_start(wc[:, k, r * F:(r + 1) * F].rearrange("p (h d) -> p h d", h=H),
                                     conv_w[r, :, k * P:(k + 1) * P, :].rearrange("h p d -> p h d")
                                     ).then_inc(s_at, 16)
                sp.wait_ge(s_xz, 1)
                full = NBLK - 1
                sp.dma_start(x_all[:, 0:full, :],
                             x[0:full * P, :].rearrange("(b p) f -> p b f", p=P)).then_inc(s_xl, 16)
                sp.dma_start(x_all[0:N - full * P, full, :], x[full * P:N, :]).then_inc(s_xl, 16)
                for buf, v in ((hb_c, h_bias), (bin_c, b_in)):
                    sp.dma_start(buf[:, :], v.rearrange("(k p) -> p k", p=P),
                                 allow_slow_non_contiguous=True).then_inc(s_ld, 16)
                sp.dma_start(bh_c[:, :, :], b_hid.rearrange("l (k p) -> p l k", p=P),
                             allow_slow_non_contiguous=True).then_inc(s_ld, 16)
                sp.dma_start(bout_b[:, :], b_out.rearrange("(o n) -> o n", o=1).to_broadcast([P, F])
                             ).then_inc(s_ld, 16)

            @block.gpsimd
            def _(pool):
                pool.iota(io_i[:, 0:P], pattern=[[1, P]], base=0, channel_multiplier=0).then_inc(s_io, 1)
                pool.iota(io_i[:, P:P + 1], pattern=[[1, 1]], base=0, channel_multiplier=1).then_inc(s_io, 1)
                pool.iota(hash_i, pattern=[[P * 251, 32], [7919, KW]], base=0, channel_multiplier=251).then_inc(s_io, 1)

            @block.vector
            def _(dve):
                for v, buf in zip((N - 1, -1, 0, 0), raw):
                    dve.memset(buf[:, 3:CT, :], v).then_inc(s_pad, 1)
                dve.memset(x_all[:, NBLK - 1:32, :], 0.0).then_inc(s_xz, 1)
                dve.memset(ones[:, :], 1.0)
                dve.memset(ones_b[:, :], 1.0)
                dve.memset(eps_c[:, :], EPS)
                c = Chain(dve, s_c)
                dve.wait_ge(s_io, 2)
                c.link(dve.tensor_copy(iota_w[:, :], io_i[:, 0:P]))
                c.link(dve.tensor_copy(iota_p[:, :], io_i[:, P:P + 1]))
                c.link(dve.tensor_scalar(ident[:, :], iota_w[:, :], iota_p[:, :], None, ALU.is_equal))
                dve.wait_ge(s_io, 3)
                c.link(dve.tensor_scalar(hash_i, hash_i, 4095, None, ALU.bitwise_and))
                c.link(dve.tensor_copy(prod[0][:, 0:32 * KW], hash_i))
                c.link(dve.tensor_tensor(hash_i, prod[0][:, 0:32 * KW], prod[0][:, 0:32 * KW], ALU.mult))
                c.link(dve.tensor_scalar(hash_i, hash_i, 12, 15, ALU.arith_shift_right, ALU.bitwise_and))
                c.link(dve.tensor_copy(whash[:, :, :].rearrange("p b k -> p (b k)"), hash_i))
                dve.wait_ge(s_rl, 48 * 4)
                for buf, to in zip(raw, (key, dstm, srcr, typr)):
                    dve.tensor_copy(to, buf).then_inc(s_cv, 1)
                dve.wait_ge(s_cv, 4)

        base_r, last_r = stg[0:H, 0:T], stg[0:H, T:2 * T]
        first_c = stg[:, 2 * T:2 * T + CT * H].rearrange("p (c h) -> p c h", h=H)
        last_c = stg[:, 2 * T + 32:2 * T + 32 + CT * H].rearrange("p (c h) -> p c h", h=H)

        def tile_ends(flag=None):
            s_fc, s_tp, s_br = sem("ends_picked"), sem("ends_turned"), sem("ends_rowed")
            with nc.Block() as block:
                @block.vector
                def _(dve):
                    with when(dve, flag):
                        dve.tensor_copy(first_c, key[:, :, 0:1].to_broadcast([P, CT, H])).then_inc(s_fc, 1)
                        dve.tensor_copy(last_c, key[:, :, P - 1:P].to_broadcast([P, CT, H])).then_inc(s_fc, 1)
                        dve.wait_ge(s_tp, 1)
                        for i, to in enumerate((base_r, last_r)):
                            dve.tensor_copy(to[:, 0:512], PS[0:H, 2 * i, :]).then_inc(s_br, 1)
                            dve.tensor_copy(to[:, 512:T], PS[0:H, 2 * i + 1, 0:P]).then_inc(s_br, 1)
                        dve.wait_ge(s_br, 4)
                        dve.sem_inc(passed, 1)

                @block.tensor
                def _(pe):
                    with when(pe, flag):
                        pe.wait_ge(s_fc, 2)
                        for i, c4 in enumerate((first_c, last_c)):
                            for c in range(CT):
                                mm = pe.transpose(PS[0:H, 2 * i + c // 4, (c % 4) * P:(c % 4 + 1) * P],
                                                  c4[:, c, :], ident[:, :])
                        mm.then_inc(s_tp, 1)

        tile_ends()

        s_k, s_ks, s_kr = sem("check_steps"), sem("check_sum"), sem("check_rows")
        bad, viol = small[:, 0:4], stg[:, 2048:2048 + CT * (P - 1)].rearrange("p (c j) -> p c j", c=CT)
        with nc.Block() as block:
            @block.vector
            def _(dve):
                c = Chain(dve, s_k)
                c.link(dve.tensor_tensor(viol, key[:, :, 1:P], key[:, :, 0:P - 1], ALU.is_lt))
                c.link(dve.tensor_reduce(bad[:, 0:1], viol, AX.XY, ALU.add))
                spans = stg[0:1, 3700:3700 + NG]
                c.link(dve.tensor_tensor(spans, last_r[0:1, U - 1:T:U], base_r[0:1, 0:T:U], ALU.subtract))
                c.link(dve.tensor_scalar(spans, spans, float(P - 1), None, ALU.is_gt))
                c.link(dve.tensor_reduce(small[0:1, 23:24], spans, AX.X, ALU.add))
                c.link(dve.tensor_tensor(stg[0:1, 3000:3000 + T - 1], last_r[0:1, 0:T - 1], base_r[0:1, 1:T],
                                         ALU.is_gt))
                c.link(dve.tensor_reduce(small[0:1, 24:25], stg[0:1, 3000:3000 + T - 1], AX.X, ALU.add))
                c.link(dve.tensor_tensor(small[0:1, 24:25], small[0:1, 23:24], small[0:1, 24:25], ALU.add))
                dve.wait_ge(s_ks, 1)
                c.link(dve.tensor_tensor(small[0:1, 25:26], PS[0:1, 0, 0:1], small[0:1, 24:25], ALU.add))
                c.link(dve.tensor_scalar(small[0:1, 26:27], small[0:1, 25:26], 0.0,
                                         float(TURNS_SORTED - TURNS), ALU.is_gt, ALU.mult))
                c.link(dve.tensor_scalar(turns_i[0:1, 0:1], small[0:1, 26:27], float(TURNS), None, ALU.add))
                c.link(dve.tensor_scalar(flags_i[0:1, 0:1], small[0:1, 25:26], 0.0, None, ALU.is_gt))

            @block.tensor
            def _(pe):
                pe.wait_ge(s_k, 2)
                pe.matmul(PS[0:1, 0, 0:1], bad[:, 0:1], ones[:, 0:1], start=True, stop=True).then_inc(s_ks, 1)

        SW = -(-(E + ADDED * N) // P)
        EXTRA = P * SW - E
        head_rows, head_cols = divmod(EXTRA, SW)
        rec_tab = dram("rec_tab", [P * SW, 4])

        def sort_edges(flag, key_array, other_array):
            rec = work[:, 8192:8192 + 4 * SW].rearrange("p (j a) -> p j a", a=4)
            raw_s = [work[:, 8192 + (4 + i) * SW:8192 + (5 + i) * SW].bitcast(I32) for i in range(3)]
            pos, hit, rank, tmp, zero = [stg[:, i * SW:(i + 1) * SW] for i in range(5)]
            entry_i, pos_i = [stg[:, (5 + i) * SW:(6 + i) * SW].bitcast(I32) for i in range(2)]
            val, place0, off = small[:, 32:33], small[:, 33:34], small[:, 34:35]
            tri = stg[:, 7 * SW:7 * SW + P]
            idx4 = idx_ring[:, 0:4]
            rec4 = stg[:, 7 * SW + P:7 * SW + P + 16].rearrange("p (s a) -> p s a", a=4)
            back = work[:, 8192:8192 + CT * 4 * P].rearrange("p (c j a) -> p c j a", c=CT, a=4)
            back_whole, back_rest = divmod(SW, P)
            s_z, s_l, s_e, s_a, s_pk, s_pp, s_pi, s_cp, s_is, s_sd, s_rl, s_rd = [sem(a) for a in (
                "rows_zeroed", "edges_loaded", "entries_numbered", "sort_steps", "ranks_ready", "offsets_ready",
                "places_ready", "records_picked", "scatters_issued", "all_scattered", "sorted_loaded", "place_steps")]
            s_sc = [nc.alloc_semaphore(f"scattered{i}_{flag}") for i in range(4)]
            STEPS = 9

            with nc.Block() as block:
                @block.sync
                def _(sp):
                    with when(sp, flag):
                        sp.wait_ge(s_z, 3)
                        for a, buf in zip((key_array, other_array, etype), raw_s):
                            sp.dma_start(buf[head_rows:head_rows + 1, head_cols:SW],
                                         a[0:SW - head_cols].rearrange("(o j) -> o j", o=1)).then_inc(s_l, 16)
                            sp.dma_start(buf[head_rows + 1:P, :],
                                         a[SW - head_cols:E].rearrange("(p j) -> p j", j=SW)).then_inc(s_l, 16)
                        sp.wait_ge(s_cp, 2 * SW)
                        sp.wait_ge(s_sd, 1)
                        rows = rec_tab.rearrange("(t j) a -> t (j a)", j=P)
                        for cc in range(back_whole + 1):
                            k = P if cc < back_whole else back_rest
                            sp.dma_start(back[0:k, cc, :, :].rearrange("p j a -> p (j a)"), rows[cc * P:cc * P + k, :]
                                         ).then_inc(s_rl, 16)

                @block.gpsimd
                def _(pool):
                    with when(pool, flag):
                        pool.iota(entry_i, pattern=[[1, SW]], base=0, channel_multiplier=SW).then_inc(s_e, 1)
                        with pool.Fori(0, SW // 4) as i:
                            for s in range(4):
                                pool.wait_ge(s_cp, i * 8 + 2 * s + 2)
                                pool.sem_inc(s_is, 1)
                                pool.indirect_dma_start(
                                    out=rec_tab[:, :], out_offset=bass.IndirectOffsetOnAxis(ap=idx4[:, s:s + 1], axis=0),
                                    in_=rec4[:, s, :], in_offset=None).then_inc(s_sc[s], 16)
                        for s in range(4):
                            pool.wait_ge(s_sc[s], 16 * (SW // 4))
                        pool.sem_inc(s_sd, 1)

                @block.tensor
                def _(pe):
                    with when(pe, flag):
                        with pe.Fori(0, N) as v:
                            pe.wait_ge(s_pk, v * STEPS + 2)
                            pe.matmul(PS[:, 0, 0:1], tri, rank[:, SW - 1:SW], start=True, stop=True)
                            pe.matmul(PS[:, 0, 1:2], ones[:, :], rank[:, SW - 1:SW], start=True, stop=True
                                      ).then_inc(s_pp, 1)

                @block.vector
                def _(dve):
                    with when(dve, flag):
                        for buf in raw_s:
                            dve.memset(buf, 0).then_inc(s_z, 1)
                        c = Chain(dve, s_a)
                        for a in (pos, zero, val):
                            c.link(dve.memset(a, 0.0))
                        c.link(dve.memset(place0, -1.0))
                        c.link(dve.tensor_scalar(tri, iota_w[:, :], iota_p[:, :], None, ALU.is_gt))
                        dve.wait_ge(s_l, 96)
                        dve.wait_ge(s_e, 1)
                        c.link(dve.tensor_copy(tmp, entry_i))
                        c.link(dve.tensor_scalar(hit, tmp, float(EXTRA), None, ALU.is_ge))
                        c.link(dve.tensor_scalar(entry_i, entry_i, 2, None, ALU.arith_shift_right))
                        c.link(dve.tensor_copy(rank, entry_i))
                        c.link(dve.tensor_scalar(rank, rank, float(N - 1), None, ALU.min))
                        c.link(dve.tensor_copy(rec[:, :, 0], raw_s[0]))
                        c.link(dve.tensor_tensor(rec[:, :, 1], rec[:, :, 0], rank, ALU.subtract))
                        c.link(dve.tensor_tensor(rec[:, :, 1], rec[:, :, 1], hit, ALU.mult))
                        c.link(dve.tensor_tensor(rec[:, :, 0], rec[:, :, 1], rank, ALU.add))
                        c.link(dve.scalar_tensor_tensor(rec[:, :, 1], rec[:, :, 0], 1.0, hit, ALU.add, ALU.mult))
                        c.link(dve.tensor_scalar(rec[:, :, 1], rec[:, :, 1], 1.0, None, ALU.subtract))
                        c.link(dve.tensor_copy(rec[:, :, 2], raw_s[1]))
                        c.link(dve.tensor_copy(rec[:, :, 3], raw_s[2]))
                        dve.sem_inc(passed, 1)
                        with dve.Fori(0, N) as v:
                            c = Chain(dve, s_pk, v * STEPS)
                            c.link(dve.tensor_scalar(hit, rec[:, :, 0], val, None, ALU.is_equal))
                            c.link(dve.tensor_tensor_scan(rank, hit, zero, 0.0, ALU.add, ALU.add))
                            dve.wait_ge(s_pp, v + 1)
                            c.link(dve.tensor_tensor(off, PS[:, 0, 0:1], place0, ALU.add))
                            c.link(dve.scalar_tensor_tensor(tmp, rank, off, hit, ALU.add, ALU.mult))
                            c.link(dve.tensor_tensor(pos, pos, tmp, ALU.add))
                            c.link(dve.tensor_scalar(deg[:, bass.ds(v, 1)], PS[:, 0, 1:2], float(ADDED), None,
                                                     ALU.subtract))
                            c.link(dve.tensor_tensor(place0, place0, PS[:, 0, 1:2], ALU.add))
                            c.link(dve.tensor_scalar(val, val, 1.0, None, ALU.add))
                            c.link(dve.tensor_copy(small[:, 35:36], place0))
                            dve.sem_inc(passed, 1)
                        dve.tensor_scalar(deg[:, N - 1:N], deg[:, N - 1:N], float(EXTRA - ADDED * N), None,
                                          ALU.subtract).then_inc(s_pi, 1)
                        dve.tensor_copy(pos_i, pos).then_inc(s_pi, 1)
                        dve.wait_ge(s_pi, 2)

                        def pick(i, first=False):
                            for s in range(4):
                                if not first:
                                    dve.wait_ge(s_sc[s], i * 16)
                                dve.tensor_copy(idx4[:, s:s + 1], pos_i[:, bass.ds(i * 4 + s, 1)]).then_inc(s_cp, 1)
                                dve.tensor_copy(rec4[:, s, :], rec[:, bass.ds(i * 4 + s, 1), :].rearrange("p o a -> p (o a)")
                                                ).then_inc(s_cp, 1)

                        pick(0, first=True)
                        with dve.Fori(1, SW // 4) as i:
                            pick(i)
                        c = Chain(dve, s_rd)
                        for a, v in zip((key, dstm, srcr, typr), (N - 1, -1, 0, 0)):
                            c.link(dve.memset(a[:, back_whole:CT, :], float(v)))
                        dve.wait_ge(s_rl, 16 * (back_whole + 1))
                        for i, a in enumerate((key, dstm, srcr, typr)):
                            c.link(dve.tensor_copy(a[:, 0:back_whole, :], back[:, 0:back_whole, :, i]))
                            c.link(dve.tensor_copy(a[0:back_rest, back_whole, :], back[0:back_rest, back_whole, :, i]))


            tile_ends(flag)

        end_phase()
        sort_edges(0, dst, src)


        def tile_tables(flag=None):
            whole = flag is None
            s_f, s_tt, s_te, s_bb, s_dr = (sem("fidx_made"), sem("rows_turned"), sem("tiles_made"),
                                           sem("base_spread"), sem("dstm_stored"))
            turned = ((srcr, src_i), (dstm, dstloc)) + (((fidx, fidx_i), (typr, typ_t)) if whole else ())
            with nc.Block() as block:
                @block.vector
                def _(dve):
                    with when(dve, flag):
                        c = Chain(dve, s_f)
                        c.link(dve.scalar_tensor_tensor(fidx, srcr, float(R), typr, ALU.mult, ALU.add))
                        e = Chain(dve, s_te)
                        for i, (_, to) in enumerate(turned):
                            dve.wait_ge(s_tt, i + 1)
                            b = 2 * (i % 2)
                            e.link(dve.tensor_copy(to[:, 0:512], PS[:, b, :]))
                            e.link(dve.tensor_copy(to[:, 512:T], PS[:, b + 1, 0:P]))
                        if whole:
                            e.link(dve.tensor_scalar(pad_t[:, :], dstloc[:, :], 0.0, -BIG, ALU.is_lt, ALU.mult))
                        dve.wait_ge(s_bb, 1)
                        pb = PS[:, 4, 0:NG]
                        places = dstloc[:, :].rearrange("p (g u) -> p g u", u=U)
                        e.link(dve.tensor_tensor(places, places, pb.unsqueeze(2).to_broadcast([P, NG, U]),
                                                 ALU.subtract))
                        e.link(dve.tensor_scalar(nodeid[:, :], pb, iota_p[:, :], None, ALU.add))
                        e.link(dve.tensor_copy(base_i[:, :], base_r[0:1, 0:T:U]))
                        dve.sem_inc(passed, 1)

                @block.tensor
                def _(pe):
                    with when(pe, flag):
                        for i, (fr, _) in enumerate(turned):
                            if i == 0:
                                pe.wait_ge(s_f, 1)
                            if i >= 2:
                                pe.wait_ge(s_te, 2 * (i - 1))
                            for c in range(CT):
                                mm = pe.transpose(PS[:, 2 * (i % 2) + c // 4, (c % 4) * P:(c % 4 + 1) * P],
                                                  fr[:, c, :], ident[:, :])
                            mm.then_inc(s_tt, 1)
                        pe.matmul(PS[:, 4, 0:NG], ones[0:1, :], base_r[0:1, 0:T:U],
                                  start=True, stop=True).then_inc(s_bb, 1)

                @block.sync
                def _(sp):
                    if whole:
                        sp.dma_start(dstm_row.rearrange("c p j -> p c j"), dstm).then_inc(s_dr, 16)
                        sp.wait_ge(s_dr, 16)

        tile_tables()

        same = sb("same", [P, T + 1])
        firstm = sb("firstm", [P, T])
        lastm = sb("lastm", [P, T])
        s_sm = sem("segments_marked")
        with nc.Block() as block:
            @block.vector
            def _(dve):
                c = Chain(dve, s_sm)
                c.link(dve.memset(same[:, :], 0.0))
                sv = same[:, 0:T].rearrange("p (c j) -> p c j", c=CT)
                c.link(dve.tensor_tensor(sv[:, :, 1:P], key[:, :, 1:P], key[:, :, 0:P - 1], ALU.is_equal))
                c.link(dve.tensor_tensor(firstm[:, :].rearrange("p (c j) -> p c j", c=CT), key,
                                         key[:, :, 0:1].to_broadcast([P, CT, P]), ALU.is_equal))
                c.link(dve.tensor_tensor(lastm[:, :].rearrange("p (c j) -> p c j", c=CT), key,
                                         key[:, :, P - 1:P].to_broadcast([P, CT, P]), ALU.is_equal))

        cont = sb("cont", [H, T + 1])
        single = sb("single", [H, T])
        with nc.Block() as block:
            s_ct = sem("conts_made")

            @block.vector
            def _(dve):
                c = Chain(dve, s_ct)
                c.link(dve.memset(cont[:, :], 0.0))
                c.link(dve.tensor_tensor(cont[:, 1:T], base_r[:, 1:T], last_r[:, 0:T - 1], ALU.is_equal))
                c.link(dve.tensor_tensor(single[:, :], base_r[:, :], last_r[:, :], ALU.is_equal))

        hN = stg[:, 0:2048].rearrange("p (s b f) -> p s b f", s=2, b=4)
        hTs = stg[:, 2048:4096].rearrange("p (s k n) -> p s k n", s=2, k=K2)
        elr = work[:, 8192:8192 + 32 * 3 * RH].rearrange("p (b i n) -> p b i n", b=32, i=3)

        def ln_stats(dve, rows, c, slot, stats_done, var_ready):
            for b in range(4):
                dve.bn_stats(stats[:, slot, b, :], rows(b)).then_inc(stats_done, 1)
            dve.wait_ge(stats_done, c * 4 + 4)
            dve.sem_inc(passed, 1)
            for b in range(4):
                dve.bn_aggr(mv[:, slot, b, :], stats[:, slot, b, :]).then_inc(var_ready, 1)

        def ln_finish(dve, rows, c, slot, std_done, rstd_done, hn_ready):
            dve.wait_ge(std_done, c + 1)
            dve.reciprocal(rstd[:, slot, :], std[:, slot, :]).then_inc(rstd_done, 1)
            dve.wait_ge(rstd_done, c + 1)
            for b in range(4):
                dve.tensor_scalar(hN[:, slot, b, :], rows(b), mv[:, slot, b, 0:1], rstd[:, slot, b:b + 1],
                                  ALU.subtract, ALU.mult).then_inc(hn_ready, 1)

        s_wi, s_bs, s_vr, s_sd, s_rs, s_hn, s_tp, s_ht, s_el, s_ee, s_et = [sem(x) for x in (
            "w_in_place", "stats_done", "var_ready", "std_done", "rstd_done", "hn_ready", "hn_turned", "ht_ready",
            "el_ready", "el_kept", "el_stored")]
        s_pr = sem("products")
        with nc.Block() as block:
            @block.vector
            def _(dve):
                def x_rows(c):
                    return lambda b: x_all[:, bass.ds(c * 4 + b, 1), :].rearrange("p o f -> p (o f)")

                def keep(c, slot):
                    dve.wait_ge(s_el, c + 1)
                    dve.tensor_scalar(elr[:, bass.ds(c * 4, 4), 0:3:2, :],
                                      PS[:, 4 + slot, 0:256].rearrange("p (b i n) -> p b i n", b=4, i=2),
                                      0.0, None, ALU.add).then_inc(s_ee, 1)

                def step(c, slot, first, last):
                    if not last:
                        ln_stats(dve, x_rows(c + 1), c + 1, 1 - slot, s_bs, s_vr)
                    if not first:
                        wait_past(dve, s_tp, c - 1)
                    ln_finish(dve, x_rows(c), c, slot, s_sd, s_rs, s_hn)
                    if not isinstance(c, int) or c > 1:
                        keep(c - 2, slot)

                c = Chain(dve, s_pr)
                dve.wait_ge(s_at, 16 * (K2 * R + 2))
                for i in range(2):
                    for k in range(K2):
                        c.link(dve.tensor_tensor(prod[k], wc[:, k, :], attn[i], ALU.mult))
                        c.link(dve.tensor_reduce(wlr[:, k, i * RH:(i + 1) * RH],
                                                 prod[k].rearrange("p (c d) -> p c d", d=D), AX.X, ALU.add))
                dve.tensor_copy(elr[:, :, 1, :], whash).then_inc(s_wi, 1)
                dve.wait_ge(s_xl, 32)
                ln_stats(dve, x_rows(0), 0, 0, s_bs, s_vr)
                over_chunks(dve, step)
                keep(NC - 2, 0)
                keep(NC - 1, 1)

            @block.gpsimd
            def _(pool):
                pool.wait_ge(s_pr, 8)
                pool.memset(hT[:, :, NP:FBLK * P], 0.0).then_inc(s_wi, 1)

            @block.scalar
            def _(act):
                def roots(c, slot):
                    act.wait_ge(s_vr, 4 * c + 4)
                    act.activation(std[:, slot, :], mv[:, slot, :, 1], ACT.Sqrt, bias=eps_c[:, :]).then_inc(s_sd, 1)

                def step(c, slot, first, last):
                    if not last:
                        roots(c + 1, 1 - slot)
                    act.wait_ge(s_tp, c + 1)
                    if not first:
                        wait_past(act, s_el, c - 1)
                    act.sem_inc(passed, 1)
                    banks = PS[:, 2 * slot:2 * slot + 2, :]
                    act.activation(hTs[:, slot, :, :], banks, ACT.Relu).then_inc(s_ht, 1)
                    act.activation(hT[:, :, bass.ds(c * CW, CW)], banks, ACT.Relu).then_inc(s_ht, 1)

                roots(0, 0)
                over_chunks(act, step)

            @block.tensor
            def _(pe):
                def halves(c, slot):
                    pe.wait_ge(s_ht, 2 * c + 1)
                    wait_past(pe, s_ee, c - 1)
                    for b in range(4):
                        for k in range(K2):
                            mm = pe.matmul(PS[:, 4 + slot, b * 2 * RH:(b + 1) * 2 * RH],
                                           hTs[:, slot, k, b * P:(b + 1) * P],
                                           wlr[:, k, :], start=(k == 0), stop=(k == K2 - 1))
                    mm.then_inc(s_el, 1)

                def step(c, slot, first, last):
                    pe.wait_ge(s_hn, c * 4 + 4)
                    if not first:
                        wait_past(pe, s_ht, 2 * (c - 1))
                    for b in range(4):
                        for k in range(K2):
                            mm = pe.transpose(PS[:, 2 * slot + k, b * P:(b + 1) * P],
                                              hN[:, slot, b, k * P:(k + 1) * P], ident[:, :])
                    mm.then_inc(s_tp, 1)
                    if not first:
                        halves(c - 1, 1 - slot)

                over_chunks(pe, step)
                halves(NC - 1, (NC - 1) % 2)

            @block.sync
            def _(sp):
                sp.wait_ge(s_wi, 2)
                sp.wait_ge(s_ld, 16 * 4)

                def store(c, slot, first, last):
                    blocks = min(4, NBLK + 1 - 4 * c) if isinstance(c, int) else 4
                    sp.wait_ge(s_ee, c + 1)
                    for tab, o in ((el_tab, 0), (er_tab, 1)):
                        sp.dma_start(tab[bass.ds(c * CW, blocks * P), :].rearrange("(b p) n -> p b n", p=P),
                                     elr[:, bass.ds(c * 4, blocks), o:o + 2, :].rearrange("p b i n -> p b (i n)")
                                     ).then_inc(s_et, 16)

                over_chunks(sp, store)
                sp.wait_ge(s_et, 32 * NC)

        end_phase()

        dst_b = stg[:, 0:G * U * P].rearrange("p (g n) -> p g n", g=G)
        onehotT = stg[:, G * U * P:2 * G * U * P].rearrange("p (g n) -> p g n", g=G)
        wd = stg[:, 6144:6400].rearrange("p (s u n) -> p s u n", s=2, u=U)
        fout = work[:, 8192:8192 + 1024].rearrange("p (s n) -> p s n", s=2)
        fblk = work[:, 9216:9216 + 512].rearrange("p (s k n) -> p s k n", s=2, k=K2)
        el_ring = work[:, 9728:9728 + TB * 2 * RH].rearrange("p (s n) -> p s n", s=TB)
        er_ring = work[:, 11264:11264 + G * 2 * RH].rearrange("p (g n) -> p g n", g=G)
        oh_b = sb("oh_b", [P, G, U, P], BF16)
        tsum = sb("tsum", [P, U, R, H])
        tmask = sb("tmask", [P, U, R])
        s_gf, s_ix, s_is, s_oh, s_er, s_wd, s_m, s_post = [sem(x) for x in (
            "group_free", "idx_ready", "gathers_issued", "onehots_ready", "er_ready", "wd_ready", "m_ready",
            "post_steps")]
        s_db = [sem(f"dst_rows{g}") for g in range(G)]
        s_ew = [sem(f"er_window{g}") for g in range(G)]
        s_fb, s_fm, s_fe, s_fs = sem("fblk_ready"), sem("feat_ready"), sem("feat_kept"), [
            sem("feat_stored0"), sem("feat_stored1")]
        s_z = sem("sums_zeroed")
        AHEAD = 3
        DEG, ERW, MCOL = 0, P, P + U * 2 * RH

        with nc.Block() as block:
            @block.gpsimd
            def _(pool):
                n = turns_of(pool)
                with pool.Fori(0, n) as i:
                    for g in range(G):
                        pool.wait_ge(s_ix, i * G + g + 1)
                        pool.sem_inc(s_is, 1)
                        for u in range(U):
                            s = g * U + u
                            pool.indirect_dma_start(
                                out=el_ring[:, s, :], out_offset=None, in_=el_tab[:, :],
                                in_offset=bass.IndirectOffsetOnAxis(ap=idx_ring[:, s:s + 1], axis=0)
                            ).then_inc(s_ga[g], 16)

            @block.sync
            def _(sp):
                n = turns_of(sp)
                with sp.Fori(0, n) as i:
                    base = window_starts(sp, i)
                    for g in range(G):
                        sp.wait_ge(s_gf, i * G + g + 1)
                        sp.dma_start(dst_b[:, g, :],
                                     dstm_row.rearrange("(o c) p j -> o (c p j)", o=1)[
                                         :, bass.ds((i * TB + g * U) * P, U * P)].to_broadcast([P, U * P])
                                     ).then_inc(s_db[g], 16)
                        sp.dma_start(er_ring[:, g, :], er_tab[bass.ds(base[g], P), :]).then_inc(s_ew[g], 16)

            @block.scalar
            def _(act):
                n = turns_of(act)
                for slot in range(2):
                    act.sem_inc(s_fs[slot], 16)

                def index(i, g):
                    act.wait_ge(s_gf, i * G + g + 1)
                    act.sem_inc(passed, 1)
                    act.copy(idx_ring[:, g * U:(g + 1) * U], src_i[:, bass.ds(i * TB + g * U, U)]
                             ).then_inc(s_ix, 1)

                def fetch(q, slot):
                    blk = (q >> 2).with_bounds(min_val=0, max_val=FBLK - 1) if not isinstance(q, int) else q >> 2
                    act.activation(fblk[:, slot, :, :], hT[:, :, bass.ds(blk * P, P)], ACT.Copy).then_inc(s_fb, 1)

                for g in range(AHEAD):
                    index(0, g)
                fetch(0, 0)
                with act.Fori(0, n) as i:
                    for g in range(G):
                        q, slot = i * G + g, g % 2
                        act.wait_ge(s_er, q + 1)
                        act.activation(wd[:, slot, :, :], PS[:, g % NBANK, ERW:MCOL].rearrange(
                            "p (u n) -> p u n", u=U)[:, :, 0:KW], ACT.Copy).then_inc(s_wd, 1)
                        index(i + (g + AHEAD) // G, (g + AHEAD) % G)
                        act.wait_ge(s_fm, q + 2)
                        act.sem_inc(passed, 1)
                        fetch(q + 1, 1 - slot)
                        act.wait_ge(s_fm, q + 3)
                        act.wait_ge(s_fs[slot], 16 * (i * (G // 2) + g // 2) + 16)
                        act.activation(fout[:, slot, :], PS[:, 6 + slot, :], ACT.Copy).then_inc(s_fe, 1)
                        act.wait_ge(s_fe, q + 1)
                        blk = (q >> 2).with_bounds(min_val=0, max_val=FBLK - 1)
                        act.dma_start(feat_tab.rearrange("(n r) f -> n (r f)", r=R)[
                            bass.ds(blk * P, P), bass.ds((q & 3) * 512, 512)],
                            fout[:, slot, :]).then_inc(s_fs[slot], 16)
                for slot in range(2):
                    act.wait_ge(s_fs[slot], n * (16 * G // 2) + 16)
                act.sem_inc(passed, 1)

            @block.tensor
            def _(pe):
                n = turns_of(pe)
                pe.sem_inc(s_fm, 2)
                with pe.Fori(0, n) as i:
                    for g in range(G):
                        q, slot, bank = i * G + g, g % 2, g % NBANK
                        pe.wait_ge(s_oh, 2 * q + 2)
                        pe.wait_ge(s_ew[g], i * 16 + 16)
                        pe.wait_ge(s_gf, q + G - NBANK + 1)
                        for u in range(U):
                            pe.matmul(PS[:, bank, DEG:ERW], ones_b[:, :], oh_b[:, g, u, :],
                                      start=(u == 0), stop=(u == U - 1))
                        for u in range(U):
                            mm = pe.matmul(PS[:, bank, ERW + u * 2 * RH:ERW + (u + 1) * 2 * RH],
                                           onehotT[:, g, u * P:(u + 1) * P], er_ring[:, g, :], start=True, stop=True)
                        mm.then_inc(s_er, 1)
                        pe.wait_ge(s_fb, q + 1)
                        for k in range(K2):
                            mm = pe.matmul(PS[:, 6 + slot, :], fblk[:, slot, k, :],
                                           wc[:, k, bass.ds((q & 3) * 512, 512)],
                                           start=(k == 0), stop=(k == K2 - 1))
                        mm.then_inc(s_fm, 1)
                        pe.wait_ge(s_wd, q + 1)
                        pe.wait_ge(s_ga[g], i * 16 * U + 16 * U)
                        for u in range(U):
                            mm = pe.matmul(PS[0:KW, bank, MCOL:MCOL + KW], wd[:, slot, u, :],
                                           el_ring[:, g * U + u, RH:RH + KW], start=(u == 0), stop=(u == U - 1))
                        mm.then_inc(s_m, 1)

            POST = 5

            @block.vector
            def _(dve):
                n = turns_of(dve)
                dve.memset(msum[:, :], 0.0).then_inc(s_z, 1)
                dve.memset(alpha[:, TURNS * TB:T, :], 0.0).then_inc(s_z, 1)
                dve.memset(deg[:, :], 0.0).then_inc(s_gf, G)
                dve.wait_ge(s_z, 2)
                dve.wait_ge(s_gf, G)
                dve.sem_inc(passed, 1)
                with dve.Fori(0, n) as i:
                    base = window_starts(dve, i)

                    def make(g):
                        dve.wait_ge(s_db[g], i * 16 + 16)
                        dve.tensor_scalar(onehotT[:, g, :], dst_b[:, g, :], nodeid[:, bass.ds(i * G + g, 1)],
                                          None, ALU.is_equal).then_inc(s_oh, 1)
                        dve.tensor_tensor(
                            oh_b[:, g, :, :], iota_w[:, :].unsqueeze(1).to_broadcast([P, U, P]),
                            dstloc[:, bass.ds(i * TB + g * U, U)].unsqueeze(2).to_broadcast([P, U, P]),
                            ALU.is_equal).then_inc(s_oh, 1)

                    def post(g):
                        q, bank = i * G + g, g % NBANK
                        tiles = bass.ds(i * TB + g * U, U)
                        dve.tensor_tensor(
                            tmask[:, :, :], typ_t[:, tiles].unsqueeze(2).to_broadcast([P, U, R]),
                            iota_w[:, 0:R].unsqueeze(1).to_broadcast([P, U, R]), ALU.is_equal).then_inc(s_post, 1)
                        dve.wait_ge(s_m, q + 1)
                        dve.tensor_tensor(deg[:, bass.ds(base[g], P)], deg[:, bass.ds(base[g], P)],
                                          PS[:, bank, DEG:ERW], ALU.add).then_inc(s_post, 1)
                        dve.tensor_tensor(msum[:, 0:KW], msum[:, 0:KW], PS[0:KW, bank, MCOL:MCOL + KW], ALU.add
                                          ).then_inc(s_post, 1)
                        dve.wait_ge(s_gf, q + G)
                        dve.tensor_tensor(
                            tsum[:, :, :, :].rearrange("p u r h -> p u (r h)"),
                            PS[:, bank, ERW:MCOL].rearrange("p (u n) -> p u n", u=U)[:, :, KW:KW + RH],
                            el_ring[:, g * U:(g + 1) * U, 0:RH], ALU.add).then_inc(s_post, 1)
                        dve.wait_ge(s_post, q * POST + 4)
                        dve.tensor_tensor(tsum[:, :, :, :].rearrange("p u r h -> p (u r) h"),
                                          tsum[:, :, :, :].rearrange("p u r h -> p (u r) h"),
                                          tmask[:, :, :].rearrange("p u r -> p (u r)").unsqueeze(2)
                                          .to_broadcast([P, U * R, H]), ALU.mult).then_inc(s_post, 1)
                        dve.wait_ge(s_post, q * POST + 5)
                        dve.tensor_reduce(alpha[:, tiles, :], tsum[:, :, :, :].rearrange("p u r h -> p u h r"),
                                          AX.X, ALU.add).then_inc(s_gf, 1)

                    make(0)
                    for g in range(1, G):
                        make(g)
                        post(g - 1)
                    post(G - 1)
                dve.wait_ge(s_gf, n * G + G)
                dve.sem_inc(passed, 1)

        s_ms, s_mt, s_mb = sem("symmetry_steps"), sem("m_turned"), sem("m_summed")
        with nc.Block() as block:
            @block.tensor
            def _(pe):
                pe.transpose(PS[0:KW, 0, 0:KW], msum[:, 0:KW], ident[0:KW, 0:KW]).then_inc(s_mt, 1)
                pe.wait_ge(s_ms, 2)
                pe.matmul(PS[0:1, 1, 0:1], msum[:, 2 * KW:2 * KW + 1], ones[0:KW, 0:1], start=True, stop=True
                          ).then_inc(s_mb, 1)

            @block.vector
            def _(dve):
                c = Chain(dve, s_ms)
                dve.wait_ge(s_mt, 1)
                c.link(dve.tensor_tensor(msum[:, KW:2 * KW], PS[0:KW, 0, 0:KW], msum[:, 0:KW], ALU.not_equal))
                c.link(dve.tensor_reduce(msum[:, 2 * KW:2 * KW + 1], msum[:, KW:2 * KW], AX.X, ALU.add))
                dve.wait_ge(s_mb, 1)
                c.link(dve.tensor_scalar(small[0:1, 40:41], PS[0:1, 1, 0:1], 0.0, None, ALU.is_gt))
                c.link(dve.tensor_copy(flags_i[0:1, 1:2], small[0:1, 40:41]))
                c.link(dve.tensor_copy(small[0:1, 41:42], turns_i[0:1, 0:1]))
                c.link(dve.scalar_tensor_tensor(small[0:1, 42:43], small[0:1, 40:41], float(TURNS_SORTED),
                                                small[0:1, 41:42], ALU.mult, ALU.max))
                c.link(dve.tensor_copy(turns_i[0:1, 1:2], small[0:1, 42:43]))

        end_phase()

        V, FW, BW = [w.rearrange("p (h c j) -> p h c j", h=H, c=CT) for w in (
            work[:, 0:4 * T], work[:, 4 * T:8 * T], work[:, 8 * T:12 * T])]
        TM = work[:, 12 * T:16 * T].rearrange("p (h c j) -> p h c j", h=H, c=CT)
        hflat = rows4
        AR, FR, PR, SR, CR, DR, CM, CS, CB = [hflat[:, i * T:(i + 1) * T] for i in range(9)]
        CONTM = hflat[:, 9 * T:10 * T + 1]
        flat = lambda a: a.rearrange("p h c j -> p (h c j)")
        lane = lambda a, h: a[:, h, :, :].rearrange("p c j -> p (c j)")
        neg = stg[:, 0:T + 1]
        fneg, lneg = stg[:, 700:700 + T], stg[:, 1400:1400 + T]

        s_q, s_qt, s_qe = sem("scores_ready"), sem("scores_turned"), sem("scores_kept")
        with nc.Block() as block:
            @block.vector
            def _(dve):
                c = Chain(dve, s_q)
                a2 = alpha[:, :, :].rearrange("p t h -> p (t h)")
                c.link(dve.tensor_tensor(alpha[:, :, :], alpha[:, :, :],
                                         pad_t[:, :].unsqueeze(2).to_broadcast([P, T, H]), ALU.add))
                c.link(dve.scalar_tensor_tensor(a2, a2, SLOPE, a2, ALU.mult, ALU.max))
                for i in range(CT):
                    dve.wait_ge(s_qt, i + 1)
                    dve.tensor_copy(V[:, :, i, :], PS[:, i, :].rearrange("p (h j) -> p h j", h=H)).then_inc(s_qe, 1)
                c.link(dve.tensor_scalar(neg[:, :], same[:, :], 1.0, BIG, ALU.subtract, ALU.mult))
                c.link(dve.tensor_scalar(fneg, firstm[:, :], 1.0, BIG, ALU.subtract, ALU.mult))
                c.link(dve.tensor_scalar(lneg, lastm[:, :], 1.0, BIG, ALU.subtract, ALU.mult))
                dve.wait_ge(s_qe, CT)

            @block.tensor
            def _(pe):
                pe.wait_ge(s_q, 2)
                for i in range(CT):
                    for h in range(H):
                        mm = pe.transpose(PS[:, i, h * P:(h + 1) * P], alpha[:, i * P:(i + 1) * P, h], ident[:, :])
                    mm.then_inc(s_qt, 1)

        def segment(op_in, op, zero, mask, fmask, lmask):
            s_s, s_p, s_b = sem("segment_steps"), sem("ends_turned"), sem("carries_turned")
            with nc.Block() as block:
                @block.vector
                def _(dve):
                    c = Chain(dve, s_s)
                    for h in range(H):
                        dve.tensor_tensor_scan(lane(FW, h), mask[:, 0:T], lane(V, h), zero, op_in, op).then_inc(s_s, 1)
                        dve.tensor_tensor_scan(lane(BW, h)[:, ::-1], mask[:, 1:T + 1][:, ::-1],
                                               lane(V, h)[:, ::-1], zero, op_in, op).then_inc(s_s, 1)
                    c.n = 2 * H
                    dve.wait_ge(s_s, 2 * H)
                    c.link(dve.tensor_tensor(CS, cont[:, 0:T], single[:, :], ALU.mult))
                    c.link(dve.tensor_tensor(CB, cont[:, 1:T + 1], single[:, :], ALU.mult))
                    c.link(dve.tensor_copy(CONTM, cont[:, :]))
                    if zero:
                        for m in (CS, CB, CONTM):
                            c.link(dve.tensor_scalar(m, m, 1.0, BIG, ALU.subtract, ALU.mult))
                    dve.wait_ge(s_p, 1)
                    for i, to in enumerate((AR, FR)):
                        c.link(dve.tensor_copy(to[:, 0:512], PS[0:H, 2 * i, :]))
                        c.link(dve.tensor_copy(to[:, 512:T], PS[0:H, 2 * i + 1, 0:P]))
                    c.link(dve.tensor_tensor_scan(PR, CS, AR, zero, op_in, op))
                    c.link(dve.tensor_tensor_scan(SR[:, ::-1], CB[:, ::-1], FR[:, ::-1], zero, op_in, op))
                    c.link(dve.memset(CR, zero))
                    c.link(dve.memset(DR, zero))
                    c.link(dve.tensor_tensor(CR[:, 1:T], PR[:, 0:T - 1], CONTM[:, 1:T], op_in))
                    c.link(dve.tensor_tensor(DR[:, 0:T - 1], SR[:, 1:T], CONTM[:, 1:T], op_in))
                    dve.sem_inc(s_b, 1)
                    dve.wait_ge(s_b, 3)
                    c.link(dve.tensor_copy(cT[:, :, :, :].rearrange("p i c h -> p (i c h)"), PS[:, 4, 0:2 * CT * H]))
                    c.link(dve.tensor_tensor(flat(FW), flat(FW), flat(BW), op))
                    if not zero:
                        c.link(dve.tensor_tensor(flat(FW), flat(FW), flat(V), ALU.subtract))
                    for i, m in enumerate((fmask, lmask)):
                        for h in range(H):
                            c.link(dve.tensor_tensor(TM[:, h, :, :], m.rearrange("p (c j) -> p c j", c=CT),
                                                     cT[:, i, :, h:h + 1].to_broadcast([P, CT, P]), op_in))
                        c.link(dve.tensor_tensor(flat(FW), flat(FW), flat(TM), op))

                @block.tensor
                def _(pe):
                    pe.wait_ge(s_s, 2 * H)
                    for i, (a, j) in enumerate(((FW, P - 1), (BW, 0))):
                        for cc in range(CT):
                            mm = pe.transpose(PS[0:H, 2 * i + cc // 4, (cc % 4) * P:(cc % 4 + 1) * P],
                                              a[:, :, cc, j], ident[:, :])
                    mm.then_inc(s_p, 1)
                    pe.wait_ge(s_b, 1)
                    for i, a in enumerate((CR, DR)):
                        for cc in range(CT):
                            mm = pe.transpose(PS[:, 4, (i * CT + cc) * H:(i * CT + cc + 1) * H],
                                              a[:, cc * P:(cc + 1) * P], ident[0:H, 0:H])
                    mm.then_inc(s_b, 2)

        segment(ALU.add, ALU.max, -BIG, neg, fneg, lneg)
        s_x, s_xe = sem("shifted"), sem("exps_ready")
        with nc.Block() as block:
            @block.vector
            def _(dve):
                dve.tensor_tensor(flat(V), flat(V), flat(FW), ALU.subtract).then_inc(s_x, 1)

            @block.scalar
            def _(act):
                act.wait_ge(s_x, 1)
                act.activation(flat(V), flat(V), ACT.Exp).then_inc(s_xe, 1)
                act.wait_ge(s_xe, 1)
        segment(ALU.mult, ALU.add, 0.0, same, firstm[:, :], lastm[:, :])
        s_al, s_at, s_ae = sem("alphas_ready"), sem("alphas_turned"), sem("alphas_kept")
        with nc.Block() as block:
            @block.vector
            def _(dve):
                c = Chain(dve, s_al)
                c.link(dve.reciprocal(flat(FW), flat(FW)))
                c.link(dve.tensor_tensor(flat(V), flat(V), flat(FW), ALU.mult))
                for i in range(CT):
                    dve.wait_ge(s_at, i + 1)
                    dve.tensor_copy(alpha[:, i * P:(i + 1) * P, :].rearrange("p t h -> p h t"),
                                    PS[:, i, :].rearrange("p (h t) -> p h t", h=H)).then_inc(s_ae, 1)
                dve.wait_ge(s_ae, CT)

            @block.tensor
            def _(pe):
                pe.wait_ge(s_al, 2)
                for i in range(CT):
                    for h in range(H):
                        mm = pe.transpose(PS[:, i, h * P:(h + 1) * P], V[:, h, i, :], ident[:, :])
                    mm.then_inc(s_at, 1)

        wout = wbuf[:, 512:1024].rearrange("p (k n) -> p k n", k=K2)
        win = wbuf[:, 0:512].rearrange("p (k n) -> p k n", k=K2)
        wag = wbuf[:, 1024:2560].rearrange("p (l k n) -> p l k n", l=LAYERS, k=K2)
        wse = wbuf[:, 2560:4096].rearrange("p (l k n) -> p l k n", l=LAYERS, k=K2)
        onehot = stg[:, 0:TB * P].rearrange("p (s n) -> p s n", s=TB)

        def edge_pass(table, idx, layer=None):
            scaled = layer is None
            before = lambda eng: gathered_turns(eng, 1 if scaled else 2 + layer)
            s_gf, s_ix, s_is, s_oh, s_mm, s_add, s_sf, s_sk, s_dg = [sem(x) for x in (
                "group_free", "idx_ready", "gathers_issued", "rows_ready", "group_summed", "group_added",
                "self_summed", "self_kept", "deg_inverted")]
            with nc.Block() as block:
                @block.gpsimd
                def _(pool):
                    n = turns_of(pool, 0 if scaled else 1)
                    with pool.Fori(0, n) as i:
                        for g in range(G):
                            pool.wait_ge(s_ix, i * G + g + 1)
                            pool.sem_inc(s_is, 1)
                            for u in range(U):
                                s = g * U + u
                                pool.indirect_dma_start(
                                    out=ring[:, s, :], out_offset=None, in_=table[:, :],
                                    in_offset=bass.IndirectOffsetOnAxis(ap=idx_ring[:, s:s + 1], axis=0)
                                ).then_inc(s_ga[g], 16)

                @block.scalar
                def _(act):
                    n = turns_of(act, 0 if scaled else 1)

                    def turn(i, with_self):
                        for g in range(G):
                            act.wait_ge(s_mm, i * G + g + 1)
                            act.sem_inc(passed, 1)
                            act.copy(idx_ring[:, g * U:(g + 1) * U], idx[:, bass.ds(i * TB + g * U, U)]
                                     ).then_inc(s_ix, 1)
                        if with_self:
                            act.wait_ge(s_sf, i + 1)
                            act.sem_inc(passed, 1)
                            for f in range(K2):
                                act.activation(hT[:, f, bass.ds(i * CW, CW)], PS[:, 4 + f, :], ACT.Identity,
                                               bias=bh_c[:, layer, f:f + 1]).then_inc(s_sk, 1)

                    if not scaled:
                        with act.Fori(0, NC) as i:
                            turn(i, True)
                    with act.Fori(0 if scaled else NC, n) as i:
                        turn(i, False)

                @block.tensor
                def _(pe):
                    n, past = turns_of(pe, 0 if scaled else 1), before(pe)
                    pe.sem_inc(s_mm, G)
                    pe.sem_inc(s_sk, K2)

                    def turn(i, with_self):
                        for g in range(G):
                            q, bank = i * G + g, g % NBANK
                            pe.wait_ge(s_oh, q + 1)
                            if not scaled:
                                pe.wait_ge(s_ga[g], (i + past) * (16 * U) + 16 * U)
                            pe.wait_ge(s_add, q + 1)
                            for k in range(K2):
                                for u in range(U):
                                    s = g * U + u
                                    mm = pe.matmul(PS[:, bank, k * P:(k + 1) * P],
                                                   ring[:, s, k * P:(k + 1) * P], onehot[:, s, :],
                                                   start=(u == 0), stop=(u == U - 1))
                            mm.then_inc(s_mm, 1)
                            if with_self and g < K2 * K2:
                                f, k = divmod(g, K2)
                                pe.wait_ge(s_sk, 2 * i + 2)
                                mm = pe.matmul(PS[:, 4 + f, :], wse[:, layer, k, f * P:(f + 1) * P],
                                               hT[:, k, bass.ds(i * CW, CW)], start=(k == 0), stop=(k == K2 - 1))
                                if g == K2 * K2 - 1:
                                    mm.then_inc(s_sf, 1)

                    if not scaled:
                        with pe.Fori(0, NC) as i:
                            turn(i, True)
                    with pe.Fori(0 if scaled else NC, n) as i:
                        turn(i, False)

                @block.vector
                def _(dve):
                    n, past = turns_of(dve, 0 if scaled else 1), before(dve)
                    dve.memset(acc[:, :, :], 0.0).then_inc(s_add, NBANK)

                    def turn(i, with_deg):
                        base = window_starts(dve, i)

                        def make(g):
                            tiles = bass.ds(i * TB + g * U, U)
                            dve.wait_ge(s_mm, i * G + g + 1)
                            ins = dve.tensor_tensor(
                                onehot[:, g * U:(g + 1) * U, :], iota_w[:, :].unsqueeze(1).to_broadcast([P, U, P]),
                                dstloc[:, tiles].unsqueeze(2).to_broadcast([P, U, P]), ALU.is_equal)
                            if scaled:
                                dve.wait_ge(s_ga[g], (i + past) * (16 * U) + 16 * U)
                                rows = ring[:, g * U:(g + 1) * U, :].rearrange("p u (h d) -> p (u h) d", h=H)
                                al = alpha[:, tiles, :].rearrange("p u h -> p (u h)").unsqueeze(2)
                                ins = dve.tensor_tensor(rows, rows, al.to_broadcast([P, U * H, D]), ALU.mult)
                            ins.then_inc(s_oh, 1)

                        def add(g):
                            q = i * G + g
                            dve.wait_ge(s_mm, q + G + 1)
                            dve.wait_ge(s_add, q + NBANK)
                            a = acc[:, :, bass.ds(base[g], P)]
                            dve.tensor_tensor(a, a, PS[:, g % NBANK, 0:K2 * P].rearrange("p (k n) -> p k n", k=K2),
                                              ALU.add).then_inc(s_add, 1)

                        make(0)
                        for g in range(1, G):
                            make(g)
                            add(g - 1)
                        add(G - 1)
                        if with_deg:
                            cols = bass.ds(i * CW, CW)
                            dve.tensor_scalar(deg[:, cols], deg[:, cols], 1.0, None, ALU.max).then_inc(s_dg, 1)
                            dve.wait_ge(s_dg, 2 * i + 1)
                            dve.sem_inc(passed, 1)
                            dve.reciprocal(deg[:, cols], deg[:, cols]).then_inc(s_dg, 1)

                    if layer == 0:
                        with dve.Fori(0, NC) as i:
                            turn(i, True)
                    with dve.Fori(NC if layer == 0 else 0, n) as i:
                        turn(i, False)
                    dve.wait_ge(s_add, n * G + NBANK)
                    dve.sem_inc(passed, 1)

        end_phase()
        edge_pass(feat_tab[0:NBLK * P * R, :], fidx_i)

        end_phase()
        sort_edges(1, src, dst)
        tile_tables(1)

        end_phase()
        b4 = lambda a: a.rearrange("p (b f) -> p b f", b=4)
        k2 = lambda a: a.rearrange("p (k n) -> p k n", k=K2)
        xs = [work[:, 8192 + 1024 * i:9216 + 1024 * i] for i in range(2)]
        ac = [k2(work[:, 10240 + 1024 * i:11264 + 1024 * i]) for i in range(2)]
        tab = work[:, 12288:13312]
        h0 = [k2(stg[:, 4096 + 1024 * i:5120 + 1024 * i]) for i in range(2)]
        (s_w, s_xl, s_sx, s_ac, s_t1, s_x1, s_bs, s_vr, s_sd, s_rs, s_hn, s_t2, s_ht, s_wi, s_h0, s_t3, s_tb) = [sem(a) for a in (
             "weights_loaded", "x_loaded", "x1_stored", "acc_biased", "acc_turned", "x1_ready", "stats_done",
             "var_ready", "std_done", "rstd_done", "hn_ready", "hn_turned", "ht_ready", "input_layer_summed",
             "h0_kept", "rows_summed", "rows_ready")]
        s_st = nc.alloc_semaphore("h0_rows_stored")
        s_xl = [s_xl, sem("x_loaded")]
        x1_rows = x1_tab.rearrange("(c b p) f -> c p b f", b=4, p=P)
        h_rows = h_tab.rearrange("(c b p) f -> c p b f", b=4, p=P)
        LAST = N - (NC - 1) * CW - P

        def rows_by_weight(pe, bank, cols, weight):
            for b in range(4):
                for k in range(K2):
                    mm = pe.matmul(PS[:, bank + b // 2, (b % 2) * F:(b % 2 + 1) * F], cols[:, k, b * P:(b + 1) * P],
                                   weight[:, k, :], start=(k == 0), stop=(k == K2 - 1))
            return mm

        def chunk_of(rows, c):
            return rows[bass.ds(c, 1), :, :, :].rearrange("o p b f -> p (o b) f")

        has = lambda c, d: not isinstance(c, int) or 0 <= c + d < NC

        with nc.Block() as block:
            @block.sync
            def _(sp):
                def store_x1(c, slot):
                    sp.wait_ge(s_x1, c + 1)
                    sp.dma_start(chunk_of(x1_rows, c), b4(xs[slot])).then_inc(s_sx, 16)

                def step(c, slot, first, last):
                    if has(c, -2):
                        sp.wait_ge(s_hn, 4 * c - 4)
                        sp.sem_inc(passed, 1)
                        sp.wait_ge(s_sx, 16 * c - 16)
                        sp.sem_inc(passed, 1)
                    if not last:
                        sp.dma_start(b4(xs[slot]), x[bass.ds(c * CW, CW), :].rearrange("(b p) f -> p b f", p=P)
                                     ).then_inc(s_xl[slot], 32)
                    else:
                        sp.dma_start(b4(xs[slot])[:, 0, :], x[c * CW:c * CW + P, :]).then_inc(s_xl[slot], 16)
                        sp.dma_start(b4(xs[slot])[0:LAST, 1, :], x[c * CW + P:N, :]).then_inc(s_xl[slot], 16)
                    if first:
                        for to, w in ((win, w_in), (wout, w_out)):
                            sp.dma_start(to, w.rearrange("(k p) n -> p k n", p=P)).then_inc(s_w, 16)
                        for to, w in ((wag, w_agg), (wse, w_self)):
                            sp.dma_start(to.rearrange("p l k n -> p (l k) n"),
                                         w.rearrange("l (k p) n -> p (l k) n", p=P)).then_inc(s_w, 16)
                    if has(c, -1):
                        store_x1(c - 1, 1 - slot)

                over_chunks(sp, step)
                store_x1(NC - 1, 1)
                sp.wait_ge(s_w, 16 * 4)
                sp.wait_ge(s_sx, 16 * NC)

            @block.scalar
            def _(act):
                def bias_acc(c, slot):
                    for k in range(K2):
                        act.activation(ac[slot][:, k, :], acc[:, k, bass.ds(c * CW, CW)], ACT.Identity,
                                       bias=hb_c[:, k:k + 1]).then_inc(s_ac, 1)

                def roots(c, slot):
                    act.wait_ge(s_vr, 4 * c + 4)
                    act.activation(std[:, slot, :], mv[:, slot, :, 1], ACT.Sqrt, bias=eps_c[:, :]).then_inc(s_sd, 1)

                def keep_h0(c, slot):
                    act.wait_ge(s_wi, c + 1)
                    wait_past(act, s_t3, c - 1)
                    act.sem_inc(passed, 1)
                    for f in range(K2):
                        act.activation(h0[slot][:, f, :], PS[:, 4 + f, :], ACT.Identity, bias=bin_c[:, f:f + 1]
                                       ).then_inc(s_h0, 1)
                    for f in range(K2):
                        act.activation(hT[:, f, bass.ds(c * CW, CW)], PS[:, 4 + f, :], ACT.Identity,
                                       bias=bin_c[:, f:f + 1]).then_inc(s_h0, 1)

                def step(c, slot, first, last):
                    if has(c, 2):
                        act.wait_ge(s_t1, c + 1)
                        act.sem_inc(passed, 1)
                        bias_acc(c + 2, slot)
                    if has(c, 1):
                        roots(c + 1, 1 - slot)
                    act.wait_ge(s_t2, c + 1)
                    wait_past(act, s_wi, c - 1)
                    act.activation(hTs[:, slot, :, :], PS[:, 2:4, :], ACT.Relu).then_inc(s_ht, 1)
                    if has(c, -1):
                        keep_h0(c - 1, 1 - slot)

                bias_acc(0, 0)
                bias_acc(1, 1)
                roots(0, 0)
                over_chunks(act, step)
                keep_h0(NC - 1, 1)

            @block.gpsimd
            def _(pool):
                def step(c, slot, first, last):
                    pool.wait_ge(s_tb, c + 1)
                    pool.sem_inc(passed, 1)
                    pool.dma_start(chunk_of(h_rows, c), b4(tab)).then_inc(s_st, 16)

                over_chunks(pool, step)
                pool.wait_ge(s_st, 16 * NC)

            @block.tensor
            def _(pe):
                def rows_of(bank, cols):
                    for b in range(4):
                        for k in range(K2):
                            mm = pe.transpose(PS[:, bank + b // 2, (b % 2) * F + k * P:(b % 2) * F + (k + 1) * P],
                                              cols[:, k, b * P:(b + 1) * P], ident[:, :])
                    return mm

                def turn_acc(c, slot):
                    pe.wait_ge(s_ac, 2 * c + 2)
                    wait_past(pe, s_x1, c)
                    rows_of(0, ac[slot]).then_inc(s_t1, 1)

                def input_layer(c, slot):
                    pe.wait_ge(s_ht, c + 1)
                    wait_past(pe, s_h0, 4 * c)
                    for f in range(K2):
                        for k in range(K2):
                            mm = pe.matmul(PS[:, 4 + f, :], win[:, k, f * P:(f + 1) * P], hTs[:, slot, k, :],
                                           start=(k == 0), stop=(k == K2 - 1))
                    mm.then_inc(s_wi, 1)

                def turn_h0(c, slot):
                    pe.wait_ge(s_h0, 4 * c + 2)
                    wait_past(pe, s_tb, c)
                    rows_by_weight(pe, 6, h0[slot], wag[:, 0, :, :]).then_inc(s_t3, 1)

                def step(c, slot, first, last):
                    pe.wait_ge(s_hn, 4 * c + 4)
                    wait_past(pe, s_ht, c)
                    for b in range(4):
                        for k in range(K2):
                            mm = pe.transpose(PS[:, 2 + k, b * P:(b + 1) * P], hN[:, slot, b, k * P:(k + 1) * P],
                                              ident[:, :])
                    mm.then_inc(s_t2, 1)
                    if has(c, -1):
                        input_layer(c - 1, 1 - slot)
                    if has(c, 2):
                        turn_acc(c + 2, slot)
                    if has(c, -2):
                        turn_h0(c - 2, slot)

                turn_acc(0, 0)
                turn_acc(1, 1)
                pe.wait_ge(s_w, 16 * 4)
                over_chunks(pe, step)
                input_layer(NC - 1, 1)
                turn_h0(NC - 2, 0)
                turn_h0(NC - 1, 1)

            @block.vector
            def _(dve):
                def add_x(c, slot):
                    dve.wait_ge(s_xl[slot], 16 * (c - slot) + 32)
                    dve.wait_ge(s_t1, c + 1)
                    dve.tensor_tensor(xs[slot].rearrange("p (j n) -> p j n", j=2), PS[:, 0:2, :],
                                      xs[slot].rearrange("p (j n) -> p j n", j=2), ALU.add).then_inc(s_x1, 1)

                def keep_rows(c):
                    dve.wait_ge(s_t3, c + 1)
                    wait_past(dve, s_st, 16 * c)
                    dve.tensor_scalar(tab.rearrange("p (j n) -> p j n", j=2), PS[:, 6:8, :], 0.0, None, ALU.add
                                      ).then_inc(s_tb, 1)

                def norm(c, slot):
                    dve.wait_ge(s_x1, c + 1)
                    wait_past(dve, s_t2, c - 1)
                    rows = lambda b: b4(xs[slot])[:, b, :]
                    ln_stats(dve, rows, c, slot, s_bs, s_vr)
                    ln_finish(dve, rows, c, slot, s_sd, s_rs, s_hn)

                def step(c, slot, first, last):
                    if has(c, 1):
                        norm(c + 1, 1 - slot)
                    if has(c, 2):
                        add_x(c + 2, slot)
                    if has(c, -2):
                        keep_rows(c - 2)

                add_x(0, 0)
                norm(0, 0)
                add_x(1, 1)
                over_chunks(dve, step)
                keep_rows(NC - 2)
                keep_rows(NC - 1)

        hs, ts = [[stg[:, 2048 * j + 1024 * i:2048 * j + 1024 * (i + 1)] for i in range(2)] for j in range(2)]
        x1b = [work[:, 8192 + 1024 * i:9216 + 1024 * i] for i in range(2)]

        def hidden(l):
            last_layer = l == LAYERS - 1
            kept = 1 if last_layer else 2
            s_sc, s_sum, s_hr, s_tn, s_tk, s_st, s_xl, s_xb = [sem(a) for a in (
                "mean_ready", "layer_summed", "h_ready", "rows_summed", "rows_ready", "rows_stored",
                "x1_loaded", "x1_biased")]
            s_xl, s_st = [s_xl, sem("x1_loaded")], [s_st, sem("rows_stored")]

            def mean(eng, c):
                cols = bass.ds(c * CW, CW)
                eng.tensor_tensor(acc[:, :, cols], acc[:, :, cols],
                                  deg[:, cols].unsqueeze(1).to_broadcast([P, K2, CW]), ALU.mult).then_inc(s_sc, 1)

            with nc.Block() as block:
                @block.vector
                def _(dve):
                    def keep_rows(c, slot):
                        dve.wait_ge(s_tn, c + 1)
                        wait_past(dve, s_st[slot], 8 * (c - slot))
                        banks, o = PS[:, 4 + 2 * slot:6 + 2 * slot, :], ts[slot].rearrange("p (j n) -> p j n", j=2)
                        if last_layer:
                            dve.wait_ge(s_xb, c + 1)
                            dve.tensor_tensor(o, banks, x1b[slot].rearrange("p (j n) -> p j n", j=2), ALU.add
                                              ).then_inc(s_tk, 1)
                        else:
                            dve.tensor_scalar(o, banks, 0.0, None, ALU.add).then_inc(s_tk, 1)

                    def add_self(c):
                        cols = bass.ds(c * CW, CW)
                        dve.wait_ge(s_sc, c + 1)
                        dve.tensor_tensor(hT[:, :, cols], hT[:, :, cols], acc[:, :, cols], ALU.add
                                          ).then_inc(s_sum, 1)

                    def step(c, slot, first, last):
                        if last_layer and has(c, 2):
                            mean(dve, c + 2)
                        if has(c, 1):
                            add_self(c + 1)
                        if has(c, -1):
                            keep_rows(c - 1, 1 - slot)

                    if last_layer:
                        mean(dve, 0)
                        mean(dve, 1)
                    add_self(0)
                    over_chunks(dve, step)
                    keep_rows(NC - 1, (NC - 1) % 2)

                @block.tensor
                def _(pe):
                    def step(c, slot, first, last):
                        pe.wait_ge(s_hr, kept * c + 1)
                        if not first:
                            wait_past(pe, s_tk, c - 1)
                        weight = wout if last_layer else wag[:, l + 1, :, :]
                        rows_by_weight(pe, 4 + 2 * slot, k2(hs[slot]), weight).then_inc(s_tn, 1)

                    over_chunks(pe, step)

                @block.scalar
                def _(act):
                    def step(c, slot, first, last):
                        cols = bass.ds(c * CW, CW)
                        act.wait_ge(s_sum, c + 1)
                        if not first:
                            wait_past(act, s_tn, c - 1)
                        act.sem_inc(passed, 1)
                        act.activation(k2(hs[slot]), hT[:, :, cols], ACT.Relu).then_inc(s_hr, 1)
                        if not last_layer:
                            act.activation(hT[:, :, cols], hT[:, :, cols], ACT.Relu).then_inc(s_hr, 1)

                    over_chunks(act, step)

                @block.gpsimd
                def _(pool):
                    def step(c, slot, first, last):
                        pool.wait_ge(s_xl[slot], 8 * (c - slot) + 16)
                        pool.tensor_tensor(b4(x1b[slot]), b4(x1b[slot]),
                                           bout_b[:, :].unsqueeze(1).to_broadcast([P, 4, F]), ALU.add
                                           ).then_inc(s_xb, 1)

                    if last_layer:
                        over_chunks(pool, step)
                    else:
                        over_chunks(pool, lambda c, slot, first, last: mean(pool, c))

                @block.sync
                def _(sp):
                    def store(c, slot, last):
                        sp.wait_ge(s_tk, c + 1)
                        if not last_layer:
                            sp.dma_start(chunk_of(h_rows, c), b4(ts[slot])).then_inc(s_st[slot], 16)
                        elif not last:
                            sp.dma_start(out[bass.ds(c * CW, CW), :].rearrange("(b p) f -> p b f", p=P),
                                         b4(ts[slot])).then_inc(s_st[slot], 16)
                        else:
                            sp.dma_start(out[c * CW:c * CW + P, :], b4(ts[slot])[:, 0, :]).then_inc(s_st[slot], 16)
                            sp.dma_start(out[c * CW + P:N, :], b4(ts[slot])[0:LAST, 1, :]).then_inc(s_st[slot], 16)

                    def step(c, slot, first, last):
                        if last_layer:
                            if not first:
                                wait_past(sp, s_tk, c - 1)
                            sp.dma_start(b4(x1b[slot]), chunk_of(x1_rows, c)).then_inc(s_xl[slot], 16)
                        if not first:
                            store(c - 1, 1 - slot, False)

                    over_chunks(sp, step)
                    store(NC - 1, (NC - 1) % 2, True)
                    sp.wait_ge(s_st[0], 16 * NC // 2)
                    sp.wait_ge(s_st[1], 16 * (NC // 2 + last_layer))

        end_phase()
        for l in range(LAYERS):
            edge_pass(h_tab[:, :], src_i, l)
            hidden(l)


_INS = ["x", "src", "dst", "edge_type_8", "L0_gnn_conv_weights", "L0_gnn_attn_l", "L0_gnn_attn_r",
        "L0_gnn_h_bias", "L1_gnn_W_in", "L1_gnn_b_in", "L1_gnn_W_agg", "L1_gnn_W_self", "L1_gnn_b_hid",
        "L1_gnn_W_out", "L1_gnn_b_out"]


def kernel(**inputs):
    import numpy as _np
    import concourse.bacc as _bacc
    from concourse import mybir as _mybir
    from concourse.bass_utils import run_bass_kernel_spmd as _run

    nc = _bacc.Bacc("TRN2", target_bir_lowering=False, num_devices=1)
    arrays, args = {}, []
    for name in _INS:
        a = _np.ascontiguousarray(inputs[name])
        arrays[f"in_{name}"] = a
        args.append(nc.dram_tensor(f"in_{name}", a.shape, _mybir.dt.from_np(a.dtype), kind="ExternalInput").ap())
    args.append(nc.dram_tensor("out_0", (N, F), _mybir.dt.float32, kind="ExternalOutput").ap())
    gnn_kernel(nc, *args)
    r = _run(nc, [arrays], core_ids=[0])
    return r.results[0]["out_0"]
```

```python
import concourse.bass as bass
from concourse import mybir
from contextlib import ExitStack, nullcontext

FP32 = mybir.dt.float32
BF16 = mybir.dt.bfloat16
I32 = mybir.dt.int32
ALU = mybir.AluOpType
ACT = mybir.ActivationFunctionType
AX = mybir.AxisListType

P = 128
N, E, F, R, H, D = 3750, 63750, 256, 8, 4, 64
LAYERS = 3
K2 = F // P
NBLK = (N + P - 1) // P
NC = 8
CW = 4 * P
NP = NC * CW
NTAB = (NBLK + 1) * P
RH = R * H
KW = 32
U, G = 4, 6
TB = U * G
ADDED = U
TURNS = -(-E // (P * TB))
TURNS_SORTED = -(-(E + ADDED * N) // (P * TB))
CT = 5
T = CT * P
NG = T // U
FBLK = TURNS_SORTED * G // 4 + 1
BIG = 1e30
EPS = 1e-5
SLOPE = 0.2
NBANK = 3
WLEN = 8192 + TB * F


class Chain:

    def __init__(self, eng, sem, before=0):
        self.eng, self.sem, self.before, self.n = eng, sem, before, 0

    def link(self, ins):
        ins.then_inc(self.sem, 1)
        self.n += 1
        self.eng.wait_ge(self.sem, self.before + self.n)


def gnn_kernel(nc, x, src, dst, etype, conv_w, attn_l, attn_r, h_bias, w_in, b_in, w_agg, w_self,
               b_hid, w_out, b_out, out):
    ctx = ExitStack()
    with ctx:
        def sb(name, shape, dt=FP32):
            return ctx.enter_context(nc.sbuf_tensor(name, shape, dt))

        def dram(name, shape, dt=FP32):
            return nc.dram_tensor(name, shape, dt, kind="Internal").ap()

        names = {}

        phase_sems = []

        def sem(name):
            names[name] = names.get(name, 0) + 1
            s = nc.alloc_semaphore(f"{name}_{names[name]}")
            phase_sems.append(s)
            return s

        passed = nc.alloc_semaphore("passed")
        s_ga = [nc.alloc_semaphore(f"rows_gathered{g}") for g in range(G)]

        def end_phase():
            with nc.Block() as block:
                @block.gpsimd
                def _(pool):
                    for s in phase_sems:
                        pool.sem_clear(s)
            for s in phase_sems:
                nc.release_semaphore(s)
            phase_sems.clear()

        el_tab = dram("el_tab", [NTAB, RH + KW])
        er_tab = dram("er_tab", [NTAB, RH + KW])
        feat_tab = dram("feat_tab", [FBLK * P * R, F])
        x1_tab = dram("x1_tab", [NP, F])
        h_tab = [dram(f"h_tab{i}", [NP, F]) for i in range(2)]
        dstm_row = dram("dstm_row", [CT, P, P])

        work = sb("work", [P, WLEN])
        hT = sb("hT", [P, K2, FBLK * P])
        deg = sb("deg", [P, NP])
        wbuf = sb("wbuf", [P, 4096])
        stg = sb("stg", [P, 6400])
        acc = work[:, 0:8192].rearrange("p (k n) -> p k n", k=K2)
        src_i = sb("src_i", [P, T + TB], I32)
        fidx_i = sb("fidx_i", [P, T + TB], I32)
        dstloc = sb("dstloc", [P, T])
        nodeid = sb("nodeid", [P, NG])
        typ_t = sb("typ_t", [P, T])
        pad_t = sb("pad_t", [P, T])
        alpha = sb("alpha", [P, T, H])
        base_i = sb("base_i", [1, NG], I32)
        io_i = sb("io_i", [P, P + 1], I32)
        iota_w = sb("iota_w", [P, P])
        iota_p = sb("iota_p", [P, 1])
        ident = sb("ident", [P, P])
        ones = sb("ones", [P, P])
        ones_b = sb("ones_b", [P, P], BF16)
        hb_c = sb("hb_c", [P, K2])
        bin_c = sb("bin_c", [P, K2])
        bh_c = sb("bh_c", [P, LAYERS, K2])
        bout_b = sb("bout_b", [P, F])
        wlr = sb("wlr", [P, K2, 2 * RH])
        eps_c = sb("eps_c", [P, 1])
        stats = sb("stats", [P, 2, 4, 6])
        mv = sb("mv", [P, 2, 4, 2])
        std = sb("std", [P, 2, 4])
        rstd = sb("rstd", [P, 2, 4])
        idx_ring = sb("idx_ring", [P, TB], I32)
        small = sb("small", [P, 64])
        turns_i = sb("turns_i", [1, 2], I32)
        flags_i = sb("flags_i", [1, 2], I32)
        cuts_i = sb("cuts_i", [1, NC + 1], I32)
        msum = sb("msum", [KW, 3 * KW])
        cT = sb("cT", [P, 2, CT, H])
        PS = ctx.enter_context(nc.psum_tensor("PS", [P, 8, 512], FP32))

        held = {}

        def base_regs(eng):
            if eng.engine not in held:
                held[eng.engine] = [eng.alloc_register(f"window{g}") for g in range(G)]
            return held[eng.engine]

        def window_starts(eng, i):
            regs = base_regs(eng)
            eng.load(regs, base_i[0:1, bass.ds(i * G, G)])
            return [eng.snap(r, min_val=0, max_val=N - 1) for r in regs]

        def turns_of(eng, which=0):
            return eng.value_load(turns_i[0:1, which:which + 1], min_val=TURNS, max_val=TURNS_SORTED)

        def when(eng, flag):
            if flag is None:
                return nullcontext()
            return eng.If(eng.value_load(flags_i[0:1, flag:flag + 1], min_val=0, max_val=1) > 0)

        def over_chunks(eng, step):
            for c in range(2):
                step(c, c, c == 0, False)
            with eng.Fori(1, NC // 2 - 1) as i:
                step(2 * i, 0, False, False)
                step(2 * i + 1, 1, False, False)
            for c in range(NC - 2, NC):
                step(c, c % 2, False, c == NC - 1)

        def wait_past(eng, s, count):
            if not isinstance(count, int) or count > 0:
                eng.wait_ge(s, count)

        def gathered_turns(eng, passes):
            past = turns_of(eng) * min(passes, 2)
            return past + turns_of(eng, 1) * (passes - 2) if passes > 2 else past

        s_io, s_c = sem("iotas"), sem("consts")
        wc = wbuf[:, :].rearrange("p (k n) -> p k n", k=K2)
        x_all = work[:, 0:8192].rearrange("p (b f) -> p b f", b=32)
        s_xz = sem("x_zeroed")
        s_ld, s_xl, s_at = [nc.alloc_semaphore(a) for a in ("vectors_loaded", "all_x_loaded", "weights_in")]
        whash = alpha[:, :, :].rearrange("p t h -> p (t h)")[:, 0:32 * KW].rearrange("p (b k) -> p b k", b=32)
        hash_i = stg[:, 4096:4096 + 32 * KW].bitcast(I32)
        prod = [work[:, 8192 + 2048 * i:8192 + 2048 * (i + 1)] for i in range(2)]

        def hrow(i):
            return hT[:, :, :].rearrange("p k n -> p (k n)")[:, i * T:(i + 1) * T].rearrange(
                "p (c j) -> p c j", c=CT)

        key, dstm, srcr, typr, fidx = [hrow(i) for i in range(5)]
        raw = [hrow(5 + i).bitcast(I32) for i in range(4)]
        rows4 = hT[0:H, :, :].rearrange("p k n -> p (k n)")
        s_pad, s_rl, s_cv = sem("pads_set"), sem("rows_loaded"), sem("rows_converted")
        whole, rest = divmod(E - 3 * P * P, P)

        attn = [hT[:, :, :].rearrange("p k n -> p (k n)")[:, 9 * T + 2048 * i:9 * T + 2048 * (i + 1)]
                for i in range(2)]

        with nc.Block() as block:
            @block.sync
            def _(sp):
                sp.wait_ge(s_pad, 4)
                for a, buf in zip((dst, dst, src, etype), raw):
                    sp.dma_start(buf[:, 0:3, :], a[0:3 * P * P].rearrange("(c p j) -> p c j", c=3, p=P)
                                 ).then_inc(s_rl, 16)
                    sp.dma_start(buf[0:whole, 3, :], a[3 * P * P:E - rest].rearrange("(p j) -> p j", j=P)
                                 ).then_inc(s_rl, 16)
                    sp.dma_start(buf[whole:whole + 1, 3, 0:rest],
                                 a[E - rest:E].rearrange("(o j) -> o j", o=1)).then_inc(s_rl, 16)
                for a, buf in zip((attn_l, attn_r), attn):
                    sp.dma_start(buf, a.rearrange("(o r) h d -> o (r h d)", o=1).to_broadcast([P, 2048])
                                 ).then_inc(s_at, 16)
                for k in range(K2):
                    for r in range(R):
                        sp.dma_start(wc[:, k, r * F:(r + 1) * F].rearrange("p (h d) -> p h d", h=H),
                                     conv_w[r, :, k * P:(k + 1) * P, :].rearrange("h p d -> p h d")
                                     ).then_inc(s_at, 16)
                sp.wait_ge(s_xz, 1)
                full = NBLK - 1
                sp.dma_start(x_all[:, 0:full, :],
                             x[0:full * P, :].rearrange("(b p) f -> p b f", p=P)).then_inc(s_xl, 16)
                sp.dma_start(x_all[0:N - full * P, full, :], x[full * P:N, :]).then_inc(s_xl, 16)
                for buf, v in ((hb_c, h_bias), (bin_c, b_in)):
                    sp.dma_start(buf[:, :], v.rearrange("(k p) -> p k", p=P),
                                 allow_slow_non_contiguous=True).then_inc(s_ld, 16)
                sp.dma_start(bh_c[:, :, :], b_hid.rearrange("l (k p) -> p l k", p=P),
                             allow_slow_non_contiguous=True).then_inc(s_ld, 16)
                sp.dma_start(bout_b[:, :], b_out.rearrange("(o n) -> o n", o=1).to_broadcast([P, F])
                             ).then_inc(s_ld, 16)

            @block.gpsimd
            def _(pool):
                pool.iota(io_i[:, 0:P], pattern=[[1, P]], base=0, channel_multiplier=0).then_inc(s_io, 1)
                pool.iota(io_i[:, P:P + 1], pattern=[[1, 1]], base=0, channel_multiplier=1).then_inc(s_io, 1)
                pool.iota(hash_i, pattern=[[P * 251, 32], [7919, KW]], base=0, channel_multiplier=251).then_inc(s_io, 1)

            @block.vector
            def _(dve):
                for v, buf in zip((N - 1, -1, 0, 0), raw):
                    dve.memset(buf[:, 3:CT, :], v).then_inc(s_pad, 1)
                dve.memset(x_all[:, NBLK - 1:32, :], 0.0).then_inc(s_xz, 1)
                dve.memset(ones[:, :], 1.0)
                for a in (src_i, fidx_i):
                    dve.memset(a[:, T:T + TB], 0)
                dve.memset(ones_b[:, :], 1.0)
                dve.memset(eps_c[:, :], EPS)
                c = Chain(dve, s_c)
                dve.wait_ge(s_io, 2)
                c.link(dve.tensor_copy(iota_w[:, :], io_i[:, 0:P]))
                c.link(dve.tensor_copy(iota_p[:, :], io_i[:, P:P + 1]))
                c.link(dve.tensor_scalar(ident[:, :], iota_w[:, :], iota_p[:, :], None, ALU.is_equal))
                dve.wait_ge(s_io, 3)
                c.link(dve.tensor_scalar(hash_i, hash_i, 4095, None, ALU.bitwise_and))
                c.link(dve.tensor_copy(prod[0][:, 0:32 * KW], hash_i))
                c.link(dve.tensor_tensor(hash_i, prod[0][:, 0:32 * KW], prod[0][:, 0:32 * KW], ALU.mult))
                c.link(dve.tensor_scalar(hash_i, hash_i, 12, 15, ALU.arith_shift_right, ALU.bitwise_and))
                c.link(dve.tensor_copy(whash[:, :, :].rearrange("p b k -> p (b k)"), hash_i))
                dve.wait_ge(s_rl, 48 * 4)
                for buf, to in zip(raw, (key, dstm, srcr, typr)):
                    dve.tensor_copy(to, buf).then_inc(s_cv, 1)
                dve.wait_ge(s_cv, 4)

        base_r, last_r = stg[0:H, 0:T], stg[0:H, T:2 * T]
        first_c = stg[:, 2 * T:2 * T + CT * H].rearrange("p (c h) -> p c h", h=H)
        last_c = stg[:, 2 * T + 32:2 * T + 32 + CT * H].rearrange("p (c h) -> p c h", h=H)

        def tile_ends(flag=None):
            s_fc, s_tp, s_br = sem("ends_picked"), sem("ends_turned"), sem("ends_rowed")
            with nc.Block() as block:
                @block.vector
                def _(dve):
                    with when(dve, flag):
                        dve.tensor_copy(first_c, key[:, :, 0:1].to_broadcast([P, CT, H])).then_inc(s_fc, 1)
                        dve.tensor_copy(last_c, key[:, :, P - 1:P].to_broadcast([P, CT, H])).then_inc(s_fc, 1)
                        dve.wait_ge(s_tp, 1)
                        for i, to in enumerate((base_r, last_r)):
                            dve.tensor_copy(to[:, 0:512], PS[0:H, 2 * i, :]).then_inc(s_br, 1)
                            dve.tensor_copy(to[:, 512:T], PS[0:H, 2 * i + 1, 0:P]).then_inc(s_br, 1)
                        dve.wait_ge(s_br, 4)
                        dve.sem_inc(passed, 1)

                @block.tensor
                def _(pe):
                    with when(pe, flag):
                        pe.wait_ge(s_fc, 2)
                        for i, c4 in enumerate((first_c, last_c)):
                            for c in range(CT):
                                mm = pe.transpose(PS[0:H, 2 * i + c // 4, (c % 4) * P:(c % 4 + 1) * P],
                                                  c4[:, c, :], ident[:, :])
                        mm.then_inc(s_tp, 1)

        tile_ends()

        s_k, s_ks = sem("check_steps"), sem("check_sum")
        bad, viol = small[:, 0:4], stg[:, 2048:2048 + CT * (P - 1)].rearrange("p (c j) -> p c j", c=CT)
        with nc.Block() as block:
            @block.vector
            def _(dve):
                c = Chain(dve, s_k)
                c.link(dve.tensor_tensor(viol, key[:, :, 1:P], key[:, :, 0:P - 1], ALU.is_lt))
                c.link(dve.tensor_reduce(bad[:, 0:1], viol, AX.XY, ALU.add))
                spans = stg[0:1, 3700:3700 + NG]
                c.link(dve.tensor_tensor(spans, last_r[0:1, U - 1:T:U], base_r[0:1, 0:T:U], ALU.subtract))
                c.link(dve.tensor_scalar(spans, spans, float(P - 1), None, ALU.is_gt))
                c.link(dve.tensor_reduce(small[0:1, 23:24], spans, AX.X, ALU.add))
                c.link(dve.tensor_tensor(stg[0:1, 3000:3000 + T - 1], last_r[0:1, 0:T - 1], base_r[0:1, 1:T],
                                         ALU.is_gt))
                c.link(dve.tensor_reduce(small[0:1, 24:25], stg[0:1, 3000:3000 + T - 1], AX.X, ALU.add))
                c.link(dve.tensor_tensor(small[0:1, 24:25], small[0:1, 23:24], small[0:1, 24:25], ALU.add))
                dve.wait_ge(s_ks, 1)
                c.link(dve.tensor_tensor(small[0:1, 25:26], PS[0:1, 0, 0:1], small[0:1, 24:25], ALU.add))
                c.link(dve.tensor_scalar(small[0:1, 26:27], small[0:1, 25:26], 0.0,
                                         float(TURNS_SORTED - TURNS), ALU.is_gt, ALU.mult))
                c.link(dve.tensor_scalar(turns_i[0:1, 0:1], small[0:1, 26:27], float(TURNS), None, ALU.add))
                c.link(dve.tensor_scalar(flags_i[0:1, 0:1], small[0:1, 25:26], 0.0, None, ALU.is_gt))

            @block.tensor
            def _(pe):
                pe.wait_ge(s_k, 2)
                pe.matmul(PS[0:1, 0, 0:1], bad[:, 0:1], ones[:, 0:1], start=True, stop=True).then_inc(s_ks, 1)

        SW = -(-(E + ADDED * N) // P)
        EXTRA = P * SW - E
        head_rows, head_cols = divmod(EXTRA, SW)
        rec_tab = dram("rec_tab", [P * SW, 4])

        def sort_edges(flag, key_array, other_array):
            rec = work[:, 8192:8192 + 4 * SW].rearrange("p (j a) -> p j a", a=4)
            raw_s = [work[:, 8192 + (4 + i) * SW:8192 + (5 + i) * SW].bitcast(I32) for i in range(3)]
            pos, hit, rank, tmp, zero = [stg[:, i * SW:(i + 1) * SW] for i in range(5)]
            entry_i, pos_i = [stg[:, (5 + i) * SW:(6 + i) * SW].bitcast(I32) for i in range(2)]
            val, place0, off = small[:, 32:33], small[:, 33:34], small[:, 34:35]
            tri = stg[:, 7 * SW:7 * SW + P]
            idx4 = idx_ring[:, 0:4]
            rec4 = stg[:, 7 * SW + P:7 * SW + P + 16].rearrange("p (s a) -> p s a", a=4)
            back = work[:, 8192:8192 + CT * 4 * P].rearrange("p (c j a) -> p c j a", c=CT, a=4)
            back_whole, back_rest = divmod(SW, P)
            s_z, s_l, s_e, s_a, s_pk, s_pp, s_pi, s_cp, s_is, s_sd, s_rl, s_rd = [sem(a) for a in (
                "rows_zeroed", "edges_loaded", "entries_numbered", "sort_steps", "ranks_ready", "offsets_ready",
                "places_ready", "records_picked", "scatters_issued", "all_scattered", "sorted_loaded", "place_steps")]
            s_sc = [nc.alloc_semaphore(f"scattered{i}_{flag}") for i in range(4)]
            STEPS = 9

            with nc.Block() as block:
                @block.sync
                def _(sp):
                    with when(sp, flag):
                        sp.wait_ge(s_z, 3)
                        for a, buf in zip((key_array, other_array, etype), raw_s):
                            sp.dma_start(buf[head_rows:head_rows + 1, head_cols:SW],
                                         a[0:SW - head_cols].rearrange("(o j) -> o j", o=1)).then_inc(s_l, 16)
                            sp.dma_start(buf[head_rows + 1:P, :],
                                         a[SW - head_cols:E].rearrange("(p j) -> p j", j=SW)).then_inc(s_l, 16)
                        sp.wait_ge(s_cp, 2 * SW)
                        sp.wait_ge(s_sd, 1)
                        rows = rec_tab.rearrange("(t j) a -> t (j a)", j=P)
                        for cc in range(back_whole + 1):
                            k = P if cc < back_whole else back_rest
                            sp.dma_start(back[0:k, cc, :, :].rearrange("p j a -> p (j a)"), rows[cc * P:cc * P + k, :]
                                         ).then_inc(s_rl, 16)

                @block.gpsimd
                def _(pool):
                    with when(pool, flag):
                        pool.iota(entry_i, pattern=[[1, SW]], base=0, channel_multiplier=SW).then_inc(s_e, 1)
                        with pool.Fori(0, SW // 4) as i:
                            for s in range(4):
                                pool.wait_ge(s_cp, i * 8 + 2 * s + 2)
                                pool.sem_inc(s_is, 1)
                                pool.indirect_dma_start(
                                    out=rec_tab[:, :], out_offset=bass.IndirectOffsetOnAxis(ap=idx4[:, s:s + 1], axis=0),
                                    in_=rec4[:, s, :], in_offset=None).then_inc(s_sc[s], 16)
                        for s in range(4):
                            pool.wait_ge(s_sc[s], 16 * (SW // 4))
                        pool.sem_inc(s_sd, 1)

                @block.tensor
                def _(pe):
                    with when(pe, flag):
                        with pe.Fori(0, N) as v:
                            pe.wait_ge(s_pk, v * STEPS + 2)
                            pe.matmul(PS[:, 0, 0:1], tri, rank[:, SW - 1:SW], start=True, stop=True)
                            pe.matmul(PS[:, 0, 1:2], ones[:, :], rank[:, SW - 1:SW], start=True, stop=True
                                      ).then_inc(s_pp, 1)

                @block.vector
                def _(dve):
                    with when(dve, flag):
                        for buf in raw_s:
                            dve.memset(buf, 0).then_inc(s_z, 1)
                        c = Chain(dve, s_a)
                        for a in (pos, zero, val):
                            c.link(dve.memset(a, 0.0))
                        c.link(dve.memset(place0, -1.0))
                        c.link(dve.tensor_scalar(tri, iota_w[:, :], iota_p[:, :], None, ALU.is_gt))
                        dve.wait_ge(s_l, 96)
                        dve.wait_ge(s_e, 1)
                        c.link(dve.tensor_copy(tmp, entry_i))
                        c.link(dve.tensor_scalar(hit, tmp, float(EXTRA), None, ALU.is_ge))
                        c.link(dve.tensor_scalar(entry_i, entry_i, 2, None, ALU.arith_shift_right))
                        c.link(dve.tensor_copy(rank, entry_i))
                        c.link(dve.tensor_scalar(rank, rank, float(N - 1), None, ALU.min))
                        c.link(dve.tensor_copy(rec[:, :, 0], raw_s[0]))
                        c.link(dve.tensor_tensor(rec[:, :, 1], rec[:, :, 0], rank, ALU.subtract))
                        c.link(dve.tensor_tensor(rec[:, :, 1], rec[:, :, 1], hit, ALU.mult))
                        c.link(dve.tensor_tensor(rec[:, :, 0], rec[:, :, 1], rank, ALU.add))
                        c.link(dve.scalar_tensor_tensor(rec[:, :, 1], rec[:, :, 0], 1.0, hit, ALU.add, ALU.mult))
                        c.link(dve.tensor_scalar(rec[:, :, 1], rec[:, :, 1], 1.0, None, ALU.subtract))
                        c.link(dve.tensor_copy(rec[:, :, 2], raw_s[1]))
                        c.link(dve.tensor_copy(rec[:, :, 3], raw_s[2]))
                        dve.sem_inc(passed, 1)
                        with dve.Fori(0, N) as v:
                            c = Chain(dve, s_pk, v * STEPS)
                            c.link(dve.tensor_scalar(hit, rec[:, :, 0], val, None, ALU.is_equal))
                            c.link(dve.tensor_tensor_scan(rank, hit, zero, 0.0, ALU.add, ALU.add))
                            dve.wait_ge(s_pp, v + 1)
                            c.link(dve.tensor_tensor(off, PS[:, 0, 0:1], place0, ALU.add))
                            c.link(dve.scalar_tensor_tensor(tmp, rank, off, hit, ALU.add, ALU.mult))
                            c.link(dve.tensor_tensor(pos, pos, tmp, ALU.add))
                            c.link(dve.tensor_scalar(deg[:, bass.ds(v, 1)], PS[:, 0, 1:2], float(ADDED), None,
                                                     ALU.subtract))
                            c.link(dve.tensor_tensor(place0, place0, PS[:, 0, 1:2], ALU.add))
                            c.link(dve.tensor_scalar(val, val, 1.0, None, ALU.add))
                            c.link(dve.tensor_copy(small[:, 35:36], place0))
                            dve.sem_inc(passed, 1)
                        dve.tensor_scalar(deg[:, N - 1:N], deg[:, N - 1:N], float(EXTRA - ADDED * N), None,
                                          ALU.subtract).then_inc(s_pi, 1)
                        dve.tensor_copy(pos_i, pos).then_inc(s_pi, 1)
                        dve.wait_ge(s_pi, 2)

                        def pick(i, first=False):
                            for s in range(4):
                                if not first:
                                    dve.wait_ge(s_sc[s], i * 16)
                                dve.tensor_copy(idx4[:, s:s + 1], pos_i[:, bass.ds(i * 4 + s, 1)]).then_inc(s_cp, 1)
                                dve.tensor_copy(rec4[:, s, :], rec[:, bass.ds(i * 4 + s, 1), :].rearrange("p o a -> p (o a)")
                                                ).then_inc(s_cp, 1)

                        pick(0, first=True)
                        with dve.Fori(1, SW // 4) as i:
                            pick(i)
                        c = Chain(dve, s_rd)
                        for a, v in zip((key, dstm, srcr, typr), (N - 1, -1, 0, 0)):
                            c.link(dve.memset(a[:, back_whole:CT, :], float(v)))
                        dve.wait_ge(s_rl, 16 * (back_whole + 1))
                        for i, a in enumerate((key, dstm, srcr, typr)):
                            c.link(dve.tensor_copy(a[:, 0:back_whole, :], back[:, 0:back_whole, :, i]))
                            c.link(dve.tensor_copy(a[0:back_rest, back_whole, :], back[0:back_rest, back_whole, :, i]))


            tile_ends(flag)

        end_phase()
        sort_edges(0, dst, src)


        def tile_tables(flag=None):
            whole = flag is None
            s_f, s_tt, s_te, s_bb, s_dr = (sem("fidx_made"), sem("rows_turned"), sem("tiles_made"),
                                           sem("base_spread"), sem("dstm_stored"))
            turned = ((srcr, src_i), (dstm, dstloc)) + (((fidx, fidx_i), (typr, typ_t)) if whole else ())
            with nc.Block() as block:
                @block.vector
                def _(dve):
                    with when(dve, flag):
                        c = Chain(dve, s_f)
                        c.link(dve.scalar_tensor_tensor(fidx, srcr, float(R), typr, ALU.mult, ALU.add))
                        e = Chain(dve, s_te)
                        for i, (_, to) in enumerate(turned):
                            dve.wait_ge(s_tt, i + 1)
                            b = 2 * (i % 2)
                            e.link(dve.tensor_copy(to[:, 0:512], PS[:, b, :]))
                            e.link(dve.tensor_copy(to[:, 512:T], PS[:, b + 1, 0:P]))
                        if whole:
                            e.link(dve.tensor_scalar(pad_t[:, :], dstloc[:, :], 0.0, -BIG, ALU.is_lt, ALU.mult))
                        dve.wait_ge(s_bb, 1)
                        pb = PS[:, 4, 0:NG]
                        places = dstloc[:, :].rearrange("p (g u) -> p g u", u=U)
                        e.link(dve.tensor_tensor(places, places, pb.unsqueeze(2).to_broadcast([P, NG, U]),
                                                 ALU.subtract))
                        e.link(dve.tensor_scalar(nodeid[:, :], pb, iota_p[:, :], None, ALU.add))
                        e.link(dve.tensor_copy(base_i[:, :], base_r[0:1, 0:T:U]))
                        dve.sem_inc(passed, 1)

                @block.tensor
                def _(pe):
                    with when(pe, flag):
                        for i, (fr, _) in enumerate(turned):
                            if i == 0:
                                pe.wait_ge(s_f, 1)
                            if i >= 2:
                                pe.wait_ge(s_te, 2 * (i - 1))
                            for c in range(CT):
                                mm = pe.transpose(PS[:, 2 * (i % 2) + c // 4, (c % 4) * P:(c % 4 + 1) * P],
                                                  fr[:, c, :], ident[:, :])
                            mm.then_inc(s_tt, 1)
                        pe.matmul(PS[:, 4, 0:NG], ones[0:1, :], base_r[0:1, 0:T:U],
                                  start=True, stop=True).then_inc(s_bb, 1)

                @block.sync
                def _(sp):
                    if whole:
                        sp.dma_start(dstm_row.rearrange("c p j -> p c j"), dstm).then_inc(s_dr, 16)
                        sp.wait_ge(s_dr, 16)

        tile_tables()

        masks = sb("masks", [P, 3 * T + 1])
        same, firstm, lastm = masks[:, 0:T + 1], masks[:, T + 1:2 * T + 1], masks[:, 2 * T + 1:3 * T + 1]
        s_sm = sem("segments_marked")
        with nc.Block() as block:
            @block.vector
            def _(dve):
                c = Chain(dve, s_sm)
                c.link(dve.memset(same[:, :], 0.0))
                sv = same[:, 0:T].rearrange("p (c j) -> p c j", c=CT)
                c.link(dve.tensor_tensor(sv[:, :, 1:P], key[:, :, 1:P], key[:, :, 0:P - 1], ALU.is_equal))
                c.link(dve.tensor_tensor(firstm[:, :].rearrange("p (c j) -> p c j", c=CT), key,
                                         key[:, :, 0:1].to_broadcast([P, CT, P]), ALU.is_equal))
                c.link(dve.tensor_tensor(lastm[:, :].rearrange("p (c j) -> p c j", c=CT), key,
                                         key[:, :, P - 1:P].to_broadcast([P, CT, P]), ALU.is_equal))

        cont = sb("cont", [H, T + 1])
        single = sb("single", [H, T])
        with nc.Block() as block:
            s_ct = sem("conts_made")

            @block.vector
            def _(dve):
                c = Chain(dve, s_ct)
                c.link(dve.memset(cont[:, :], 0.0))
                c.link(dve.tensor_tensor(cont[:, 1:T], base_r[:, 1:T], last_r[:, 0:T - 1], ALU.is_equal))
                c.link(dve.tensor_tensor(single[:, :], base_r[:, :], last_r[:, :], ALU.is_equal))

        hN = stg[:, 0:2048].rearrange("p (s b f) -> p s b f", s=2, b=4)
        hTs = stg[:, 2048:4096].rearrange("p (s k n) -> p s k n", s=2, k=K2)
        elr = work[:, 8192:8192 + 32 * 3 * RH].rearrange("p (b i n) -> p b i n", b=32, i=3)

        def ln_stats(dve, rows, c, slot, stats_done, var_ready):
            for b in range(4):
                dve.bn_stats(stats[:, slot, b, :], rows(b)).then_inc(stats_done, 1)
            dve.wait_ge(stats_done, c * 4 + 4)
            dve.sem_inc(passed, 1)
            for b in range(4):
                dve.bn_aggr(mv[:, slot, b, :], stats[:, slot, b, :]).then_inc(var_ready, 1)

        def ln_finish(dve, rows, c, slot, std_done, rstd_done, hn_ready, to):
            dve.wait_ge(std_done, c + 1)
            dve.reciprocal(rstd[:, slot, :], std[:, slot, :]).then_inc(rstd_done, 1)
            dve.wait_ge(rstd_done, c + 1)
            for b in range(4):
                dve.tensor_scalar(to[:, b, :], rows(b), mv[:, slot, b, 0:1], rstd[:, slot, b:b + 1],
                                  ALU.subtract, ALU.mult).then_inc(hn_ready, 1)

        s_wi, s_bs, s_vr, s_sd, s_rs, s_hn, s_tp, s_ht, s_el, s_ee, s_et = [sem(x) for x in (
            "w_in_place", "stats_done", "var_ready", "std_done", "rstd_done", "hn_ready", "hn_turned", "ht_ready",
            "el_ready", "el_kept", "el_stored")]
        s_pr, s_pp = sem("products"), sem("pool_products")
        with nc.Block() as block:
            @block.vector
            def _(dve):
                def x_rows(c):
                    return lambda b: x_all[:, bass.ds(c * 4 + b, 1), :].rearrange("p o f -> p (o f)")

                def keep(c, slot):
                    dve.wait_ge(s_el, c + 1)
                    dve.tensor_scalar(elr[:, bass.ds(c * 4, 4), 0:3:2, :],
                                      PS[:, 4 + slot, 0:256].rearrange("p (b i n) -> p b i n", b=4, i=2),
                                      0.0, None, ALU.add).then_inc(s_ee, 1)

                def step(c, slot, first, last):
                    if not last:
                        ln_stats(dve, x_rows(c + 1), c + 1, 1 - slot, s_bs, s_vr)
                    if not first:
                        wait_past(dve, s_tp, c - 1)
                    ln_finish(dve, x_rows(c), c, slot, s_sd, s_rs, s_hn, hN[:, slot, :, :])
                    if not isinstance(c, int) or c > 1:
                        keep(c - 2, slot)

                c = Chain(dve, s_pr)
                dve.wait_ge(s_at, 16 * (K2 * R + 2))
                for i in range(2):
                    c.link(dve.tensor_tensor(prod[0], wc[:, 0, :], attn[i], ALU.mult))
                    for k in range(K2):
                        if k == 1:
                            dve.wait_ge(s_pp, i + 1)
                        c.link(dve.tensor_reduce(wlr[:, k, i * RH:(i + 1) * RH],
                                                 prod[k].rearrange("p (c d) -> p c d", d=D), AX.X, ALU.add))
                dve.tensor_copy(elr[:, :, 1, :], whash).then_inc(s_wi, 1)
                dve.wait_ge(s_xl, 32)
                ln_stats(dve, x_rows(0), 0, 0, s_bs, s_vr)
                over_chunks(dve, step)
                keep(NC - 2, 0)
                keep(NC - 1, 1)

            @block.gpsimd
            def _(pool):
                pool.wait_ge(s_at, 16 * (K2 * R + 2))
                for i in range(2):
                    if i == 1:
                        pool.wait_ge(s_pr, 3)
                    pool.tensor_tensor(prod[1], wc[:, 1, :], attn[i], ALU.mult).then_inc(s_pp, 1)
                pool.wait_ge(s_pr, 6)
                pool.memset(hT[:, :, NP:FBLK * P], 0.0).then_inc(s_wi, 1)

            @block.scalar
            def _(act):
                def roots(c, slot):
                    act.wait_ge(s_vr, 4 * c + 4)
                    act.activation(std[:, slot, :], mv[:, slot, :, 1], ACT.Sqrt, bias=eps_c[:, :]).then_inc(s_sd, 1)

                def step(c, slot, first, last):
                    if not last:
                        roots(c + 1, 1 - slot)
                    act.wait_ge(s_tp, c + 1)
                    if not first:
                        wait_past(act, s_el, c - 1)
                    act.sem_inc(passed, 1)
                    banks = PS[:, 2 * slot:2 * slot + 2, :]
                    act.activation(hTs[:, slot, :, :], banks, ACT.Relu).then_inc(s_ht, 1)
                    act.activation(hT[:, :, bass.ds(c * CW, CW)], banks, ACT.Relu).then_inc(s_ht, 1)

                roots(0, 0)
                over_chunks(act, step)

            @block.tensor
            def _(pe):
                def halves(c, slot):
                    pe.wait_ge(s_ht, 2 * c + 1)
                    wait_past(pe, s_ee, c - 1)
                    for b in range(4):
                        for k in range(K2):
                            mm = pe.matmul(PS[:, 4 + slot, b * 2 * RH:(b + 1) * 2 * RH],
                                           hTs[:, slot, k, b * P:(b + 1) * P],
                                           wlr[:, k, :], start=(k == 0), stop=(k == K2 - 1))
                    mm.then_inc(s_el, 1)

                def step(c, slot, first, last):
                    pe.wait_ge(s_hn, c * 4 + 4)
                    if not first:
                        wait_past(pe, s_ht, 2 * (c - 1))
                    for b in range(4):
                        for k in range(K2):
                            mm = pe.transpose(PS[:, 2 * slot + k, b * P:(b + 1) * P],
                                              hN[:, slot, b, k * P:(k + 1) * P], ident[:, :])
                    mm.then_inc(s_tp, 1)
                    if not first:
                        halves(c - 1, 1 - slot)

                over_chunks(pe, step)
                halves(NC - 1, (NC - 1) % 2)

            @block.sync
            def _(sp):
                sp.wait_ge(s_wi, 2)
                sp.wait_ge(s_ld, 16 * 4)

                def store(c, slot, first, last):
                    blocks = min(4, NBLK + 1 - 4 * c) if isinstance(c, int) else 4
                    sp.wait_ge(s_ee, c + 1)
                    for tab, o in ((el_tab, 0), (er_tab, 1)):
                        sp.dma_start(tab[bass.ds(c * CW, blocks * P), :].rearrange("(b p) n -> p b n", p=P),
                                     elr[:, bass.ds(c * 4, blocks), o:o + 2, :].rearrange("p b i n -> p b (i n)")
                                     ).then_inc(s_et, 16)

                over_chunks(sp, store)
                sp.wait_ge(s_et, 32 * NC)

        end_phase()

        dst_b = stg[:, 0:G * U * P].rearrange("p (g n) -> p g n", g=G)
        onehotT = stg[:, G * U * P:2 * G * U * P].rearrange("p (g n) -> p g n", g=G)
        wd = stg[:, 6144:6400].rearrange("p (s u n) -> p s u n", s=2, u=U)
        fout = work[:, 8192:8192 + 1024].rearrange("p (s n) -> p s n", s=2)
        fblk = work[:, 9216:9216 + 512].rearrange("p (s k n) -> p s k n", s=2, k=K2)
        el_ring = work[:, 9728:9728 + TB * 2 * RH].rearrange("p (s n) -> p s n", s=TB)
        er_ring = work[:, 11264:11264 + G * 2 * RH].rearrange("p (g n) -> p g n", g=G)
        oh_b = sb("oh_b", [P, G, U, P], BF16)
        tsum = sb("tsum", [P, U, R, H])
        tmask = sb("tmask", [P, U, R])
        s_gf, s_ix, s_is, s_oh, s_er, s_wd, s_m, s_post = [sem(x) for x in (
            "group_free", "idx_ready", "gathers_issued", "onehots_ready", "er_ready", "wd_ready", "m_ready",
            "post_steps")]
        s_db = [sem(f"dst_rows{g}") for g in range(G)]
        s_ew = [sem(f"er_window{g}") for g in range(G)]
        s_fb, s_fm, s_fe, s_fs = sem("fblk_ready"), sem("feat_ready"), sem("feat_kept"), [
            sem("feat_stored0"), sem("feat_stored1")]
        s_z = sem("sums_zeroed")
        AHEAD = 3
        DEG, ERW, MCOL = 0, P, P + U * 2 * RH

        with nc.Block() as block:
            @block.gpsimd
            def _(pool):
                n = turns_of(pool)
                with pool.Fori(0, n) as i:
                    for g in range(G):
                        pool.wait_ge(s_ix, i * G + g + 1)
                        pool.sem_inc(s_is, 1)
                        for u in range(U):
                            s = g * U + u
                            pool.indirect_dma_start(
                                out=el_ring[:, s, :], out_offset=None, in_=el_tab[:, :],
                                in_offset=bass.IndirectOffsetOnAxis(ap=idx_ring[:, s:s + 1], axis=0)
                            ).then_inc(s_ga[g], 16)

            @block.sync
            def _(sp):
                n = turns_of(sp)
                with sp.Fori(0, n) as i:
                    base = window_starts(sp, i)
                    for g in range(G):
                        sp.wait_ge(s_gf, i * G + g + 1)
                        sp.dma_start(dst_b[:, g, :],
                                     dstm_row.rearrange("(o c) p j -> o (c p j)", o=1)[
                                         :, bass.ds((i * TB + g * U) * P, U * P)].to_broadcast([P, U * P])
                                     ).then_inc(s_db[g], 16)
                        sp.dma_start(er_ring[:, g, :], er_tab[bass.ds(base[g], P), :]).then_inc(s_ew[g], 16)

            @block.scalar
            def _(act):
                n = turns_of(act)
                for slot in range(2):
                    act.sem_inc(s_fs[slot], 16)

                def index(i, g):
                    act.wait_ge(s_gf, i * G + g + 1)
                    act.sem_inc(passed, 1)
                    act.copy(idx_ring[:, g * U:(g + 1) * U], src_i[:, bass.ds(i * TB + g * U, U)]
                             ).then_inc(s_ix, 1)

                def fetch(q, slot):
                    blk = (q >> 2).with_bounds(min_val=0, max_val=FBLK - 1) if not isinstance(q, int) else q >> 2
                    act.activation(fblk[:, slot, :, :], hT[:, :, bass.ds(blk * P, P)], ACT.Copy).then_inc(s_fb, 1)

                for g in range(AHEAD):
                    index(0, g)
                fetch(0, 0)
                with act.Fori(0, n) as i:
                    for g in range(G):
                        q, slot = i * G + g, g % 2
                        act.wait_ge(s_er, q + 1)
                        act.activation(wd[:, slot, :, :], PS[:, g % NBANK, ERW:MCOL].rearrange(
                            "p (u n) -> p u n", u=U)[:, :, 0:KW], ACT.Copy).then_inc(s_wd, 1)
                        index(i + (g + AHEAD) // G, (g + AHEAD) % G)
                        act.wait_ge(s_fm, q + 2)
                        act.sem_inc(passed, 1)
                        fetch(q + 1, 1 - slot)
                        act.wait_ge(s_fm, q + 3)
                        act.wait_ge(s_fs[slot], 16 * (i * (G // 2) + g // 2) + 16)
                        act.activation(fout[:, slot, :], PS[:, 6 + slot, :], ACT.Copy).then_inc(s_fe, 1)
                        act.wait_ge(s_fe, q + 1)
                        blk = (q >> 2).with_bounds(min_val=0, max_val=FBLK - 1)
                        act.dma_start(feat_tab.rearrange("(n r) f -> n (r f)", r=R)[
                            bass.ds(blk * P, P), bass.ds((q & 3) * 512, 512)],
                            fout[:, slot, :]).then_inc(s_fs[slot], 16)
                for slot in range(2):
                    act.wait_ge(s_fs[slot], n * (16 * G // 2) + 16)
                act.sem_inc(passed, 1)

            @block.tensor
            def _(pe):
                n = turns_of(pe)
                pe.sem_inc(s_fm, 2)
                with pe.Fori(0, n) as i:
                    for g in range(G):
                        q, slot, bank = i * G + g, g % 2, g % NBANK
                        pe.wait_ge(s_oh, 2 * q + 2)
                        pe.wait_ge(s_ew[g], i * 16 + 16)
                        pe.wait_ge(s_gf, q + G - NBANK + 1)
                        for u in range(U):
                            pe.matmul(PS[:, bank, DEG:ERW], ones_b[:, :], oh_b[:, g, u, :],
                                      start=(u == 0), stop=(u == U - 1))
                        for u in range(U):
                            mm = pe.matmul(PS[:, bank, ERW + u * 2 * RH:ERW + (u + 1) * 2 * RH],
                                           onehotT[:, g, u * P:(u + 1) * P], er_ring[:, g, :], start=True, stop=True)
                        mm.then_inc(s_er, 1)
                        pe.wait_ge(s_fb, q + 1)
                        for k in range(K2):
                            mm = pe.matmul(PS[:, 6 + slot, :], fblk[:, slot, k, :],
                                           wc[:, k, bass.ds((q & 3) * 512, 512)],
                                           start=(k == 0), stop=(k == K2 - 1))
                        mm.then_inc(s_fm, 1)
                        pe.wait_ge(s_wd, q + 1)
                        pe.wait_ge(s_ga[g], i * 16 * U + 16 * U)
                        for u in range(U):
                            mm = pe.matmul(PS[0:KW, bank, MCOL:MCOL + KW], wd[:, slot, u, :],
                                           el_ring[:, g * U + u, RH:RH + KW], start=(u == 0), stop=(u == U - 1))
                        mm.then_inc(s_m, 1)

            POST = 5

            @block.vector
            def _(dve):
                n = turns_of(dve)
                dve.memset(msum[:, :], 0.0).then_inc(s_z, 1)
                dve.memset(alpha[:, TURNS * TB:T, :], 0.0).then_inc(s_z, 1)
                dve.memset(deg[:, :], 0.0).then_inc(s_gf, G)
                dve.wait_ge(s_z, 2)
                dve.wait_ge(s_gf, G)
                dve.sem_inc(passed, 1)
                with dve.Fori(0, n) as i:
                    base = window_starts(dve, i)

                    def make(g):
                        dve.wait_ge(s_db[g], i * 16 + 16)
                        dve.tensor_scalar(onehotT[:, g, :], dst_b[:, g, :], nodeid[:, bass.ds(i * G + g, 1)],
                                          None, ALU.is_equal).then_inc(s_oh, 1)
                        dve.tensor_tensor(
                            oh_b[:, g, :, :], iota_w[:, :].unsqueeze(1).to_broadcast([P, U, P]),
                            dstloc[:, bass.ds(i * TB + g * U, U)].unsqueeze(2).to_broadcast([P, U, P]),
                            ALU.is_equal).then_inc(s_oh, 1)

                    def post(g):
                        q, bank = i * G + g, g % NBANK
                        tiles = bass.ds(i * TB + g * U, U)
                        dve.tensor_tensor(
                            tmask[:, :, :], typ_t[:, tiles].unsqueeze(2).to_broadcast([P, U, R]),
                            iota_w[:, 0:R].unsqueeze(1).to_broadcast([P, U, R]), ALU.is_equal).then_inc(s_post, 1)
                        dve.wait_ge(s_m, q + 1)
                        dve.tensor_tensor(deg[:, bass.ds(base[g], P)], deg[:, bass.ds(base[g], P)],
                                          PS[:, bank, DEG:ERW], ALU.add).then_inc(s_post, 1)
                        dve.tensor_tensor(msum[:, 0:KW], msum[:, 0:KW], PS[0:KW, bank, MCOL:MCOL + KW], ALU.add
                                          ).then_inc(s_post, 1)
                        dve.wait_ge(s_gf, q + G)
                        dve.tensor_tensor(
                            tsum[:, :, :, :].rearrange("p u r h -> p u (r h)"),
                            PS[:, bank, ERW:MCOL].rearrange("p (u n) -> p u n", u=U)[:, :, KW:KW + RH],
                            el_ring[:, g * U:(g + 1) * U, 0:RH], ALU.add).then_inc(s_post, 1)
                        dve.wait_ge(s_post, q * POST + 4)
                        dve.tensor_tensor(tsum[:, :, :, :].rearrange("p u r h -> p (u r) h"),
                                          tsum[:, :, :, :].rearrange("p u r h -> p (u r) h"),
                                          tmask[:, :, :].rearrange("p u r -> p (u r)").unsqueeze(2)
                                          .to_broadcast([P, U * R, H]), ALU.mult).then_inc(s_post, 1)
                        dve.wait_ge(s_post, q * POST + 5)
                        dve.tensor_reduce(alpha[:, tiles, :], tsum[:, :, :, :].rearrange("p u r h -> p u h r"),
                                          AX.X, ALU.add).then_inc(s_gf, 1)

                    make(0)
                    for g in range(1, G):
                        make(g)
                        post(g - 1)
                    post(G - 1)
                dve.wait_ge(s_gf, n * G + G)
                dve.sem_inc(passed, 1)

        s_ms, s_mt, s_mb = sem("symmetry_steps"), sem("m_turned"), sem("m_summed")
        with nc.Block() as block:
            @block.tensor
            def _(pe):
                pe.transpose(PS[0:KW, 0, 0:KW], msum[:, 0:KW], ident[0:KW, 0:KW]).then_inc(s_mt, 1)
                pe.wait_ge(s_ms, 2)
                pe.matmul(PS[0:1, 1, 0:1], msum[:, 2 * KW:2 * KW + 1], ones[0:KW, 0:1], start=True, stop=True
                          ).then_inc(s_mb, 1)

            @block.vector
            def _(dve):
                c = Chain(dve, s_ms)
                dve.wait_ge(s_mt, 1)
                c.link(dve.tensor_tensor(msum[:, KW:2 * KW], PS[0:KW, 0, 0:KW], msum[:, 0:KW], ALU.not_equal))
                c.link(dve.tensor_reduce(msum[:, 2 * KW:2 * KW + 1], msum[:, KW:2 * KW], AX.X, ALU.add))
                dve.wait_ge(s_mb, 1)
                c.link(dve.tensor_scalar(small[0:1, 40:41], PS[0:1, 1, 0:1], 0.0, None, ALU.is_gt))
                c.link(dve.tensor_copy(flags_i[0:1, 1:2], small[0:1, 40:41]))
                c.link(dve.tensor_copy(small[0:1, 41:42], turns_i[0:1, 0:1]))
                c.link(dve.scalar_tensor_tensor(small[0:1, 42:43], small[0:1, 40:41], float(TURNS_SORTED),
                                                small[0:1, 41:42], ALU.mult, ALU.max))
                c.link(dve.tensor_copy(turns_i[0:1, 1:2], small[0:1, 42:43]))

        end_phase()

        V, FW, BW = [w.rearrange("p (h c j) -> p h c j", h=H, c=CT) for w in (
            work[:, 0:4 * T], work[:, 4 * T:8 * T], work[:, 8 * T:12 * T])]
        hflat = rows4
        AR, FR, PR, SR, CR, DR, CM, CS, CB = [hflat[:, i * T:(i + 1) * T] for i in range(9)]
        CONTM = hflat[:, 9 * T:10 * T + 1]
        flat = lambda a: a.rearrange("p h c j -> p (h c j)")
        lane = lambda a, h: a[:, h, :, :].rearrange("p c j -> p (c j)")
        neg = stg[:, 0:T + 1]
        fneg, lneg = stg[:, 700:700 + T], stg[:, 1400:1400 + T]

        s_q, s_qt, s_qe = sem("scores_ready"), sem("scores_turned"), sem("scores_kept")
        with nc.Block() as block:
            @block.vector
            def _(dve):
                c = Chain(dve, s_q)
                a2 = alpha[:, :, :].rearrange("p t h -> p (t h)")
                c.link(dve.tensor_tensor(alpha[:, :, :], alpha[:, :, :],
                                         pad_t[:, :].unsqueeze(2).to_broadcast([P, T, H]), ALU.add))
                c.link(dve.scalar_tensor_tensor(a2, a2, SLOPE, a2, ALU.mult, ALU.max))
                for i in range(CT):
                    dve.wait_ge(s_qt, i + 1)
                    dve.tensor_copy(V[:, :, i, :], PS[:, i, :].rearrange("p (h j) -> p h j", h=H)).then_inc(s_qe, 1)
                c.link(dve.tensor_scalar(neg[:, :], same[:, :], 1.0, BIG, ALU.subtract, ALU.mult))
                c.link(dve.tensor_scalar(fneg, firstm[:, :], 1.0, BIG, ALU.subtract, ALU.mult))
                c.link(dve.tensor_scalar(lneg, lastm[:, :], 1.0, BIG, ALU.subtract, ALU.mult))
                dve.wait_ge(s_qe, CT)

            @block.tensor
            def _(pe):
                pe.wait_ge(s_q, 2)
                for i in range(CT):
                    for h in range(H):
                        mm = pe.transpose(PS[:, i, h * P:(h + 1) * P], alpha[:, i * P:(i + 1) * P, h], ident[:, :])
                    mm.then_inc(s_qt, 1)

        def segment(op_in, op, zero, mask, fmask, lmask):
            s_s, s_p, s_b = sem("segment_steps"), sem("ends_turned"), sem("carries_turned")
            with nc.Block() as block:
                @block.vector
                def _(dve):
                    c = Chain(dve, s_s)
                    for h in range(H):
                        dve.tensor_tensor_scan(lane(FW, h), mask[:, 0:T], lane(V, h), zero, op_in, op).then_inc(s_s, 1)
                        dve.tensor_tensor_scan(lane(BW, h)[:, ::-1], mask[:, 1:T + 1][:, ::-1],
                                               lane(V, h)[:, ::-1], zero, op_in, op).then_inc(s_s, 1)
                    c.n = 2 * H
                    dve.wait_ge(s_s, 2 * H)
                    c.link(dve.tensor_tensor(CS, cont[:, 0:T], single[:, :], ALU.mult))
                    c.link(dve.tensor_tensor(CB, cont[:, 1:T + 1], single[:, :], ALU.mult))
                    c.link(dve.tensor_copy(CONTM, cont[:, :]))
                    if zero:
                        for m in (CS, CB, CONTM):
                            c.link(dve.tensor_scalar(m, m, 1.0, BIG, ALU.subtract, ALU.mult))
                    dve.wait_ge(s_p, 1)
                    for i, to in enumerate((AR, FR)):
                        c.link(dve.tensor_copy(to[:, 0:512], PS[0:H, 2 * i, :]))
                        c.link(dve.tensor_copy(to[:, 512:T], PS[0:H, 2 * i + 1, 0:P]))
                    c.link(dve.tensor_tensor_scan(PR, CS, AR, zero, op_in, op))
                    c.link(dve.tensor_tensor_scan(SR[:, ::-1], CB[:, ::-1], FR[:, ::-1], zero, op_in, op))
                    c.link(dve.memset(CR, zero))
                    c.link(dve.memset(DR, zero))
                    c.link(dve.tensor_tensor(CR[:, 1:T], PR[:, 0:T - 1], CONTM[:, 1:T], op_in))
                    c.link(dve.tensor_tensor(DR[:, 0:T - 1], SR[:, 1:T], CONTM[:, 1:T], op_in))
                    dve.sem_inc(s_b, 1)
                    dve.wait_ge(s_b, 3)
                    c.link(dve.tensor_copy(cT[:, :, :, :].rearrange("p i c h -> p (i c h)"), PS[:, 4, 0:2 * CT * H]))
                    c.link(dve.tensor_tensor(flat(FW), flat(FW), flat(BW), op))
                    if not zero:
                        c.link(dve.tensor_tensor(flat(FW), flat(FW), flat(V), ALU.subtract))
                    for i, m in enumerate((fmask, lmask)):
                        for h in range(H):
                            for cc in range(CT):
                                dve.scalar_tensor_tensor(FW[:, h, cc, :], m[:, cc * P:(cc + 1) * P],
                                                         cT[:, i, cc, h:h + 1], FW[:, h, cc, :], op_in, op
                                                         ).then_inc(s_s, 1)
                        c.n += H * CT
                        dve.wait_ge(s_s, c.n)

                @block.tensor
                def _(pe):
                    pe.wait_ge(s_s, 2 * H)
                    for i, (a, j) in enumerate(((FW, P - 1), (BW, 0))):
                        for cc in range(CT):
                            mm = pe.transpose(PS[0:H, 2 * i + cc // 4, (cc % 4) * P:(cc % 4 + 1) * P],
                                              a[:, :, cc, j], ident[:, :])
                    mm.then_inc(s_p, 1)
                    pe.wait_ge(s_b, 1)
                    for i, a in enumerate((CR, DR)):
                        for cc in range(CT):
                            mm = pe.transpose(PS[:, 4, (i * CT + cc) * H:(i * CT + cc + 1) * H],
                                              a[:, cc * P:(cc + 1) * P], ident[0:H, 0:H])
                    mm.then_inc(s_b, 2)

        segment(ALU.add, ALU.max, -BIG, neg, fneg, lneg)
        s_x, s_xe = sem("shifted"), sem("exps_ready")
        with nc.Block() as block:
            @block.vector
            def _(dve):
                dve.tensor_tensor(flat(V), flat(V), flat(FW), ALU.subtract).then_inc(s_x, 1)

            @block.scalar
            def _(act):
                act.wait_ge(s_x, 1)
                act.activation(flat(V), flat(V), ACT.Exp).then_inc(s_xe, 1)
                act.wait_ge(s_xe, 1)
        segment(ALU.mult, ALU.add, 0.0, same, firstm[:, :], lastm[:, :])
        s_al, s_at, s_ae, s_fx = [sem(a) for a in ("alphas_ready", "alphas_turned", "alphas_kept", "first_indexed")]
        ring = work[:, 8192:WLEN].rearrange("p (s f) -> p s f", s=TB)

        def gather_group(pool, table, g):
            for u in range(U):
                s = g * U + u
                pool.indirect_dma_start(
                    out=ring[:, s, :], out_offset=None, in_=table[:, :],
                    in_offset=bass.IndirectOffsetOnAxis(ap=idx_ring[:, s:s + 1], axis=0)).then_inc(s_ga[g], 16)

        with nc.Block() as block:
            @block.scalar
            def _(act):
                act.copy(idx_ring[:, :], fidx_i[:, 0:TB]).then_inc(s_fx, 1)

            @block.gpsimd
            def _(pool):
                pool.wait_ge(s_fx, 1)
                for g in range(G):
                    gather_group(pool, feat_tab[0:NBLK * P * R, :], g)

            @block.vector
            def _(dve):
                c = Chain(dve, s_al)
                c.link(dve.reciprocal(flat(FW), flat(FW)))
                c.link(dve.tensor_tensor(flat(V), flat(V), flat(FW), ALU.mult))
                for i in range(CT):
                    dve.wait_ge(s_at, i + 1)
                    dve.tensor_copy(alpha[:, i * P:(i + 1) * P, :].rearrange("p t h -> p h t"),
                                    PS[:, i, :].rearrange("p (h t) -> p h t", h=H)).then_inc(s_ae, 1)
                dve.wait_ge(s_ae, CT)

            @block.tensor
            def _(pe):
                pe.wait_ge(s_al, 2)
                for i in range(CT):
                    for h in range(H):
                        mm = pe.transpose(PS[:, i, h * P:(h + 1) * P], V[:, h, i, :], ident[:, :])
                    mm.then_inc(s_at, 1)

        def find_cuts(which):
            s_ct = sem("cut_steps")
            spots = -(-NG // G)
            row = stg[0:1, 0:spots]
            below = stg[0:1, 64:64 + (NC - 1) * spots].rearrange("p (c j) -> p c j", c=NC - 1)
            with nc.Block() as block:
                @block.vector
                def _(dve):
                    c = Chain(dve, s_ct)
                    c.link(dve.tensor_copy(row, base_i[0:1, 0:NG:G]))
                    c.link(dve.tensor_scalar(small[0:1, 44:44 + NC - 1], iota_w[0:1, 1:NC], float(CW), None, ALU.mult))
                    c.link(dve.tensor_tensor(
                        below, row.unsqueeze(1).to_broadcast([1, NC - 1, spots]),
                        small[0:1, 44:44 + NC - 1].unsqueeze(2).to_broadcast([1, NC - 1, spots]), ALU.is_lt))
                    c.link(dve.tensor_reduce(small[0:1, 52:52 + NC - 1], below, AX.X, ALU.add))
                    c.link(dve.memset(cuts_i[0:1, 0:1], 0))
                    c.link(dve.tensor_copy(cuts_i[0:1, 1:NC], small[0:1, 52:52 + NC - 1]))
                    c.link(dve.tensor_copy(cuts_i[0:1, NC:NC + 1], turns_i[0:1, which:which + 1]))

        wout = wbuf[:, 512:1024].rearrange("p (k n) -> p k n", k=K2)
        win = wbuf[:, 0:512].rearrange("p (k n) -> p k n", k=K2)
        wag = wbuf[:, 1024:2560].rearrange("p (l k n) -> p l k n", l=LAYERS, k=K2)
        wse = wbuf[:, 2560:4096].rearrange("p (l k n) -> p l k n", l=LAYERS, k=K2)
        onehot = stg[:, 0:TB * P].rearrange("p (s n) -> p s n", s=TB)
        bufs = [stg[:, 3072 + 1024 * i:4096 + 1024 * i] for i in range(3)]
        b4 = lambda a: a.rearrange("p (b f) -> p b f", b=4)
        k2 = lambda a: a.rearrange("p (k n) -> p k n", k=K2)
        x1_rows = x1_tab.rearrange("(c b p) f -> c p b f", b=4, p=P)
        h_rows = [t.rearrange("(c b p) f -> c p b f", b=4, p=P) for t in h_tab]
        LAST = N - (NC - 1) * CW - P

        def chunk_of(rows, c):
            return rows[bass.ds(c, 1), :, :, :].rearrange("o p b f -> p (o b) f")

        def rows_by_weight(pe, cols, weight):
            for b in range(4):
                for k in range(K2):
                    mm = pe.matmul(PS[:, 6 + b // 2, (b % 2) * F:(b % 2 + 1) * F], cols[:, k, b * P:(b + 1) * P],
                                   weight[:, k, :], start=(k == 0), stop=(k == K2 - 1))
            return mm

        def edge_pass(table, idx, scaled, which, before, dense):
            s_ix, s_is, s_oh, s_mm, s_az = [sem(x) for x in (
                "idx_ready", "gathers_issued", "rows_ready", "group_summed", "acc_zeroed")]
            s_add = dense["added"]

            def walk(eng, turn, part):
                def chunk(c):
                    past, upto = [eng.value_load(cuts_i[0:1, bass.ds(c + j, 1)], min_val=0, max_val=TURNS_SORTED)
                                  for j in range(2)]
                    with eng.If(upto - past > 0):
                        with eng.Fori(past, upto) as i:
                            turn(i)
                    part(eng, c, upto)

                if dense["late"]:
                    chunk(0)
                    with eng.Fori(1, NC) as c:
                        chunk(c)
                    part(eng, NC, None)
                else:
                    with eng.Fori(0, NC) as c:
                        chunk(c)

            with nc.Block() as block:
                @block.gpsimd
                def _(pool):
                    n = turns_of(pool, which)
                    if scaled:
                        pool.memset(acc[:, 1, :], 0.0).then_inc(s_az, 1)
                    with pool.Fori(1 if scaled else 0, n) as i:
                        for g in range(G):
                            pool.wait_ge(s_ix, i * G + g + 1)
                            pool.sem_inc(s_is, 1)
                            gather_group(pool, table, g)

                @block.scalar
                def _(act):
                    def turn(i):
                        for g in range(G):
                            act.wait_ge(s_mm, i * G + g + 1)
                            act.sem_inc(passed, 1)
                            act.copy(idx_ring[:, g * U:(g + 1) * U], idx[:, bass.ds((i + 1) * TB + g * U, U)]
                                     ).then_inc(s_ix, 1)

                    if scaled:
                        act.sem_inc(s_ix, G)
                    else:
                        act.copy(idx_ring[:, :], idx[:, 0:TB]).then_inc(s_ix, G)
                    walk(act, turn, dense["scalar"])

                @block.tensor
                def _(pe):
                    past = gathered_turns(pe, before)

                    def turn(i):
                        for g in range(G):
                            q, bank = i * G + g, g % NBANK
                            pe.wait_ge(s_oh, q + 1)
                            if not scaled:
                                pe.wait_ge(s_ga[g], (i + past) * (16 * U) + 16 * U)
                            pe.wait_ge(s_add, q + 1)
                            for k in range(K2):
                                for u in range(U):
                                    s = g * U + u
                                    mm = pe.matmul(PS[:, bank, k * P:(k + 1) * P],
                                                   ring[:, s, k * P:(k + 1) * P], onehot[:, s, :],
                                                   start=(u == 0), stop=(u == U - 1))
                            mm.then_inc(s_mm, 1)

                    walk(pe, turn, dense["tensor"])

                @block.vector
                def _(dve):
                    past = gathered_turns(dve, before)

                    def turn(i):
                        base = window_starts(dve, i)

                        def make(g):
                            tiles = bass.ds(i * TB + g * U, U)
                            dve.wait_ge(s_ix, i * G + g + 1)
                            ins = dve.tensor_tensor(
                                onehot[:, g * U:(g + 1) * U, :], iota_w[:, :].unsqueeze(1).to_broadcast([P, U, P]),
                                dstloc[:, tiles].unsqueeze(2).to_broadcast([P, U, P]), ALU.is_equal)
                            if scaled:
                                dve.wait_ge(s_ga[g], (i + past) * (16 * U) + 16 * U)
                                rows = ring[:, g * U:(g + 1) * U, :].rearrange("p u (h d) -> p (u h) d", h=H)
                                al = alpha[:, tiles, :].rearrange("p u h -> p (u h)").unsqueeze(2)
                                ins = dve.tensor_tensor(rows, rows, al.to_broadcast([P, U * H, D]), ALU.mult)
                            ins.then_inc(s_oh, 1)

                        def add(g):
                            q = i * G + g
                            dve.wait_ge(s_mm, q + 1)
                            dve.wait_ge(s_add, q + NBANK)
                            a = acc[:, :, bass.ds(base[g], P)]
                            dve.tensor_tensor(a, a, PS[:, g % NBANK, 0:K2 * P].rearrange("p (k n) -> p k n", k=K2),
                                              ALU.add).then_inc(s_add, 1)

                        make(0)
                        for g in range(1, G):
                            make(g)
                            add(g - 1)
                        add(G - 1)

                    if scaled:
                        dve.memset(acc[:, 0, :], 0.0).then_inc(s_add, NBANK)
                        dve.wait_ge(s_az, 1)
                    else:
                        dve.memset(acc[:, :, :], 0.0).then_inc(s_add, NBANK)
                    walk(dve, turn, dense["vector"])

                @block.sync
                def _(sp):
                    dense["sync"](sp)

        def input_part():
            (s_add, s_w, s_xl, s_sx, s_ac, s_t1, s_x1, s_xb, s_bs, s_vr, s_sd, s_rs, s_hn, s_t2, s_ht, s_wi, s_h0,
             s_t3, s_tb, s_st) = [sem(a) for a in (
                 "group_added", "weights_loaded", "x_loaded", "x1_stored", "acc_biased", "acc_turned", "x1_ready",
                 "x1_biased", "stats_done", "var_ready", "std_done", "rstd_done", "hn_ready", "hn_turned", "ht_ready",
                 "input_layer_summed", "h0_kept", "rows_summed", "rows_ready", "rows_stored")]
            x1, mid, h0 = bufs
            biased = oh_b[:, :, :, :].rearrange("p g u n -> p (g u n)").bitcast(FP32)[:, 0:1024]
            hn = b4(masks[:, 0:1024])
            first = lambda c: isinstance(c, int) and c == 0
            last = lambda c: isinstance(c, int) and c == NC

            def scalar(act, c, upto):
                if not last(c):
                    act.wait_ge(s_add, upto * G + NBANK)
                    wait_past(act, s_t1, c)
                    act.sem_inc(passed, 1)
                    for k in range(K2):
                        act.activation(k2(biased)[:, k, :], acc[:, k, bass.ds(c * CW, CW)], ACT.Identity,
                                       bias=hb_c[:, k:k + 1]).then_inc(s_ac, 1)
                if not first(c):
                    act.wait_ge(s_t2, c)
                    act.wait_ge(s_st, 16 * c)
                    act.activation(k2(mid), PS[:, 6:8, :], ACT.Relu).then_inc(s_ht, 1)
                if not last(c):
                    act.wait_ge(s_vr, 4 * c + 4)
                    act.activation(std[:, 0, :], mv[:, 0, :, 1], ACT.Sqrt, bias=eps_c[:, :]).then_inc(s_sd, 1)
                if not first(c):
                    act.wait_ge(s_wi, c)
                    act.sem_inc(passed, 1)
                    for f in range(K2):
                        act.activation(k2(h0)[:, f, :], PS[:, 4 + f, :], ACT.Identity, bias=bin_c[:, f:f + 1]
                                       ).then_inc(s_h0, 1)
                    for f in range(K2):
                        act.activation(hT[:, f, bass.ds((c - 1) * CW, CW)], PS[:, 4 + f, :], ACT.Identity,
                                       bias=bin_c[:, f:f + 1]).then_inc(s_h0, 1)
                    act.wait_ge(s_t3, c)
                    act.activation(mid.rearrange("p (j n) -> p j n", j=2), PS[:, 6:8, :], ACT.Copy
                                   ).then_inc(s_tb, 1)

            def tensor(pe, c, upto):
                if not first(c):
                    pe.wait_ge(s_hn, 4 * c)
                    pe.wait_ge(s_tb, c)
                    for b in range(4):
                        for k in range(K2):
                            mm = pe.transpose(PS[:, 6 + k, b * P:(b + 1) * P], hn[:, b, k * P:(k + 1) * P],
                                              ident[:, :])
                    mm.then_inc(s_t2, 1)
                if not last(c):
                    pe.wait_ge(s_ac, 2 * c + 2)
                    wait_past(pe, s_h0, 4 * c)
                    for b in range(4):
                        for k in range(K2):
                            mm = pe.transpose(PS[:, 4 + b // 2, (b % 2) * F + k * P:(b % 2) * F + (k + 1) * P],
                                              k2(biased)[:, k, b * P:(b + 1) * P], ident[:, :])
                    mm.then_inc(s_t1, 1)
                if not first(c):
                    pe.wait_ge(s_ht, c)
                    pe.wait_ge(s_w, 16 * 4)
                    if not last(c):
                        pe.wait_ge(s_x1, c + 1)
                    for f in range(K2):
                        for k in range(K2):
                            mm = pe.matmul(PS[:, 4 + f, :], win[:, k, f * P:(f + 1) * P], k2(mid)[:, k, :],
                                           start=(k == 0), stop=(k == K2 - 1))
                    mm.then_inc(s_wi, 1)
                    pe.wait_ge(s_h0, 4 * c + 2)
                    rows_by_weight(pe, k2(h0), wag[:, 0, :, :]).then_inc(s_t3, 1)

            def vector(dve, c, upto):
                if last(c):
                    return
                dve.wait_ge(s_xl, 32 * c + 32)
                dve.wait_ge(s_t1, c + 1)
                x1j = x1.rearrange("p (j n) -> p j n", j=2)
                dve.tensor_tensor(x1j, PS[:, 4:6, :], x1j, ALU.add).then_inc(s_x1, 1)
                dve.wait_ge(s_x1, c + 1)
                rows = lambda b: b4(x1)[:, b, :]
                ln_stats(dve, rows, c, 0, s_bs, s_vr)
                wait_past(dve, s_t2, c)
                ln_finish(dve, rows, c, 0, s_sd, s_rs, s_hn, hn)
                dve.wait_ge(s_hn, 4 * c + 4)
                dve.tensor_tensor(b4(x1), b4(x1), bout_b[:, :].unsqueeze(1).to_broadcast([P, 4, F]), ALU.add
                                  ).then_inc(s_xb, 1)

            def sync(sp):
                def store_rows(c):
                    sp.wait_ge(s_tb, c + 2)
                    sp.dma_start(chunk_of(h_rows[0], c), b4(mid)).then_inc(s_st, 16)

                def step(c, last):
                    wait_past(sp, s_sx, 16 * c)
                    if not last:
                        sp.dma_start(b4(x1), x[bass.ds(c * CW, CW), :].rearrange("(b p) f -> p b f", p=P)
                                     ).then_inc(s_xl, 32)
                    else:
                        sp.dma_start(b4(x1)[:, 0, :], x[c * CW:c * CW + P, :]).then_inc(s_xl, 16)
                        sp.dma_start(b4(x1)[0:LAST, 1, :], x[c * CW + P:N, :]).then_inc(s_xl, 16)
                    sp.wait_ge(s_xb, c + 1)
                    sp.dma_start(chunk_of(x1_rows, c), b4(x1)).then_inc(s_sx, 16)
                    if not first(c):
                        store_rows(c - 1)

                sp.sem_inc(s_tb, 1)
                sp.sem_inc(s_st, 16)
                sp.sem_inc(s_h0, 4)
                for to, w in ((win, w_in), (wout, w_out)):
                    sp.dma_start(to, w.rearrange("(k p) n -> p k n", p=P)).then_inc(s_w, 16)
                for to, w in ((wag, w_agg), (wse, w_self)):
                    sp.dma_start(to.rearrange("p l k n -> p (l k) n"),
                                 w.rearrange("l (k p) n -> p (l k) n", p=P)).then_inc(s_w, 16)
                step(0, False)
                with sp.Fori(1, NC - 1) as c:
                    step(c, False)
                step(NC - 1, True)
                store_rows(NC - 1)
                sp.wait_ge(s_sx, 16 * NC)
                sp.wait_ge(s_st, 16 * NC + 16)

            return dict(late=True, added=s_add, scalar=scalar, tensor=tensor, vector=vector, sync=sync)

        def layer_part(l):
            last_layer = l == LAYERS - 1
            s_add, s_dg, s_sc, s_self, s_sum, s_hr, s_hd, s_tn, s_tk, s_st, s_xl = [sem(a) for a in (
                "group_added", "deg_inverted", "mean_ready", "self_summed", "layer_summed", "h_ready", "h_kept",
                "rows_summed", "rows_ready", "rows_stored", "x1_loaded")]
            mean, hs, ts = bufs

            def scalar(act, c, upto):
                cols = bass.ds(c * CW, CW)
                act.wait_ge(s_sum, c + 1)
                act.sem_inc(passed, 1)
                for f in range(K2):
                    act.activation(k2(hs)[:, f, :], k2(mean)[:, f, :], ACT.Relu, bias=bh_c[:, l, f:f + 1]
                                   ).then_inc(s_hr, 1)
                if not last_layer:
                    for f in range(K2):
                        act.activation(hT[:, f, cols], k2(mean)[:, f, :], ACT.Relu, bias=bh_c[:, l, f:f + 1]
                                       ).then_inc(s_hd, 1)
                    act.wait_ge(s_tn, c + 1)
                    act.wait_ge(s_st, 16 * c + 16)
                    act.activation(ts.rearrange("p (j n) -> p j n", j=2), PS[:, 6:8, :], ACT.Copy
                                   ).then_inc(s_tk, 1)

            def tensor(pe, c, upto):
                for f in range(K2):
                    for k in range(K2):
                        mm = pe.matmul(PS[:, 4 + f, :], wse[:, l, k, f * P:(f + 1) * P],
                                       hT[:, k, bass.ds(c * CW, CW)], start=(k == 0), stop=(k == K2 - 1))
                mm.then_inc(s_self, 1)
                pe.wait_ge(s_hr, K2 * c + K2)
                rows_by_weight(pe, k2(hs), wout if last_layer else wag[:, l + 1, :, :]).then_inc(s_tn, 1)

            def vector(dve, c, upto):
                cols = bass.ds(c * CW, CW)
                if l == 0:
                    dve.tensor_scalar(deg[:, cols], deg[:, cols], 1.0, None, ALU.max).then_inc(s_dg, 1)
                    dve.wait_ge(s_dg, 2 * c + 1)
                    dve.sem_inc(passed, 1)
                    dve.reciprocal(deg[:, cols], deg[:, cols]).then_inc(s_dg, 1)
                    dve.wait_ge(s_dg, 2 * c + 2)
                dve.wait_ge(s_add, upto * G + NBANK)
                if not last_layer:
                    dve.wait_ge(s_hd, K2 * c + K2)
                dve.tensor_tensor(k2(mean), acc[:, :, cols], deg[:, cols].unsqueeze(1).to_broadcast([P, K2, CW]),
                                  ALU.mult).then_inc(s_sc, 1)
                dve.wait_ge(s_sc, c + 1)
                dve.wait_ge(s_self, c + 1)
                dve.tensor_tensor(k2(mean), k2(mean), PS[:, 4:6, :], ALU.add).then_inc(s_sum, 1)
                if last_layer:
                    dve.wait_ge(s_tn, c + 1)
                    dve.wait_ge(s_xl, 16 * c + 16)
                    o = ts.rearrange("p (j n) -> p j n", j=2)
                    dve.tensor_tensor(o, PS[:, 6:8, :], o, ALU.add).then_inc(s_tk, 1)

            def sync(sp):
                def step(c, last):
                    if last_layer:
                        sp.wait_ge(s_st, 16 * c + 16)
                        sp.dma_start(b4(ts), chunk_of(x1_rows, c)).then_inc(s_xl, 16)
                    sp.wait_ge(s_tk, c + 1)
                    if not last_layer:
                        sp.dma_start(chunk_of(h_rows[(l + 1) % 2], c), b4(ts)).then_inc(s_st, 16)
                    elif not last:
                        sp.dma_start(out[bass.ds(c * CW, CW), :].rearrange("(b p) f -> p b f", p=P),
                                     b4(ts)).then_inc(s_st, 16)
                    else:
                        sp.dma_start(out[c * CW:c * CW + P, :], b4(ts)[:, 0, :]).then_inc(s_st, 16)
                        sp.dma_start(out[c * CW + P:N, :], b4(ts)[0:LAST, 1, :]).then_inc(s_st, 16)

                sp.sem_inc(s_st, 16)
                sp.sem_inc(s_hd, K2)
                with sp.Fori(0, NC - 1) as c:
                    step(c, False)
                step(NC - 1, True)
                sp.wait_ge(s_st, 16 * (NC + 1 + last_layer))

            return dict(late=False, added=s_add, scalar=scalar, tensor=tensor, vector=vector, sync=sync)

        end_phase()
        find_cuts(0)
        edge_pass(feat_tab[0:NBLK * P * R, :], fidx_i, True, 0, 1, input_part())

        end_phase()
        key, dstm, srcr, typr, fidx = [work[:, i * T:(i + 1) * T].rearrange("p (c j) -> p c j", c=CT)
                                       for i in range(5)]
        sort_edges(1, src, dst)
        tile_tables(1)
        find_cuts(1)
        end_phase()
        for l in range(LAYERS):
            edge_pass(h_tab[l % 2][:, :], src_i, False, 1, 2 + l, layer_part(l))


_INS = ["x", "src", "dst", "edge_type_8", "L0_gnn_conv_weights", "L0_gnn_attn_l", "L0_gnn_attn_r",
        "L0_gnn_h_bias", "L1_gnn_W_in", "L1_gnn_b_in", "L1_gnn_W_agg", "L1_gnn_W_self", "L1_gnn_b_hid",
        "L1_gnn_W_out", "L1_gnn_b_out"]


def kernel(**inputs):
    import numpy as _np
    import concourse.bacc as _bacc
    from concourse import mybir as _mybir
    from concourse.bass_utils import run_bass_kernel_spmd as _run

    nc = _bacc.Bacc("TRN2", target_bir_lowering=False, num_devices=1)
    arrays, args = {}, []
    for name in _INS:
        a = _np.ascontiguousarray(inputs[name])
        arrays[f"in_{name}"] = a
        args.append(nc.dram_tensor(f"in_{name}", a.shape, _mybir.dt.from_np(a.dtype), kind="ExternalInput").ap())
    args.append(nc.dram_tensor("out_0", (N, F), _mybir.dt.float32, kind="ExternalOutput").ap())
    gnn_kernel(nc, *args)
    r = _run(nc, [arrays], core_ids=[0])
    return r.results[0]["out_0"]
```
